# Optimizing a Trainium2 kernel written in Bass

```python
import numpy as np
import jax
import jax.numpy as jnp

def _softmax(x, axis=-1):
    return jax.nn.softmax(x, axis=axis)

def _gelu(x):
    return jax.nn.gelu(x, approximate=True)

def _silu(x):
    return jax.nn.silu(x)

def _sigmoid(x):
    return jax.nn.sigmoid(x)

def _layernorm(x, axis=-1, eps=1e-05):
    m = jnp.mean(x, axis=axis, keepdims=True)
    v = jnp.var(x, axis=axis, keepdims=True)
    return (x - m) / jnp.sqrt(v + eps)

def _scatter_add(tgt, idx, src, axis=0):
    return tgt.at[idx].add(src)

def _segment_sum(src, seg, n):
    return jax.ops.segment_sum(src, seg, n)
kernel_name = 'mk_xattn_seq_d2_seqx_r4_954af4'

def setup_inputs(seed: int=0):
    np.random.seed(seed)
    _w = jnp.asarray

    def _rec_inputs():
        import jax
        import jax.numpy as jnp
        _rk = jax.random.key(seed)
        x = -0.0002928 + 1 * jax.random.normal(jax.random.fold_in(_rk, 1), (16, 256, 512), jnp.float32)
        _lenS = 256 - jax.random.randint(jax.random.fold_in(_rk, 7), (16,), 0, max(1, 256 // 4) + 1, jnp.int32)
        _lenS2 = 256 - jax.random.randint(jax.random.fold_in(_rk, 8), (16,), 0, max(1, 256 // 4) + 1, jnp.int32)
        _ctx_2048P = jax.random.normal(jax.random.fold_in(_rk, 11), (16, 16, 512), jnp.float32)
        _ctx_2048c = jax.random.dirichlet(jax.random.fold_in(_rk, 511), 0.3 * jnp.ones((16,), jnp.float32), (16, 256))
        _ctx_2048t = jnp.einsum('bsk,bkd->bsd', _ctx_2048c, _ctx_2048P)
        _ctx_2048t = _ctx_2048t * jax.lax.rsqrt(jnp.mean(jnp.square(_ctx_2048t)) + 1e-12) * 0.953939
        ctx_2048 = -1.39393e-06 + 0.999914 * (_ctx_2048t + 0.3 * jax.random.normal(jax.random.fold_in(_rk, 611), (16, 256, 512), jnp.float32))
        _validS = jnp.arange(256)[None, :] < _lenS[:, None]
        _validS2 = jnp.arange(256)[None, :] < _lenS2[:, None]
        _causal = jnp.tril(jnp.ones((256, 256), dtype=bool))
        mask_1x1xSxS2_fc1 = jnp.where(jnp.broadcast_to(_validS2[0:1, None, None, :], (1, 1, 256, 256)), 1.0, 0.0).astype(jnp.float32)
        mask_Bx1xSxS2_ff1 = jnp.where(jnp.ones((16, 1, 256, 256), dtype=bool), 1.0, 0.0).astype(jnp.float32)
        return (x, ctx_2048, mask_1x1xSxS2_fc1, mask_Bx1xSxS2_ff1)
    x, ctx_2048, mask_1x1xSxS2_fc1, mask_Bx1xSxS2_ff1 = _rec_inputs()

    def _L0_xattn_setup():
        import jax, jax.numpy as jnp
        import numpy as np
        H = 512
        NH = 16
        HD = H // NH
        EPS = 1e-05

        def gelu(x):
            return 0.5 * x * (1.0 + jnp.tanh(0.7978845608028654 * x * (1.0 + 0.044715 * x * x)))

        def layernorm(x, scale, bias):
            m = jnp.mean(x, axis=-1, keepdims=True)
            v = jnp.mean(jnp.square(x - m), axis=-1, keepdims=True)
            return (x - m) * jax.lax.rsqrt(v + EPS) * scale + bias

        def split_heads(x):
            b, s, _ = x.shape
            return x.reshape(b, s, NH, HD).transpose(0, 2, 1, 3)

        def merge_heads(x):
            b, nh, s, hd = x.shape
            return x.transpose(0, 2, 1, 3).reshape(b, s, nh * hd)

        def attention(q, k, v, mask):
            scores = jnp.einsum('bhqd,bhkd->bhqk', q, k) / jnp.sqrt(jnp.float32(HD))
            scores = scores * mask - 10000.0 * (1.0 - mask)
            probs = jax.nn.softmax(scores, axis=-1)
            return jnp.einsum('bhqk,bhkd->bhqd', probs, v)
        key = jax.random.key(seed)
        ks = jax.random.split(key, 16)
        b, s, t = (2, 256, 256)
        w = lambda k, i, o: jax.random.normal(k, (i, o), jnp.float32) * 0.02
        inp = {'hidden_states': jax.random.normal(ks[0], (b, s, H), jnp.float32), 'encoder_states': jax.random.normal(ks[1], (b, t, H), jnp.float32), 'ltor_mask': jnp.tril(jnp.ones((1, 1, s, s), jnp.float32)), 'cross_mask': jnp.ones((b, 1, s, t), jnp.float32), 'ln1_s': jnp.ones((H,), jnp.float32), 'ln1_b': jnp.zeros((H,), jnp.float32), 'w_qkv': w(ks[2], H, 3 * H), 'b_qkv': jnp.zeros((3 * H,), jnp.float32), 'w_ao': w(ks[3], H, H), 'b_ao': jnp.zeros((H,), jnp.float32), 'ln2_s': jnp.ones((H,), jnp.float32), 'ln2_b': jnp.zeros((H,), jnp.float32), 'w_q': w(ks[4], H, H), 'b_q': jnp.zeros((H,), jnp.float32), 'w_kv': w(ks[5], H, 2 * H), 'b_kv': jnp.zeros((2 * H,), jnp.float32), 'w_co': w(ks[6], H, H), 'b_co': jnp.zeros((H,), jnp.float32), 'ln3_s': jnp.ones((H,), jnp.float32), 'ln3_b': jnp.zeros((H,), jnp.float32), 'w1': w(ks[7], H, 4 * H), 'b1': jnp.zeros((4 * H,), jnp.float32), 'w2': w(ks[8], 4 * H, H), 'b2': jnp.zeros((H,), jnp.float32)}
        return inp
    _L0_xattn_all = _L0_xattn_setup()
    _L0_xattn_in = {k: v for k, v in _L0_xattn_all.items() if k in ('ln1_s', 'ln1_b', 'w_qkv', 'b_qkv', 'w_ao', 'b_ao', 'ln2_s', 'ln2_b', 'w_q', 'b_q', 'w_kv', 'b_kv', 'w_co', 'b_co', 'ln3_s', 'ln3_b', 'w1', 'b1', 'w2', 'b2')}
    del _L0_xattn_all

    def _L1_xattn_setup():
        import jax, jax.numpy as jnp
        import numpy as np
        N_HEAD = 32
        EPS = 1e-05

        def _ln(x, w, b):
            m = jnp.mean(x, axis=-1, keepdims=True)
            v = jnp.mean((x - m) ** 2, axis=-1, keepdims=True)
            return (x - m) * jax.lax.rsqrt(v + EPS) * w + b

        def _forward(x, state, i, ln1_w, ln1_b, ln2_w, ln2_b, maa_x, maa_w, maa_k, maa_v, maa_r, maa_g, maa_w1, maa_w2, time_decay, decay_w1, decay_w2, faaaa, Wr, Wk, Wv, Wg, Wo, gn_w, gn_b, fmaa_k, fmaa_r, fWk, fWr, fWv):
            B, L, C = x.shape
            H = N_HEAD
            S = C // H
            i0 = (2 + S) * i
            xa = _ln(x, ln1_w, ln1_b)
            sx = jnp.concatenate([state[:, i0 + 1][:, None], xa[:, :-1]], axis=1) - xa
            xxx = xa + sx * maa_x
            t = jnp.tanh(xxx @ maa_w1).reshape(B, L, 5, -1)
            m = jnp.einsum('blfd,fdc->blfc', t, maa_w2)
            mw, mk, mv, mr, mg = (m[:, :, j] for j in range(5))
            xw = xa + sx * (maa_w + mw)
            xk = xa + sx * (maa_k + mk)
            xv = xa + sx * (maa_v + mv)
            xr = xa + sx * (maa_r + mr)
            xg = xa + sx * (maa_g + mg)
            w = time_decay + jnp.tanh(xw @ decay_w1) @ decay_w2
            w = jnp.exp(-jnp.exp(w)).reshape(B, L, H, S)
            r = (xr @ Wr.T).reshape(B, L, H, S)
            k = (xk @ Wk.T).reshape(B, L, H, S)
            v = (xv @ Wv.T).reshape(B, L, H, S)
            g = jax.nn.silu(xg @ Wg.T)
            s0 = state[:, i0 + 2:i0 + 2 + S].reshape(B, H, S, S)

            def step(s, inp):
                k_l, v_l, w_l, r_l = inp
                a = k_l[..., :, None] * v_l[..., None, :]
                out = jnp.einsum('bhs,bhst->bht', r_l, faaaa * a + s)
                s_new = a + w_l[..., None] * s
                return (s_new, out)
            seq = tuple((z.transpose(1, 0, 2, 3) for z in (k, v, w, r)))
            _, outs = jax.lax.scan(step, s0, seq)
            y = outs.transpose(1, 0, 2, 3)
            gm = jnp.mean(y, axis=-1, keepdims=True)
            gv = jnp.mean((y - gm) ** 2, axis=-1, keepdims=True)
            y = ((y - gm) * jax.lax.rsqrt(gv + EPS)).reshape(B, L, C) * gn_w + gn_b
            x = x + y * g @ Wo.T
            xc = _ln(x, ln2_w, ln2_b)
            sxc = jnp.concatenate([state[:, i0][:, None], xc[:, :-1]], axis=1) - xc
            xk2 = xc + sxc * fmaa_k
            xr2 = xc + sxc * fmaa_r
            rr = jax.nn.sigmoid(xr2 @ fWr.T)
            kk = jnp.square(jax.nn.relu(xk2 @ fWk.T))
            x = x + rr * (kk @ fWv.T)
            return x
        key = jax.random.key(seed)
        B, L, C, H = (8, 128, 512, N_HEAD)
        S = C // H
        DM, DD = (32, 64)
        ks = jax.random.split(key, 32)
        n = lambda k, shp, s=1.0: jax.random.normal(k, shp, dtype=jnp.float32) * s
        u = lambda k, shp: jax.random.uniform(k, shp, dtype=jnp.float32)
        inp = {'x': n(ks[0], (B, L, C)), 'state': n(ks[1], (B, 2 + S, C), 0.1), 'i': 0, 'ln1_w': jnp.ones((C,), jnp.float32), 'ln1_b': jnp.zeros((C,), jnp.float32), 'ln2_w': jnp.ones((C,), jnp.float32), 'ln2_b': jnp.zeros((C,), jnp.float32), 'maa_x': u(ks[2], (C,)), 'maa_w': u(ks[3], (C,)), 'maa_k': u(ks[4], (C,)), 'maa_v': u(ks[5], (C,)), 'maa_r': u(ks[6], (C,)), 'maa_g': u(ks[7], (C,)), 'maa_w1': n(ks[8], (C, 5 * DM), 0.02), 'maa_w2': n(ks[9], (5, DM, C), 0.02), 'time_decay': n(ks[10], (C,), 0.5), 'decay_w1': n(ks[11], (C, DD), 0.02), 'decay_w2': n(ks[12], (DD, C), 0.02), 'faaaa': n(ks[13], (H, S, 1), 0.1), 'Wr': n(ks[14], (C, C), 0.02), 'Wk': n(ks[15], (C, C), 0.02), 'Wv': n(ks[16], (C, C), 0.02), 'Wg': n(ks[17], (C, C), 0.02), 'Wo': n(ks[18], (C, C), 0.02), 'gn_w': jnp.ones((C,), jnp.float32), 'gn_b': jnp.zeros((C,), jnp.float32), 'fmaa_k': u(ks[19], (C,)), 'fmaa_r': u(ks[20], (C,)), 'fWk': n(ks[21], (C, C), 0.02), 'fWr': n(ks[22], (C, C), 0.02), 'fWv': n(ks[23], (C, C), 0.02)}
        return inp
    _L1_xattn_all = _L1_xattn_setup()
    _L1_xattn_in = {k: v for k, v in _L1_xattn_all.items() if k in ('ln1_w', 'ln1_b', 'ln2_w', 'ln2_b', 'maa_x', 'maa_w', 'maa_k', 'maa_v', 'maa_r', 'maa_g', 'maa_w1', 'maa_w2', 'time_decay', 'decay_w1', 'decay_w2', 'faaaa', 'Wr', 'Wk', 'Wv', 'Wg', 'Wo', 'gn_w', 'gn_b', 'fmaa_k', 'fmaa_r', 'fWk', 'fWr', 'fWv')}
    del _L1_xattn_all
    return {'x': x, 'ctx_2048': ctx_2048, 'mask_1x1xSxS2_fc1': mask_1x1xSxS2_fc1, 'mask_Bx1xSxS2_ff1': mask_Bx1xSxS2_ff1, 'L0_xattn_ln1_s': _L0_xattn_in['ln1_s'], 'L0_xattn_ln1_b': _L0_xattn_in['ln1_b'], 'L0_xattn_w_qkv': _L0_xattn_in['w_qkv'], 'L0_xattn_b_qkv': _L0_xattn_in['b_qkv'], 'L0_xattn_w_ao': _L0_xattn_in['w_ao'], 'L0_xattn_b_ao': _L0_xattn_in['b_ao'], 'L0_xattn_ln2_s': _L0_xattn_in['ln2_s'], 'L0_xattn_ln2_b': _L0_xattn_in['ln2_b'], 'L0_xattn_w_q': _L0_xattn_in['w_q'], 'L0_xattn_b_q': _L0_xattn_in['b_q'], 'L0_xattn_w_kv': _L0_xattn_in['w_kv'], 'L0_xattn_b_kv': _L0_xattn_in['b_kv'], 'L0_xattn_w_co': _L0_xattn_in['w_co'], 'L0_xattn_b_co': _L0_xattn_in['b_co'], 'L0_xattn_ln3_s': _L0_xattn_in['ln3_s'], 'L0_xattn_ln3_b': _L0_xattn_in['ln3_b'], 'L0_xattn_w1': _L0_xattn_in['w1'], 'L0_xattn_b1': _L0_xattn_in['b1'], 'L0_xattn_w2': _L0_xattn_in['w2'], 'L0_xattn_b2': _L0_xattn_in['b2'], 'L1_xattn_ln1_w': _L1_xattn_in['ln1_w'], 'L1_xattn_ln1_b': _L1_xattn_in['ln1_b'], 'L1_xattn_ln2_w': _L1_xattn_in['ln2_w'], 'L1_xattn_ln2_b': _L1_xattn_in['ln2_b'], 'L1_xattn_maa_x': _L1_xattn_in['maa_x'], 'L1_xattn_maa_w': _L1_xattn_in['maa_w'], 'L1_xattn_maa_k': _L1_xattn_in['maa_k'], 'L1_xattn_maa_v': _L1_xattn_in['maa_v'], 'L1_xattn_maa_r': _L1_xattn_in['maa_r'], 'L1_xattn_maa_g': _L1_xattn_in['maa_g'], 'L1_xattn_maa_w1': _L1_xattn_in['maa_w1'], 'L1_xattn_maa_w2': _L1_xattn_in['maa_w2'], 'L1_xattn_time_decay': _L1_xattn_in['time_decay'], 'L1_xattn_decay_w1': _L1_xattn_in['decay_w1'], 'L1_xattn_decay_w2': _L1_xattn_in['decay_w2'], 'L1_xattn_faaaa': _L1_xattn_in['faaaa'], 'L1_xattn_Wr': _L1_xattn_in['Wr'], 'L1_xattn_Wk': _L1_xattn_in['Wk'], 'L1_xattn_Wv': _L1_xattn_in['Wv'], 'L1_xattn_Wg': _L1_xattn_in['Wg'], 'L1_xattn_Wo': _L1_xattn_in['Wo'], 'L1_xattn_gn_w': _L1_xattn_in['gn_w'], 'L1_xattn_gn_b': _L1_xattn_in['gn_b'], 'L1_xattn_fmaa_k': _L1_xattn_in['fmaa_k'], 'L1_xattn_fmaa_r': _L1_xattn_in['fmaa_r'], 'L1_xattn_fWk': _L1_xattn_in['fWk'], 'L1_xattn_fWr': _L1_xattn_in['fWr'], 'L1_xattn_fWv': _L1_xattn_in['fWv']}

def reference(x, ctx_2048, mask_1x1xSxS2_fc1, mask_Bx1xSxS2_ff1, L0_xattn_ln1_s, L0_xattn_ln1_b, L0_xattn_w_qkv, L0_xattn_b_qkv, L0_xattn_w_ao, L0_xattn_b_ao, L0_xattn_ln2_s, L0_xattn_ln2_b, L0_xattn_w_q, L0_xattn_b_q, L0_xattn_w_kv, L0_xattn_b_kv, L0_xattn_w_co, L0_xattn_b_co, L0_xattn_ln3_s, L0_xattn_ln3_b, L0_xattn_w1, L0_xattn_b1, L0_xattn_w2, L0_xattn_b2, L1_xattn_ln1_w, L1_xattn_ln1_b, L1_xattn_ln2_w, L1_xattn_ln2_b, L1_xattn_maa_x, L1_xattn_maa_w, L1_xattn_maa_k, L1_xattn_maa_v, L1_xattn_maa_r, L1_xattn_maa_g, L1_xattn_maa_w1, L1_xattn_maa_w2, L1_xattn_time_decay, L1_xattn_decay_w1, L1_xattn_decay_w2, L1_xattn_faaaa, L1_xattn_Wr, L1_xattn_Wk, L1_xattn_Wv, L1_xattn_Wg, L1_xattn_Wo, L1_xattn_gn_w, L1_xattn_gn_b, L1_xattn_fmaa_k, L1_xattn_fmaa_r, L1_xattn_fWk, L1_xattn_fWr, L1_xattn_fWv):
    import jax
    import jax.numpy as jnp

    def _L0_xattn_ref(hidden_states, encoder_states, ltor_mask, cross_mask, ln1_s, ln1_b, w_qkv, b_qkv, w_ao, b_ao, ln2_s, ln2_b, w_q, b_q, w_kv, b_kv, w_co, b_co, ln3_s, ln3_b, w1, b1, w2, b2):
        import jax, jax.numpy as jnp
        import numpy as np
        H = 512
        NH = 16
        HD = H // NH
        EPS = 1e-05

        def gelu(x):
            return 0.5 * x * (1.0 + jnp.tanh(0.7978845608028654 * x * (1.0 + 0.044715 * x * x)))

        def layernorm(x, scale, bias):
            m = jnp.mean(x, axis=-1, keepdims=True)
            v = jnp.mean(jnp.square(x - m), axis=-1, keepdims=True)
            return (x - m) * jax.lax.rsqrt(v + EPS) * scale + bias

        def split_heads(x):
            b, s, _ = x.shape
            return x.reshape(b, s, NH, HD).transpose(0, 2, 1, 3)

        def merge_heads(x):
            b, nh, s, hd = x.shape
            return x.transpose(0, 2, 1, 3).reshape(b, s, nh * hd)

        def attention(q, k, v, mask):
            scores = jnp.einsum('bhqd,bhkd->bhqk', q, k) / jnp.sqrt(jnp.float32(HD))
            scores = scores * mask - 10000.0 * (1.0 - mask)
            probs = jax.nn.softmax(scores, axis=-1)
            return jnp.einsum('bhqk,bhkd->bhqd', probs, v)
        ln_out = layernorm(hidden_states, ln1_s, ln1_b)
        qkv = ln_out @ w_qkv + b_qkv
        q, k, v = jnp.split(qkv, 3, axis=-1)
        ctx = merge_heads(attention(split_heads(q), split_heads(k), split_heads(v), ltor_mask))
        attn_out = ctx @ w_ao + b_ao
        x = hidden_states + attn_out
        ln_out = layernorm(x, ln2_s, ln2_b)
        q = ln_out @ w_q + b_q
        kv = encoder_states @ w_kv + b_kv
        k, v = jnp.split(kv, 2, axis=-1)
        ctx = merge_heads(attention(split_heads(q), split_heads(k), split_heads(v), cross_mask))
        cross_out = ctx @ w_co + b_co
        x = x + cross_out
        ln_out = layernorm(x, ln3_s, ln3_b)
        mlp_out = gelu(ln_out @ w1 + b1) @ w2 + b2
        return x + mlp_out

    def _L1_xattn_ref(x, state, i, ln1_w, ln1_b, ln2_w, ln2_b, maa_x, maa_w, maa_k, maa_v, maa_r, maa_g, maa_w1, maa_w2, time_decay, decay_w1, decay_w2, faaaa, Wr, Wk, Wv, Wg, Wo, gn_w, gn_b, fmaa_k, fmaa_r, fWk, fWr, fWv):
        import jax, jax.numpy as jnp
        import numpy as np
        N_HEAD = 32
        EPS = 1e-05

        def _ln(x, w, b):
            m = jnp.mean(x, axis=-1, keepdims=True)
            v = jnp.mean((x - m) ** 2, axis=-1, keepdims=True)
            return (x - m) * jax.lax.rsqrt(v + EPS) * w + b

        def _forward(x, state, i, ln1_w, ln1_b, ln2_w, ln2_b, maa_x, maa_w, maa_k, maa_v, maa_r, maa_g, maa_w1, maa_w2, time_decay, decay_w1, decay_w2, faaaa, Wr, Wk, Wv, Wg, Wo, gn_w, gn_b, fmaa_k, fmaa_r, fWk, fWr, fWv):
            B, L, C = x.shape
            H = N_HEAD
            S = C // H
            i0 = (2 + S) * i
            xa = _ln(x, ln1_w, ln1_b)
            sx = jnp.concatenate([state[:, i0 + 1][:, None], xa[:, :-1]], axis=1) - xa
            xxx = xa + sx * maa_x
            t = jnp.tanh(xxx @ maa_w1).reshape(B, L, 5, -1)
            m = jnp.einsum('blfd,fdc->blfc', t, maa_w2)
            mw, mk, mv, mr, mg = (m[:, :, j] for j in range(5))
            xw = xa + sx * (maa_w + mw)
            xk = xa + sx * (maa_k + mk)
            xv = xa + sx * (maa_v + mv)
            xr = xa + sx * (maa_r + mr)
            xg = xa + sx * (maa_g + mg)
            w = time_decay + jnp.tanh(xw @ decay_w1) @ decay_w2
            w = jnp.exp(-jnp.exp(w)).reshape(B, L, H, S)
            r = (xr @ Wr.T).reshape(B, L, H, S)
            k = (xk @ Wk.T).reshape(B, L, H, S)
            v = (xv @ Wv.T).reshape(B, L, H, S)
            g = jax.nn.silu(xg @ Wg.T)
            s0 = state[:, i0 + 2:i0 + 2 + S].reshape(B, H, S, S)

            def step(s, inp):
                k_l, v_l, w_l, r_l = inp
                a = k_l[..., :, None] * v_l[..., None, :]
                out = jnp.einsum('bhs,bhst->bht', r_l, faaaa * a + s)
                s_new = a + w_l[..., None] * s
                return (s_new, out)
            seq = tuple((z.transpose(1, 0, 2, 3) for z in (k, v, w, r)))
            _, outs = jax.lax.scan(step, s0, seq)
            y = outs.transpose(1, 0, 2, 3)
            gm = jnp.mean(y, axis=-1, keepdims=True)
            gv = jnp.mean((y - gm) ** 2, axis=-1, keepdims=True)
            y = ((y - gm) * jax.lax.rsqrt(gv + EPS)).reshape(B, L, C) * gn_w + gn_b
            x = x + y * g @ Wo.T
            xc = _ln(x, ln2_w, ln2_b)
            sxc = jnp.concatenate([state[:, i0][:, None], xc[:, :-1]], axis=1) - xc
            xk2 = xc + sxc * fmaa_k
            xr2 = xc + sxc * fmaa_r
            rr = jax.nn.sigmoid(xr2 @ fWr.T)
            kk = jnp.square(jax.nn.relu(xk2 @ fWk.T))
            x = x + rr * (kk @ fWv.T)
            return x
        return _forward(x, state, i, ln1_w, ln1_b, ln2_w, ln2_b, maa_x, maa_w, maa_k, maa_v, maa_r, maa_g, maa_w1, maa_w2, time_decay, decay_w1, decay_w2, faaaa, Wr, Wk, Wv, Wg, Wo, gn_w, gn_b, fmaa_k, fmaa_r, fWk, fWr, fWv)
    x = _L0_xattn_ref(x, ctx_2048, mask_1x1xSxS2_fc1, mask_Bx1xSxS2_ff1, L0_xattn_ln1_s, L0_xattn_ln1_b, L0_xattn_w_qkv, L0_xattn_b_qkv, L0_xattn_w_ao, L0_xattn_b_ao, L0_xattn_ln2_s, L0_xattn_ln2_b, L0_xattn_w_q, L0_xattn_b_q, L0_xattn_w_kv, L0_xattn_b_kv, L0_xattn_w_co, L0_xattn_b_co, L0_xattn_ln3_s, L0_xattn_ln3_b, L0_xattn_w1, L0_xattn_b1, L0_xattn_w2, L0_xattn_b2)
    x = _L1_xattn_ref(x, ctx_2048, 0, L1_xattn_ln1_w, L1_xattn_ln1_b, L1_xattn_ln2_w, L1_xattn_ln2_b, L1_xattn_maa_x, L1_xattn_maa_w, L1_xattn_maa_k, L1_xattn_maa_v, L1_xattn_maa_r, L1_xattn_maa_g, L1_xattn_maa_w1, L1_xattn_maa_w2, L1_xattn_time_decay, L1_xattn_decay_w1, L1_xattn_decay_w2, L1_xattn_faaaa, L1_xattn_Wr, L1_xattn_Wk, L1_xattn_Wv, L1_xattn_Wg, L1_xattn_Wo, L1_xattn_gn_w, L1_xattn_gn_b, L1_xattn_fmaa_k, L1_xattn_fmaa_r, L1_xattn_fWk, L1_xattn_fWr, L1_xattn_fWv)
    return x

_drawn_inputs = setup_inputs


def setup_inputs(seed=0):
    import zlib

    import numpy as np

    out = dict(_drawn_inputs(seed))
    spreads = {'L0_xattn_ln1_s': (1.0, 0.6),
     'L0_xattn_ln1_b': (0.0, 0.392),
     'L0_xattn_b_qkv': (0.0, 0.1),
     'L0_xattn_b_ao': (0.0, 0.1),
     'L0_xattn_ln2_s': (1.0, 0.6),
     'L0_xattn_ln2_b': (0.0, 2.0),
     'L0_xattn_b_q': (0.0, 2.0),
     'L0_xattn_b_kv': (0.0, 0.1),
     'L0_xattn_b_co': (0.0, 0.1),
     'L0_xattn_ln3_s': (1.0, 0.2),
     'L0_xattn_ln3_b': (0.0, 0.318),
     'L0_xattn_b1': (0.0, 0.1),
     'L0_xattn_b2': (0.0, 0.1),
     'L1_xattn_ln1_w': (1.0, 0.2),
     'L1_xattn_ln1_b': (0.0, 0.297),
     'L1_xattn_ln2_w': (1.0, 0.6),
     'L1_xattn_ln2_b': (0.0, 0.8),
     'L1_xattn_gn_w': (1.0, 0.6),
     'L1_xattn_gn_b': (0.0, 0.8)}
    factors = {'L0_xattn_w_q': 52.205,
     'L1_xattn_maa_x': 7.399,
     'L1_xattn_maa_w': 8.0,
     'L1_xattn_maa_w1': 3.734,
     'L1_xattn_maa_w2': 3.727,
     'L1_xattn_decay_w1': 8.0,
     'L1_xattn_decay_w2': 8.0,
     'L1_xattn_faaaa': 3.942,
     'L1_xattn_fmaa_k': 2.838,
     'L1_xattn_fmaa_r': 8.0,
     'L1_xattn_fWr': 7.829}
    for name, (base, spread) in spreads.items():
        noise = np.random.default_rng([zlib.crc32(name.encode()), seed]).standard_normal(out[name].shape)
        drawn = base * np.exp(spread * noise) if base else spread * noise
        out[name] = jnp.asarray(drawn.astype(out[name].dtype))
    for name, factor in factors.items():
        out[name] = (out[name] * factor).astype(out[name].dtype)
    return out
```

```python
from contextlib import ExitStack

import concourse.bass as bass
import numpy as np
from concourse import mybir

F32 = mybir.dt.float32
ALU = mybir.AluOpType
ACT = mybir.ActivationFunctionType
AX = mybir.AxisListType.X

P = 128
B, T, C = 16, 256, 512
KC = C // P
TC = T // P
NH, HD = 16, 32
HPC = P // HD
FF = 4 * C
FC = FF // P
RH, RS = 32, 16
DM, NMIX = 32, 5
DD = 64
EPS = 1e-5
SCALE = float(HD) ** -0.5
GELU_A, GELU_B = 0.7978845608028654, 0.044715

COLUMNS = [("ln1_s", KC), ("ln1_b", KC), ("b_q", KC), ("b_k", KC), ("b_v", KC), ("ln2_s", KC), ("ln2_b", KC), ("b_qx", KC),
           ("b_kx", KC), ("b_vx", KC), ("ln3_s", KC), ("ln3_b", KC), ("b1", FC), ("rln1_w", KC), ("rln1_b", KC),
           ("rln2_w", KC), ("rln2_b", KC), ("maa_x", KC), ("maa_w", KC), ("maa_k", KC), ("maa_v", KC),
           ("maa_r", KC), ("maa_g", KC), ("time_decay", KC), ("faaaa", KC), ("fmaa_k", KC), ("fmaa_r", KC)]
COL_AT, NCOL = {}, 0
for _name, _n in COLUMNS:
    COL_AT[_name] = NCOL
    NCOL += _n
ROWS = ["b_ao", "b_co", "b2", "gn_w", "gn_b"]


class Units:

    def __init__(self, uses):
        self.uses = uses
        self.at = {name: i for i, (name, _, _) in enumerate(uses)}
        self.per = {}
        self.order = {}
        for name, _, reader in uses:
            self.per[reader] = self.per.get(reader, 0) + 1
            self.order[name] = self.per[reader]

    def filled(self, it, name):
        return it * len(self.uses) + (self.at[name] + 1)

    def emptied(self, it, name):
        per = self.per[self.reader(name)]
        return it * per + (per + self.order[name])

    def emptied_last(self, it, name):
        return it * self.per[self.reader(name)] + self.order[name]

    def reader(self, name):
        return self.uses[self.at[name]][2]

    def unit(self, name):
        return self.uses[self.at[name]][1]

    def before(self, it, name):
        here = self.at[name]
        same = [u for u in self.uses if u[1] == self.unit(name)]
        k = same.index(self.uses[here])
        last = same[k - 1]
        per = self.per[last[2]]
        return last[2], it * per + (self.order[last[0]] + (per if k else 0))


def col(cols, name, c):
    return cols[:, COL_AT[name] + c:COL_AT[name] + c + 1]


def layernorm_stats(nc, x, stats, mv, ve):
    for tc in range(TC):
        nc.vector.bn_stats(stats[:, tc, :], x[:, tc, :])
    nc.vector.drain()
    for tc in range(TC):
        nc.vector.bn_aggr(mv[:, tc, :], stats[:, tc, :])
    nc.vector.drain()
    return nc.vector.tensor_scalar(ve[:, :], mv[:, :, 1], EPS, None, ALU.add)


def layernorm_apply(nc, x, mv, rstd, xhat):
    for tc in range(TC):
        last = nc.vector.tensor_scalar(xhat[:, tc, :], x[:, tc, :], mv[:, tc, 0:1], rstd[:, tc:tc + 1],
                                       ALU.subtract, ALU.mult)
    return last


def phase_a(nc, d, w, dsem):
    with ExitStack() as ctx:
        def sb(name, *shape):
            return ctx.enter_context(nc.sbuf_tensor("a_" + name, list(shape), F32))

        def sem(name):
            return ctx.enter_context(nc.semaphore("a_" + name))

        units = Units([(n, i % 3, r) for i, (n, r) in enumerate([
            ("encT0", "act"), ("encT1", "act"), ("kx0", "act"), ("kx1", "act"),
            ("lnT00", "act"), ("lnT01", "act"), ("q00", "act"), ("q01", "act"), ("k0", "act"), ("k1", "act"),
            ("v00", "dve"), ("v01", "dve"), ("ctx00", "act"), ("ctx01", "act"), ("ctx02", "act"), ("ctx03", "act"), ("out00", "dve"), ("out01", "dve"),
            ("v10", "dve"), ("v11", "dve"), ("lnT10", "act"), ("lnT11", "act"), ("q10", "act"), ("q11", "act"),
            ("ctx10", "act"), ("ctx11", "act"), ("ctx12", "act"), ("ctx13", "act"), ("out10", "dve"), ("out11", "dve")])])

        x_in = sb("x_in", P, TC, C)
        enc = sb("enc", P, TC, C)
        mask_in = sb("mask_in", P, TC, T)
        mask = [sb("mask_self", P, TC, T), sb("mask_cross", P, TC, T)]
        mneg = [sb("mneg_self", P, TC, T), sb("mneg_cross", P, TC, T)]
        xhat = sb("xhat", P, TC, C)
        lnT = sb("lnT", P, KC, T)
        encT = sb("encT", P, KC, T)
        qT = sb("qT", P, KC, T)
        kT = [sb("kT_self", P, KC, T), sb("kT_cross", P, KC, T)]
        v = [sb("v_self", P, TC, C), sb("v_cross", P, TC, C)]
        ctxT = lnT
        xb = sb("xb", P, TC, C)
        x3 = sb("x3", P, TC, C)
        t = sb("t", P, 2, TC, T)
        prob = sb("prob", P, 4, TC, T)
        probT = sb("probT", P, 2, TC, T)
        tmin = sb("tmin", P, NH, TC)
        psums = sb("psums", P, NH, TC)
        rsums = sb("rsums", P, NH, TC)
        stats = sb("stats", P, TC, 6)
        mv = sb("mv", P, TC, 2)
        ve = sb("ve", P, TC)
        rstd = sb("rstd", P, TC)
        bq = sb("bq", P, 2, KC)
        row_out = [sb("row_" + n, P, C) for n in ("b_ao", "b_co")]

        ps = ctx.enter_context(nc.psum_tensor("a_ps", [P, 3, 512], F32))
        ps_s = ctx.enter_context(nc.psum_tensor("a_ps_s", [P, 2, TC, T], F32))
        ps_t = ctx.enter_context(nc.psum_tensor("a_ps_t", [P, 2, TC, T], F32))

        rows_loaded = sem("rows_loaded")
        enc_loaded, x_loaded, mask_loaded = sem("enc_loaded"), sem("x_loaded"), sem("mask_loaded")
        self_mask_loaded = sem("self_mask_loaded")
        x3_stored = sem("x3_stored")
        x_released = sem("x_released")
        mask_released = sem("mask_released")
        filled = sem("filled")
        emptied = {"act": sem("emptied_act"), "dve": sem("emptied_dve")}
        stats_ready, rstd_ready, xhat_ready = sem("stats_ready"), sem("rstd_ready"), sem("xhat_ready")
        xb_ready, x3_ready = sem("xb_ready"), sem("x3_ready")
        bq_ready = sem("bq_ready")
        s_filled, s_read, t_ready = sem("s_filled"), sem("s_read"), sem("t_ready")
        exp_done, rsum_ready, prob_ready = sem("exp_done"), sem("rsum_ready"), sem("prob_ready")
        pt_filled, pt_copied, pv_done = sem("pt_filled"), sem("pt_copied"), sem("pv_done")
        LT, LV = 3, 4

        def head(it, r, h):
            return it * (2 * NH) + (r * NH + h + 1)

        x_d = d["x"].rearrange("b (c p) n -> b p c n", p=P)
        enc_d = d["ctx_2048"].rearrange("b (c p) n -> b p c n", p=P)
        mask_d = d["mask_cross"].rearrange("b o (c p) n -> b p (o c) n", p=P)
        self_d = d["mask_self"].rearrange("a o (c p) n -> p (a o c) n", p=P)
        x3_d = d["x3"].rearrange("b (c p) n -> b p c n", p=P)

        with nc.Block() as block:

            @block.sync
            def _(sp):
                sp.sem_inc(x3_stored, 16)
                sp.dma_start(w["ident"][:, :], d["ident"]).then_inc(dsem["ident"], 16)
                sp.dma_start(enc[:, :, :], enc_d[0]).then_inc(enc_loaded, 16)
                sp.dma_start(x_in[:, :, :], x_d[0]).then_inc(x_loaded, 16)
                sp.dma_start(w["cols"][:, :], d["cols"]).then_inc(dsem["cols"], 16)
                sp.dma_start(w["kv"][:, :, :], d["w_kv"].rearrange("(c p) n -> p c n", p=P)).then_inc(dsem["kv"], 16)
                sp.dma_start(w["qkv"][:, :, :], d["w_qkv"].rearrange("(c p) n -> p c n", p=P)).then_inc(dsem["qkv"], 16)
                for n, row in zip(("b_ao", "b_co"), row_out):
                    sp.dma_start(row[:, :], d["rows"][ROWS.index(n)].partition_broadcast(P)).then_inc(rows_loaded, 16)
                sp.dma_start(mask[0][:, :, :], self_d).then_inc(self_mask_loaded, 16)
                sp.dma_start(mask_in[:, :, :], mask_d[0]).then_inc(mask_loaded, 16)
                for n in ("ao", "q", "co"):
                    sp.dma_start(w[n][:, :, :], d["w_" + n].rearrange("(c p) n -> p c n", p=P)).then_inc(dsem[n], 16)
                sp.dma_start(w["w1"][:, :, :], d["w1"].rearrange("(c p) n -> p c n", p=P)).then_inc(dsem["w1"], 16)
                sp.dma_start(w["w2"][:, :, :], d["w2"].rearrange("(c p) n -> p c n", p=P)).then_inc(dsem["w2"], 16)
                with sp.Fori(0, B - 1) as it:
                    sp.wait_ge(filled, units.filled(it, "encT1"))
                    sp.dma_start(enc[:, :, :], enc_d[it + 1]).then_inc(enc_loaded, 16)
                    sp.wait_ge(x_released, it + 1)
                    sp.dma_start(x_in[:, :, :], x_d[it + 1]).then_inc(x_loaded, 16)
                    sp.wait_ge(mask_released, it + 1)
                    sp.dma_start(mask_in[:, :, :], mask_d[it + 1]).then_inc(mask_loaded, 16)
                    sp.wait_ge(x3_ready, it + 1)
                    sp.dma_start(x3_d[it], x3[:, :, :]).then_inc(x3_stored, 16)
                sp.wait_ge(x3_ready, B)
                sp.dma_start(x3_d[B - 1], x3[:, :, :]).then_inc(x3_stored, 16)
                sp.wait_ge(x3_stored, (B + 1) * 16)

            @block.gpsimd
            def _(pool):
                nc.gpsimd.memset(w["neghalf"][:, :], -0.5)
                nc.gpsimd.drain()
                pool.wait_ge(rows_loaded, 32)

                def inverse_deviation(k):
                    pool.wait_ge(stats_ready, k)
                    nc.gpsimd.tensor_tensor(rstd[:, :], ve[:, :], w["neghalf"][:, :], ALU.pow).then_inc(rstd_ready, 1)

                inverse_deviation(1)

                def item(it, last):
                    for r in range(2):
                        if r == 0:
                            pool.wait_ge(xhat_ready, 2 * it + 1)
                            pool.wait_ge(emptied["dve"], units.emptied_last(it, "out11"))
                            src = x_in
                        else:
                            inverse_deviation(2 * it + 2)
                            pool.wait_ge(xhat_ready, 2 * it + 2)
                            src = xb
                        done = nc.gpsimd.tensor_tensor(
                            xb[:, :, :], src[:, :, :], row_out[r][:, :].unsqueeze(1).to_broadcast([P, TC, C]), ALU.add)
                        done.then_inc(xb_ready, 1)
                        if r == 0:
                            pool.wait_ge(xb_ready, 2 * it + 1)
                            pool.sem_inc(x_released, 1)
                        for h in range(NH):
                            pool.wait_ge(rsum_ready, head(it, r, h))
                            nc.gpsimd.tensor_tensor(prob[:, h % 4, :, :], prob[:, h % 4, :, :],
                                                    rsums[:, h, :].unsqueeze(2).to_broadcast([P, TC, T]),
                                                    ALU.mult).then_inc(prob_ready, 1)
                    if not last:
                        inverse_deviation(2 * it + 3)

                with pool.Fori(0, B - 1) as it:
                    item(it, False)
                item(B - 1, True)

            @block.scalar
            def _(act):
                act.wait_ge(dsem["cols"], 16)
                act.sem_inc(emptied["act"], units.per["act"])
                for r, n in enumerate(("b_q", "b_qx")):
                    nc.scalar.mul(bq[:, r, :], w["cols"][:, COL_AT[n]:COL_AT[n] + KC], -SCALE)
                nc.scalar.drain()

                def move(it, name, outs, scales, biases):
                    act.wait_ge(filled, units.filled(it, name))
                    u = ps[:, units.unit(name), :].rearrange("p (a n) -> p a n", a=2)
                    for a in range(2):
                        op = nc.scalar.activation(outs[a], u[:, a, :], ACT.Identity, bias=biases[a], scale=scales[a])
                    op.then_inc(emptied["act"], 1)

                def move_all(it, prefix, out, scale, bias):
                    for a in range(2):
                        m = (2 * a, 2 * a + 1)
                        scales = [col(w["cols"], scale, c) if isinstance(scale, str) else scale for c in m]
                        biases = [bias(c) for c in m]
                        move(it, prefix + str(a), [out[:, c, :] for c in m], scales, biases)

                with act.Fori(0, B) as it:
                    for a in range(2):
                        act.wait_ge(filled, units.filled(it, f"encT{a}"))
                        nc.scalar.copy(encT[:, 2 * a:2 * a + 2, :],
                                       ps[:, units.unit(f"encT{a}"), :].rearrange("p (a n) -> p a n", a=2)
                                       ).then_inc(emptied["act"], 1)
                    move_all(it, "kx", kT[1], 1.0, lambda c: col(w["cols"], "b_kx", c))
                    for r in range(2):
                        ln = ("ln1", "ln2")[r]
                        move_all(it, f"lnT{r}", lnT, ln + "_s", lambda c: col(w["cols"], ln + "_b", c))
                        move_all(it, f"q{r}", qT, -SCALE, lambda c: bq[:, r, c:c + 1])
                        if r == 0:
                            move_all(it, "k", kT[0], 1.0, lambda c: col(w["cols"], "b_k", c))
                        for n in range(NH + LV + 1):
                            if n < NH:
                                act.wait_ge(t_ready, head(it, r, n))
                                for tc in range(TC):
                                    op = nc.scalar.activation(prob[:, n % 4, tc, :], t[:, n % 2, tc, :], ACT.Exp,
                                                              bias=tmin[:, n, tc:tc + 1], scale=-1.0,
                                                              accum_out=psums[:, n, tc:tc + 1])
                                op.then_inc(exp_done, 1)
                            h = n - LT
                            if 0 <= h < NH:
                                act.wait_ge(pt_filled, head(it, r, h))
                                if h >= 2:
                                    act.wait_ge(pv_done, head(it, r, h - 2))
                                nc.scalar.copy(probT[:, h % 2, :, :], ps_t[:, h % 2, :, :]).then_inc(pt_copied, 1)
                            h = n - LV - 1
                            if h >= 0 and h % HPC == HPC - 1:
                                m = h // HPC
                                name = f"ctx{r}{m}"
                                act.wait_ge(filled, units.filled(it, name))
                                nc.scalar.activation(ctxT[:, m, :], ps[:, units.unit(name), 0:T], ACT.Identity,
                                                     bias=col(w["cols"], ("b_v", "b_vx")[r], m)).then_inc(emptied["act"], 1)

            @block.vector
            def _(dve):
                dve.sem_inc(emptied["dve"], units.per["dve"])
                dve.wait_ge(self_mask_loaded, 16)
                nc.vector.tensor_scalar(mneg[0][:, :, :], mask[0][:, :, :], -10000.0, 10000.0, ALU.mult, ALU.add)
                dve.wait_ge(rows_loaded, 32)

                def normalise(x, k):
                    layernorm_stats(nc, x, stats, mv, ve).then_inc(stats_ready, 1)
                    dve.wait_ge(rstd_ready, k)
                    layernorm_apply(nc, x, mv, rstd, xhat).then_inc(xhat_ready, 1)

                def move_v(it, r):
                    for tc in range(TC):
                        name = f"v{r}{tc}"
                        dve.wait_ge(filled, units.filled(it, name))
                        nc.vector.tensor_copy(v[r][:, tc, :], ps[:, units.unit(name), :]).then_inc(emptied["dve"], 1)

                def attention(it, r):
                    for n in range(NH + 1):
                        if n < NH:
                            dve.wait_ge(s_filled, head(it, r, n))
                            if n >= 2:
                                dve.wait_ge(exp_done, head(it, r, n - 2))
                            nc.vector.tensor_tensor(t[:, n % 2, :, :], ps_s[:, n % 2, :, :], mask[r][:, :, :],
                                                    ALU.mult).then_inc(s_read, 1)
                            nc.vector.drain()
                            for tc in range(TC):
                                s = t[:, n % 2, tc, :]
                                op = nc.vector.tensor_tensor_reduce(
                                    out=s, in0=s, in1=mneg[r][:, tc, :], scale=1.0, scalar=3.0e38,
                                    op0=ALU.add, op1=ALU.min, accum_out=tmin[:, n, tc:tc + 1])
                            op.then_inc(t_ready, 1)
                        if n >= 1:
                            dve.wait_ge(exp_done, head(it, r, n - 1))
                            nc.vector.reciprocal(rsums[:, n - 1, :], psums[:, n - 1, :]).then_inc(rsum_ready, 1)

                def residual(it, r, out):
                    dve.wait_ge(xb_ready, 2 * it + r + 1)
                    for tc in range(TC):
                        name = f"out{r}{tc}"
                        dve.wait_ge(filled, units.filled(it, name))
                        if r == 1 and tc == 0:
                            dve.wait_ge(x3_stored, 16 * it + 16)
                        op = nc.vector.tensor_tensor(out[:, tc, :], ps[:, units.unit(name), :], xb[:, tc, :], ALU.add)
                        op.then_inc(emptied["dve"], 1)

                def item(it, last):
                    move_v(it, 0)
                    attention(it, 0)
                    residual(it, 0, xb)
                    nc.vector.drain()
                    normalise(xb, 2 * it + 2)
                    move_v(it, 1)
                    dve.wait_ge(mask_loaded, 16 * it + 16)
                    nc.vector.tensor_copy(mask[1][:, :, :], mask_in[:, :, :])
                    nc.vector.tensor_scalar(mneg[1][:, :, :], mask_in[:, :, :], -10000.0, 10000.0, ALU.mult, ALU.add)
                    nc.vector.drain()
                    dve.sem_inc(mask_released, 1)
                    attention(it, 1)
                    if not last:
                        dve.wait_ge(x_loaded, 16 * it + 32)
                        normalise(x_in, 2 * it + 3)
                    residual(it, 1, x3)
                    nc.vector.drain()
                    dve.sem_inc(x3_ready, 1)

                dve.wait_ge(x_loaded, 16)
                normalise(x_in, 1)
                with dve.Fori(0, B - 1) as it:
                    item(it, False)
                item(B - 1, True)

            @block.tensor
            def _(pe):
                pe.wait_ge(dsem["ident"], 16)

                def unit(it, name):
                    reader, value = units.before(it, name)
                    pe.wait_ge(emptied[reader], value)
                    return ps[:, units.unit(name), :]

                def transposes(it, prefix, src):
                    for a in range(2):
                        u = unit(it, prefix + str(a)).rearrange("p (a n) -> p a n", a=2)
                        for c in range(2):
                            for tc in range(TC):
                                op = nc.tensor.transpose(u[:, c, tc * P:(tc + 1) * P],
                                                         src[:, tc, (2 * a + c) * P:(2 * a + c + 1) * P], w["ident"][:, :])
                        op.then_inc(filled, 1)

                def to_channels(it, prefix, weights, n0, src):
                    for a in range(2):
                        u = unit(it, prefix + str(a)).rearrange("p (a n) -> p a n", a=2)
                        for m in range(2):
                            at = n0 + (2 * a + m) * P
                            for c in range(KC):
                                op = nc.tensor.matmul(u[:, m, :], weights[:, c, at:at + P], src[:, c, :],
                                                      start=(c == 0), stop=(c == KC - 1))
                        op.then_inc(filled, 1)

                def to_tokens(it, prefix, src, weights, n0):
                    for tc in range(TC):
                        u = unit(it, prefix + str(tc))
                        for c in range(KC):
                            op = nc.tensor.matmul(u, src[:, c, tc * P:(tc + 1) * P], weights[:, c, n0:n0 + C],
                                                  start=(c == 0), stop=(c == KC - 1))
                        op.then_inc(filled, 1)

                def attention(it, r):
                    for n in range(NH + LV):
                        if n < NH:
                            m, g = divmod(n, HPC)
                            rows_of = slice(HD * g, HD * (g + 1))
                            if n >= 2:
                                pe.wait_ge(s_read, head(it, r, n - 2))
                            for tc in range(TC):
                                op = nc.tensor.matmul(ps_s[:, n % 2, tc, :], qT[rows_of, m, tc * P:(tc + 1) * P],
                                                      kT[r][rows_of, m, :], start=True, stop=True)
                            op.then_inc(s_filled, 1)
                        h = n - LT
                        if 0 <= h < NH:
                            pe.wait_ge(prob_ready, head(it, r, h))
                            if h >= 2:
                                pe.wait_ge(pt_copied, head(it, r, h - 2))
                            for kc in range(TC):
                                for tc in range(TC):
                                    op = nc.tensor.transpose(ps_t[:, h % 2, kc, tc * P:(tc + 1) * P],
                                                             prob[:, h % 4, tc, kc * P:(kc + 1) * P], w["ident"][:, :])
                            op.then_inc(pt_filled, 1)
                        h = n - LV
                        if 0 <= h < NH:
                            m, g = divmod(h, HPC)
                            if g == 0:
                                u = unit(it, f"ctx{r}{m}")
                            pe.wait_ge(pt_copied, head(it, r, h))
                            for kc in range(TC):
                                op = nc.tensor.matmul(u[HD * g:HD * (g + 1), 0:T],
                                                      v[r][:, kc, h * HD:(h + 1) * HD], probT[:, h % 2, kc, :],
                                                      start=(kc == 0), stop=(kc == TC - 1))
                            op.then_inc(pv_done, 1)
                            if g == HPC - 1:
                                pe.wait_ge(pv_done, head(it, r, h))
                                pe.sem_inc(filled, 1)

                with pe.Fori(0, B) as it:
                    pe.wait_ge(enc_loaded, 16 * it + 16)
                    transposes(it, "encT", enc)
                    pe.wait_ge(dsem["kv"], 16)
                    pe.wait_ge(emptied["act"], units.emptied(it, "encT1"))
                    to_channels(it, "kx", w["kv"], 0, encT)
                    for r in range(2):
                        if r == 1:
                            to_tokens(it, "v1", encT, w["kv"], C)
                            pe.wait_ge(dsem["q"], 16)
                        pe.wait_ge(xhat_ready, 2 * it + r + 1)
                        transposes(it, f"lnT{r}", xhat)
                        pe.wait_ge(dsem["qkv"], 16)
                        pe.wait_ge(emptied["act"], units.emptied(it, f"lnT{r}1"))
                        if r == 0:
                            to_channels(it, "q0", w["qkv"], 0, lnT)
                            to_channels(it, "k", w["qkv"], C, lnT)
                            to_tokens(it, "v0", lnT, w["qkv"], 2 * C)
                            pe.wait_ge(emptied["act"], units.emptied(it, "k1"))
                        else:
                            to_channels(it, "q1", w["q"], 0, lnT)
                            pe.wait_ge(emptied["act"], units.emptied(it, "q11"))
                        pe.wait_ge(emptied["dve"], units.emptied(it, f"v{r}1"))
                        attention(it, r)
                        pe.wait_ge(dsem[("ao", "co")[r]], 16)
                        pe.wait_ge(emptied["act"], units.emptied(it, f"ctx{r}3"))
                        to_tokens(it, f"out{r}", ctxT, w[("ao", "co")[r]], 0)


def phase_b(nc, d, w, dsem):
    with ExitStack() as ctx:
        def sb(name, *shape):
            return ctx.enter_context(nc.sbuf_tensor("b_" + name, list(shape), F32))

        def sem(name):
            return ctx.enter_context(nc.semaphore("b_" + name))

        units = Units([("lnT0", 0, "act"), ("lnT1", 1, "act")] +
                      [(f"up{i}", (i + 2) % 6, "act") for i in range(FC // 2)] +
                      [("down0", 6, "dve"), ("down1", 7, "dve")])
        NU = FC // 2

        x_in = sb("x_in", P, TC, C)
        xb = sb("xb", P, TC, C)
        x4 = sb("x4", P, TC, C)
        xhat = sb("xhat", P, TC, C)
        lnT = sb("lnT", P, KC, T)
        h = sb("h", P, 2, 2, T)
        hh = sb("hh", P, 2, 2, T)
        act2 = sb("act2", P, FC, T)
        stats = sb("stats", P, TC, 6)
        mv = sb("mv", P, TC, 2)
        ve = sb("ve", P, TC)
        rstd = sb("rstd", P, TC)
        row_b2 = sb("row_b2", P, C)
        ps = ctx.enter_context(nc.psum_tensor("b_ps", [P, 8, 512], F32))

        row_loaded, x_loaded, x4_stored = sem("row_loaded"), sem("x_loaded"), sem("x4_stored")
        filled = sem("filled")
        emptied = {"act": sem("emptied_act"), "dve": sem("emptied_dve")}
        stats_ready, rstd_ready, xhat_ready = sem("stats_ready"), sem("rstd_ready"), sem("xhat_ready")
        xb_ready, x4_ready = sem("xb_ready"), sem("x4_ready")
        inner_ready, tanh_ready, gelu_ready = sem("inner_ready"), sem("tanh_ready"), sem("gelu_ready")

        x_d = d["x3"].rearrange("b (c p) n -> b p c n", p=P)
        x4_d = d["x4"].rearrange("b (c p) n -> b p c n", p=P)

        with nc.Block() as block:

            @block.sync
            def _(sp):
                sp.sem_inc(x4_stored, 16)
                sp.dma_start(x_in[:, :, :], x_d[0]).then_inc(x_loaded, 16)
                sp.dma_start(row_b2[:, :], d["rows"][ROWS.index("b2")].partition_broadcast(P)).then_inc(row_loaded, 16)
                for n in WEIGHTS_C:
                    rows = d[n].shape[0]
                    sp.dma_start(w[n][0:rows], d[n]).then_inc(dsem["c"], 16)
                with sp.Fori(0, B - 1) as it:
                    sp.wait_ge(xb_ready, it + 1)
                    sp.dma_start(x_in[:, :, :], x_d[it + 1]).then_inc(x_loaded, 16)
                    sp.wait_ge(x4_ready, it + 1)
                    sp.dma_start(x4_d[it], x4[:, :, :]).then_inc(x4_stored, 16)
                sp.wait_ge(x4_ready, B)
                sp.dma_start(x4_d[B - 1], x4[:, :, :]).then_inc(x4_stored, 16)
                sp.wait_ge(x4_stored, (B + 1) * 16)

            @block.gpsimd
            def _(pool):
                pool.wait_ge(row_loaded, 16)

                def inverse_deviation(k):
                    pool.wait_ge(stats_ready, k)
                    nc.gpsimd.tensor_tensor(rstd[:, :], ve[:, :], w["neghalf"][:, :], ALU.pow).then_inc(rstd_ready, 1)

                def item(it, last):
                    pool.wait_ge(xhat_ready, it + 1)
                    pool.wait_ge(emptied["dve"], units.emptied_last(it, "down1"))
                    nc.gpsimd.tensor_tensor(xb[:, :, :], x_in[:, :, :],
                                            row_b2[:, :].unsqueeze(1).to_broadcast([P, TC, C]),
                                            ALU.add).then_inc(xb_ready, 1)
                    if not last:
                        inverse_deviation(it + 2)

                inverse_deviation(1)
                with pool.Fori(0, B - 1) as it:
                    item(it, False)
                item(B - 1, True)

            @block.scalar
            def _(act):
                act.sem_inc(emptied["act"], units.per["act"])

                def halves(name):
                    return ps[:, units.unit(name), :].rearrange("p (a n) -> p a n", a=2)

                with act.Fori(0, B) as it:
                    for a in range(2):
                        name = f"lnT{a}"
                        act.wait_ge(filled, units.filled(it, name))
                        for c in range(2):
                            op = nc.scalar.activation(lnT[:, 2 * a + c, :], halves(name)[:, c, :], ACT.Identity,
                                                      bias=col(w["cols"], "ln3_b", 2 * a + c),
                                                      scale=col(w["cols"], "ln3_s", 2 * a + c))
                        op.then_inc(emptied["act"], 1)
                    for i in range(NU + 1):
                        if i < NU:
                            name = f"up{i}"
                            act.wait_ge(filled, units.filled(it, name))
                            if i >= 2:
                                act.wait_ge(gelu_ready, it * NU + (i - 1))
                            for c in range(2):
                                bias = col(w["cols"], "b1", 2 * i + c)
                                nc.scalar.activation(h[:, i % 2, c, :], halves(name)[:, c, :], ACT.Identity, bias=bias)
                                op = nc.scalar.activation(hh[:, i % 2, c, :], halves(name)[:, c, :], ACT.Square, bias=bias)
                            op.then_inc(emptied["act"], 1)
                        if i >= 1:
                            act.wait_ge(inner_ready, it * NU + i)
                            s = hh[:, (i - 1) % 2, :, :]
                            nc.scalar.activation(s, s, ACT.Tanh, scale=GELU_A).then_inc(tanh_ready, 1)

            @block.vector
            def _(dve):
                dve.sem_inc(emptied["dve"], units.per["dve"])

                def normalise(k):
                    dve.wait_ge(x_loaded, 16 * k)
                    layernorm_stats(nc, x_in, stats, mv, ve).then_inc(stats_ready, 1)
                    dve.wait_ge(rstd_ready, k)
                    layernorm_apply(nc, x_in, mv, rstd, xhat).then_inc(xhat_ready, 1)

                def gelu(it):
                    for i in range(NU + 1):
                        if i < NU:
                            dve.wait_ge(emptied["act"], units.emptied(it, f"up{i}"))
                            s = hh[:, i % 2, :, :]
                            nc.vector.tensor_scalar(s, s, GELU_B, 1.0, ALU.mult, ALU.add)
                            nc.vector.drain()
                            nc.vector.tensor_tensor(s, s, h[:, i % 2, :, :], ALU.mult).then_inc(inner_ready, 1)
                        if i >= 1:
                            j = i - 1
                            dve.wait_ge(tanh_ready, it * NU + i)
                            nc.vector.scalar_tensor_tensor(act2[:, 2 * j:2 * j + 2, :], hh[:, j % 2, :, :], 1.0,
                                                           h[:, j % 2, :, :], ALU.add, ALU.mult).then_inc(gelu_ready, 1)

                def item(it, last):
                    gelu(it)
                    if not last:
                        normalise(it + 2)
                    dve.wait_ge(xb_ready, it + 1)
                    dve.wait_ge(x4_stored, 16 * it + 16)
                    for tc in range(TC):
                        name = f"down{tc}"
                        dve.wait_ge(filled, units.filled(it, name))
                        nc.vector.scalar_tensor_tensor(x4[:, tc, :], ps[:, units.unit(name), :], 0.5, xb[:, tc, :],
                                                       ALU.mult, ALU.add).then_inc(emptied["dve"], 1)
                    nc.vector.drain()
                    dve.sem_inc(x4_ready, 1)

                normalise(1)
                with dve.Fori(0, B - 1) as it:
                    item(it, False)
                item(B - 1, True)

            @block.tensor
            def _(pe):
                def unit(it, name):
                    reader, value = units.before(it, name)
                    pe.wait_ge(emptied[reader], value)
                    return ps[:, units.unit(name), :]

                with pe.Fori(0, B) as it:
                    pe.wait_ge(xhat_ready, it + 1)
                    for a in range(2):
                        u = unit(it, f"lnT{a}").rearrange("p (a n) -> p a n", a=2)
                        for c in range(2):
                            for tc in range(TC):
                                op = nc.tensor.transpose(u[:, c, tc * P:(tc + 1) * P],
                                                         xhat[:, tc, (2 * a + c) * P:(2 * a + c + 1) * P],
                                                         w["ident"][:, :])
                        op.then_inc(filled, 1)
                    pe.wait_ge(dsem["w1"], 16)
                    pe.wait_ge(emptied["act"], units.emptied(it, "lnT1"))
                    for i in range(NU):
                        u = unit(it, f"up{i}").rearrange("p (a n) -> p a n", a=2)
                        for a in range(2):
                            at = (2 * i + a) * P
                            for c in range(KC):
                                op = nc.tensor.matmul(u[:, a, :], w["w1"][:, c, at:at + P], lnT[:, c, :],
                                                      start=(c == 0), stop=(c == KC - 1))
                        op.then_inc(filled, 1)
                    pe.wait_ge(dsem["w2"], 16)
                    for tc in range(TC):
                        u = unit(it, f"down{tc}")
                        for m in range(FC):
                            if tc == 0 and m % 2 == 0:
                                pe.wait_ge(gelu_ready, it * NU + (m // 2 + 1))
                            op = nc.tensor.matmul(u, act2[:, m, tc * P:(tc + 1) * P], w["w2"][:, m, :],
                                                  start=(m == 0), stop=(m == FC - 1))
                        op.then_inc(filled, 1)


def phase_c(nc, d, out, w, dsem):
    with ExitStack() as ctx:
        def sb(name, *shape):
            return ctx.enter_context(nc.sbuf_tensor("c_" + name, list(shape), F32))

        def sem(name):
            return ctx.enter_context(nc.semaphore("c_" + name))

        MIX = ("w", "k", "v", "r", "g")
        units = Units([("xaT", 0, "act"), ("t", 1, "act"), ("mw", 2, "dve"), ("mk", 0, "dve"), ("mv", 1, "dve"),
                       ("mr", 2, "dve"), ("mg", 0, "dve"), ("dec1", 1, "act"), ("dec2", 2, "act"), ("k", 0, "act"),
                       ("v", 1, "act"), ("r", 2, "act"), ("g", 0, "dve"), ("bonus", 1, "dve")] +
                      [(f"vb{j}", (j + 2) % 3, "dve") for j in range(RS)] +
                      [("wkv", 3, "dve"), ("y", 0, "dve"), ("zT", 1, "act"), ("o", 2, "dve"), ("xcT", 0, "act"),
                       ("kk", 1, "act"), ("rr", 2, "act"), ("kv", 0, "dve")])
        AHEAD = 2

        x_in = sb("x_in", P, TC, C)
        xhat = sb("xhat", P, TC, C)
        state_in = sb("state_in", P, 2, KC)
        s0_in = sb("s0_in", P, KC, RS)
        xaT = sb("xaT", P, KC, T + 1)
        sx = sb("sx", P, KC, T)
        xxx = sb("xxx", P, KC, T)
        tT = sb("tT", P, 2, T)
        xj = {n: sb("x" + n, P, KC, T) for n in MIX}
        decT = sb("decT", DD, T)
        wT = sb("wT", P, KC, T)
        kT, vT, rT = sb("kT", P, KC, T), sb("vT", P, KC, T), sb("rT", P, KC, T)
        g2 = sb("g2", P, TC, C)
        th = sb("th", P, TC, C)
        bonusT = sb("bonusT", P, KC, T)
        a = sb("a", P, 2, KC, T)
        S = sb("S", P, 2, KC, T)
        z = sb("z", P, 2, KC, T)
        x5 = sb("x5", P, TC, C)
        x6 = sb("x6", P, TC, C)
        stats = sb("stats", P, TC, 6)
        mv = sb("mv", P, TC, 2)
        ve = sb("ve", P, TC)
        rstd = sb("rstd", P, TC)
        NG = TC * RH
        gmean, gvar, grstd, gtmp = sb("gmean", P, NG), sb("gvar", P, NG), sb("grstd", P, NG), sb("gtmp", P, NG)
        row_w, row_b = sb("row_gn_w", P, C), sb("row_gn_b", P, C)
        late = {n: sb(n, P, KC, C) for n in ("Wo", "fWk", "fWr", "fWv")}
        w = {**w, **late}
        yT, zT, kkT, xk2, xr2 = xj["k"], xj["g"], xj["w"], xj["k"], xj["v"]
        yc, zn, sq = [x[:, :, :].rearrange("p (t a) n -> p t (a n)", t=TC) for x in (xj["v"], xj["r"], xxx)]
        rrt = th

        ps = ctx.enter_context(nc.psum_tensor("c_ps", [P, 4, 1024], F32))

        rows_loaded, x_loaded, state_loaded = sem("rows_loaded"), sem("x_loaded"), sem("state_loaded")
        x6_stored, x_released, state_released = sem("x6_stored"), sem("x_released"), sem("state_released")
        filled = sem("filled")
        emptied = {"act": sem("emptied_act"), "dve": sem("emptied_dve")}
        stats_ready, rstd_ready, xhat_ready = sem("stats_ready"), sem("rstd_ready"), sem("xhat_ready")
        shift_ready = sem("shift_ready")
        xj_ready, th_ready, ruk_ready = sem("xj_ready"), sem("th_ready"), sem("ruk_ready")
        a0_ready, scanned, z_ready, summed = sem("a0_ready"), sem("scanned"), sem("z_ready"), sem("summed")
        yT_ready, yc_ready, sq_ready, gve_ready, gdev_ready, zn_ready = (
            sem("yT_ready"), sem("yc_ready"), sem("sq_ready"), sem("gve_ready"), sem("gdev_ready"), sem("zn_ready"))
        late_loaded = sem("late_loaded")
        kk_ready, x6_ready = sem("kk_ready"), sem("x6_ready")

        x_d = d["x4"].rearrange("b (c p) n -> b p c n", p=P)
        out_d = out.rearrange("b (c p) n -> b p c n", p=P)

        def cols(name, c):
            return col(w["cols"], name, c)

        with nc.Block() as block:

            @block.sync
            def _(sp):
                sp.sem_inc(x6_stored, 16)
                for n, row in zip(("gn_w", "gn_b"), (row_w, row_b)):
                    sp.dma_start(row[:, :], d["rows"][ROWS.index(n)].partition_broadcast(P)).then_inc(rows_loaded, 16)

                def load(it):
                    sp.dma_start(x_in[:, :, :], x_d[it]).then_inc(x_loaded, 16)
                    sp.dma_start(state_in[:, :, :], d["state_cols"][it]).then_inc(state_loaded, 16)
                    sp.dma_start(s0_in[:, :, :], d["s0"][it]).then_inc(state_loaded, 16)

                load(0)
                for n in late:
                    sp.dma_start(w[n][:, :, :], d[n].rearrange("(c p) n -> p c n", p=P)).then_inc(late_loaded, 16)
                with sp.Fori(0, B - 1) as it:
                    sp.wait_ge(x_released, it + 1)
                    sp.wait_ge(state_released, it + 1)
                    load(it + 1)
                    sp.wait_ge(x6_ready, it + 1)
                    sp.dma_start(out_d[it], x6[:, :, :]).then_inc(x6_stored, 16)
                sp.wait_ge(x6_ready, B)
                sp.dma_start(out_d[B - 1], x6[:, :, :]).then_inc(x6_stored, 16)
                sp.wait_ge(x6_stored, (B + 1) * 16)

            @block.gpsimd
            def _(pool):
                with pool.Fori(0, B) as it:
                    def inverse_deviation(k):
                        pool.wait_ge(stats_ready, 2 * it + k)
                        nc.gpsimd.tensor_tensor(rstd[:, :], ve[:, :], w["neghalf"][:, :], ALU.pow).then_inc(rstd_ready, 1)

                    inverse_deviation(1)
                    for j, n in enumerate(MIX):
                        pool.wait_ge(emptied["dve"], units.emptied(it, "m" + n))
                        nc.gpsimd.tensor_tensor(xj[n][:, :, :], xj[n][:, :, :], xaT[:, :, 1:T + 1],
                                                ALU.add).then_inc(xj_ready, 1)
                    pool.wait_ge(emptied["act"], units.emptied(it, "r"))
                    for j in range(RS):
                        pool.wait_ge(scanned, it * RS + (j + 1))
                        if j >= 2:
                            pool.wait_ge(summed, it * RS + (j - 1))
                        nc.gpsimd.tensor_tensor(z[:, j % 2, :, :], S[:, j % 2, :, :], rT[:, :, :],
                                                ALU.mult).then_inc(z_ready, 1)
                    inverse_deviation(2)

            @block.scalar
            def _(act):
                act.sem_inc(emptied["act"], units.per["act"])

                def chunks(name):
                    return ps[:, units.unit(name), :].rearrange("p (c n) -> p c n", c=KC)

                with act.Fori(0, B) as it:
                    def filled_with(name):
                        act.wait_ge(filled, units.filled(it, name))

                    def shifted(name, row, scale, bias):
                        filled_with(name)
                        nc.scalar.copy(xaT[:, :, 0], state_in[:, row, :])
                        for c in range(KC):
                            op = nc.scalar.activation(xaT[:, c, 1:T + 1], chunks(name)[:, c, :], ACT.Identity,
                                                      bias=cols(bias, c), scale=cols(scale, c))
                        op.then_inc(emptied["act"], 1)

                    act.wait_ge(state_loaded, 32 * it + 32)
                    shifted("xaT", 1, "rln1_w", "rln1_b")
                    filled_with("t")
                    nc.scalar.activation(tT[:, 0, :], chunks("t")[:, 0, :], ACT.Tanh)
                    nc.scalar.activation(tT[0:DM, 1, :], chunks("t")[0:DM, 1, :], ACT.Tanh).then_inc(emptied["act"], 1)
                    filled_with("dec1")
                    nc.scalar.activation(decT[:, :], chunks("dec1")[0:DD, 0, :], ACT.Tanh).then_inc(emptied["act"], 1)
                    filled_with("dec2")
                    for c in range(KC):
                        nc.scalar.activation(wT[:, c, 1:T], chunks("dec2")[:, c, 0:T - 1], ACT.Exp, bias=cols("time_decay", c))
                    nc.scalar.drain()
                    nc.scalar.activation(wT[:, :, 1:T], wT[:, :, 1:T], ACT.Exp, scale=-1.0).then_inc(emptied["act"], 1)
                    for n, dst in (("k", kT), ("v", vT), ("r", rT)):
                        filled_with(n)
                        nc.scalar.copy(dst[:, :, :], chunks(n)).then_inc(emptied["act"], 1)
                    filled_with("g")
                    nc.scalar.activation(th[:, :, :], ps[:, units.unit("g"), :].rearrange("p (t n) -> p t n", t=TC),
                                         ACT.Tanh, scale=0.5).then_inc(th_ready, 1)
                    for j in range(RS):
                        if j >= 2:
                            act.wait_ge(scanned, it * RS + (j - 1))
                        nc.scalar.copy(a[:, j % 2, :, 0], s0_in[:, :, j]).then_inc(a0_ready, 1)
                    act.wait_ge(yc_ready, it + 1)
                    nc.scalar.activation(sq, yc, ACT.Square).then_inc(sq_ready, 1)
                    act.wait_ge(gve_ready, it + 1)
                    nc.scalar.activation(grstd[:, :], gvar[:, :], ACT.Sqrt).then_inc(gdev_ready, 1)
                    filled_with("zT")
                    nc.scalar.copy(zT[:, :, :], chunks("zT")).then_inc(emptied["act"], 1)
                    shifted("xcT", 0, "rln2_w", "rln2_b")
                    nc.scalar.drain()
                    act.sem_inc(state_released, 1)
                    filled_with("kk")
                    nc.scalar.activation(kkT[:, :, :], chunks("kk"), ACT.Relu).then_inc(emptied["act"], 1)
                    filled_with("rr")
                    nc.scalar.activation(rrt[:, :, :], ps[:, units.unit("rr"), :].rearrange("p (t n) -> p t n", t=TC),
                                         ACT.Tanh, scale=0.5).then_inc(emptied["act"], 1)

            @block.vector
            def _(dve):
                dve.sem_inc(emptied["dve"], units.per["dve"])
                nc.vector.memset(wT[:, :, 0:1], 0.0)
                dve.wait_ge(rows_loaded, 32)

                def chunks(name):
                    return ps[:, units.unit(name), :].rearrange("p (c n) -> p c n", c=KC)

                def tokens(name):
                    return ps[:, units.unit(name), :].rearrange("p (t n) -> p t n", t=TC)

                def groups(x):
                    return x.rearrange("p t (h s) -> p (t h) s", s=RS)

                def over_group(x):
                    return x[:, :].unsqueeze(2).to_broadcast([P, NG, RS])

                with dve.Fori(0, B) as it:
                    def filled_with(name):
                        dve.wait_ge(filled, units.filled(it, name))

                    def normalise(x, k):
                        layernorm_stats(nc, x, stats, mv, ve).then_inc(stats_ready, 1)
                        dve.wait_ge(rstd_ready, 2 * it + k)
                        layernorm_apply(nc, x, mv, rstd, xhat).then_inc(xhat_ready, 1)

                    def shift(name, mixes):
                        dve.wait_ge(emptied["act"], units.emptied(it, name))
                        nc.vector.tensor_tensor(sx[:, :, :], xaT[:, :, 0:T], xaT[:, :, 1:T + 1], ALU.subtract)
                        nc.vector.drain()
                        for dst, mix in mixes:
                            for c in range(KC):
                                op = nc.vector.scalar_tensor_tensor(dst[:, c, :], sx[:, c, :], cols(mix, c),
                                                                    xaT[:, c, 1:T + 1], ALU.mult, ALU.add)
                            op.then_inc(shift_ready, 1)

                    dve.wait_ge(x_loaded, 16 * it + 16)
                    normalise(x_in, 1)
                    shift("xaT", [(xxx, "maa_x")])
                    for n in MIX:
                        filled_with("m" + n)
                        for c in range(KC):
                            op = nc.vector.scalar_tensor_tensor(xj[n][:, c, :], chunks("m" + n)[:, c, :],
                                                                cols("maa_" + n, c), sx[:, c, :], ALU.add, ALU.mult)
                        op.then_inc(emptied["dve"], 1)
                    dve.wait_ge(emptied["act"], units.emptied(it, "r"))
                    for c in range(KC):
                        op = nc.vector.scalar_tensor_tensor(bonusT[:, c, :], rT[:, c, :], cols("faaaa", c), kT[:, c, :],
                                                            ALU.mult, ALU.mult)
                    op.then_inc(ruk_ready, 1)
                    dve.wait_ge(th_ready, it + 1)
                    nc.vector.scalar_tensor_tensor(g2[:, :, :], th[:, :, :], 1.0, tokens("g"), ALU.add,
                                                   ALU.mult).then_inc(emptied["dve"], 1)
                    filled_with("bonus")
                    nc.vector.tensor_tensor(bonusT[:, :, :], chunks("bonus"), vT[:, :, :],
                                            ALU.mult).then_inc(emptied["dve"], 1)
                    for j in range(RS):
                        filled_with(f"vb{j}")
                        nc.vector.tensor_tensor(a[:, j % 2, :, 1:T], kT[:, :, 0:T - 1],
                                                chunks(f"vb{j}")[:, :, 0:T - 1],
                                                ALU.mult).then_inc(emptied["dve"], 1)
                        dve.wait_ge(emptied["dve"], units.emptied(it, f"vb{j}"))
                        dve.wait_ge(a0_ready, it * RS + (j + 1))
                        if j >= 2:
                            dve.wait_ge(z_ready, it * RS + (j - 1))
                        nc.vector.tensor_tensor_scan(S[:, j % 2, :, :].rearrange("p c n -> p (c n)"),
                                                     wT[:, :, :].rearrange("p c n -> p (c n)"),
                                                     a[:, j % 2, :, :].rearrange("p c n -> p (c n)"),
                                                     0.0, ALU.mult, ALU.add).then_inc(scanned, 1)
                    filled_with("wkv")
                    nc.vector.tensor_tensor(yT[:, :, :], chunks("wkv"), bonusT[:, :, :],
                                            ALU.add).then_inc(emptied["dve"], 1)
                    filled_with("y")
                    nc.vector.reduce_sum(gmean[:, :], groups(tokens("y")), axis=AX)
                    nc.vector.drain()
                    nc.vector.tensor_scalar(gmean[:, :], gmean[:, :], 1.0 / RS, None, ALU.mult)
                    nc.vector.drain()
                    nc.vector.tensor_tensor(groups(yc), groups(tokens("y")), over_group(gmean), ALU.subtract)
                    nc.vector.drain()
                    dve.sem_inc(emptied["dve"], 1)
                    dve.sem_inc(yc_ready, 1)
                    dve.wait_ge(sq_ready, it + 1)
                    nc.vector.reduce_sum(gvar[:, :], groups(sq), axis=AX)
                    nc.vector.drain()
                    nc.vector.tensor_scalar(gvar[:, :], gvar[:, :], 1.0 / RS, EPS, ALU.mult, ALU.add).then_inc(gve_ready, 1)
                    dve.wait_ge(gdev_ready, it + 1)
                    nc.vector.reciprocal(grstd[:, :], grstd[:, :])
                    nc.vector.drain()
                    nc.vector.tensor_tensor(gtmp[:, :], grstd[:, :], grstd[:, :], ALU.mult)
                    nc.vector.drain()
                    nc.vector.tensor_tensor(gtmp[:, :], gtmp[:, :], gvar[:, :], ALU.mult)
                    nc.vector.drain()
                    nc.vector.tensor_scalar(gtmp[:, :], gtmp[:, :], -0.5, 1.5, ALU.mult, ALU.add)
                    nc.vector.drain()
                    nc.vector.tensor_tensor(grstd[:, :], grstd[:, :], gtmp[:, :], ALU.mult)
                    nc.vector.drain()
                    nc.vector.tensor_tensor(groups(zn), groups(yc), over_group(grstd), ALU.mult)
                    nc.vector.drain()
                    nc.vector.tensor_tensor(zn, zn, row_w[:, :].unsqueeze(1).to_broadcast([P, TC, C]), ALU.mult)
                    nc.vector.drain()
                    nc.vector.tensor_tensor(zn, zn, row_b[:, :].unsqueeze(1).to_broadcast([P, TC, C]), ALU.add)
                    nc.vector.drain()
                    nc.vector.tensor_tensor(zn, zn, g2[:, :, :], ALU.mult).then_inc(zn_ready, 1)
                    filled_with("o")
                    nc.vector.scalar_tensor_tensor(x5[:, :, :], tokens("o"), 0.5, x_in[:, :, :], ALU.mult,
                                                   ALU.add).then_inc(emptied["dve"], 1)
                    nc.vector.drain()
                    dve.sem_inc(x_released, 1)
                    normalise(x5, 2)
                    shift("xcT", [(xk2, "fmaa_k"), (xr2, "fmaa_r")])
                    dve.wait_ge(emptied["act"], units.emptied(it, "kk"))
                    nc.vector.tensor_tensor(kkT[:, :, :], kkT[:, :, :], kkT[:, :, :], ALU.mult).then_inc(kk_ready, 1)
                    filled_with("kv")
                    dve.wait_ge(emptied["act"], units.emptied(it, "rr"))
                    dve.wait_ge(x6_stored, 16 * it + 16)
                    nc.vector.scalar_tensor_tensor(x6[:, :, :], rrt[:, :, :], 1.0, tokens("kv"), ALU.add,
                                                   ALU.mult).then_inc(emptied["dve"], 1)
                    nc.vector.drain()
                    nc.vector.scalar_tensor_tensor(x6[:, :, :], x6[:, :, :], 0.5, x5[:, :, :], ALU.mult,
                                                   ALU.add).then_inc(x6_ready, 1)

            @block.tensor
            def _(pe):
                pe.wait_ge(dsem["c"], 16 * len(WEIGHTS_C))
                pe.wait_ge(late_loaded, 16 * 4)

                with pe.Fori(0, B) as it:
                    def unit(name):
                        reader, value = units.before(it, name)
                        pe.wait_ge(emptied[reader], value)
                        return ps[:, units.unit(name), :]

                    def chunks(name):
                        return unit(name).rearrange("p (c n) -> p c n", c=KC)

                    def tokens(name):
                        return unit(name).rearrange("p (t n) -> p t n", t=TC)

                    def to_channel_layout(name, src):
                        u = chunks(name)
                        for c in range(KC):
                            for tc in range(TC):
                                op = nc.tensor.transpose(u[:, c, tc * P:(tc + 1) * P], src[:, tc, c * P:(c + 1) * P],
                                                         w["ident"][:, :])
                        op.then_inc(filled, 1)

                    def channels(name, weights, src):
                        u = chunks(name)
                        for m in range(KC):
                            for c in range(KC):
                                op = nc.tensor.matmul(u[:, m, :], weights[:, c, m * P:(m + 1) * P], src[:, c, :],
                                                      start=(c == 0), stop=(c == KC - 1))
                        op.then_inc(filled, 1)

                    def to_tokens(name, src, weights):
                        u = tokens(name)
                        for tc in range(TC):
                            for c in range(KC):
                                op = nc.tensor.matmul(u[:, tc, :], src[:, c, tc * P:(tc + 1) * P], weights[:, c, :],
                                                      start=(c == 0), stop=(c == KC - 1))
                        op.then_inc(filled, 1)

                    def shift_done(k):
                        pe.wait_ge(shift_ready, it * 3 + k)

                    def halves(x):
                        return [x[:, 2 * i:2 * i + 2, :].rearrange("p c n -> p (c n)") for i in range(2)]

                    pe.wait_ge(xhat_ready, 2 * it + 1)
                    to_channel_layout("xaT", xhat)
                    shift_done(1)
                    u = chunks("t")
                    for n0, n in ((0, P), (P, DM)):
                        for c in range(KC):
                            op = nc.tensor.matmul(u[0:n, n0 // P, :], w["maa_w1"][:, c, n0:n0 + n], xxx[:, c, :],
                                                  start=(c == 0), stop=(c == KC - 1))
                    op.then_inc(filled, 1)
                    pe.wait_ge(emptied["act"], units.emptied(it, "t"))
                    for j, n in enumerate(MIX):
                        u = chunks("m" + n)
                        at, half = DM * j % P, DM * j // P
                        for c in range(KC):
                            op = nc.tensor.matmul(u[:, c, :], w["maa_w2"][at:at + DM, half, c * P:(c + 1) * P],
                                                  tT[at:at + DM, half, :], start=True, stop=True)
                        op.then_inc(filled, 1)
                    pe.wait_ge(xj_ready, it * NMIX + 1)
                    u = chunks("dec1")
                    for c in range(KC):
                        op = nc.tensor.matmul(u[0:DD, 0, :], w["decay_w1"][:, c, :], xj["w"][:, c, :],
                                              start=(c == 0), stop=(c == KC - 1))
                    op.then_inc(filled, 1)
                    pe.wait_ge(emptied["act"], units.emptied(it, "dec1"))
                    u = chunks("dec2")
                    for c in range(KC):
                        op = nc.tensor.matmul(u[:, c, :], w["decay_w2"][0:DD, c * P:(c + 1) * P], decT[:, :],
                                              start=True, stop=True)
                    op.then_inc(filled, 1)
                    for i, n in enumerate(("k", "v", "r")):
                        pe.wait_ge(xj_ready, it * NMIX + (2 + i))
                        channels(n, w["W" + n], xj[n])
                    pe.wait_ge(xj_ready, it * NMIX + 5)
                    to_tokens("g", xj["g"], w["Wg"])
                    pe.wait_ge(ruk_ready, it + 1)
                    u = unit("bonus")
                    for i in range(2):
                        op = nc.tensor.matmul(u[:, i * 512:(i + 1) * 512], w["same_head"][:, :], halves(bonusT)[i],
                                              start=True, stop=True)
                    op.then_inc(filled, 1)
                    acc = unit("wkv")
                    for n in range(RS + AHEAD):
                        if n < RS:
                            u = unit(f"vb{n}")
                            for i in range(2):
                                op = nc.tensor.matmul(u[:, i * 512:(i + 1) * 512], w["spread"][:, n, :], halves(vT)[i],
                                                      start=True, stop=True)
                            op.then_inc(filled, 1)
                        j = n - AHEAD
                        if j >= 0:
                            pe.wait_ge(z_ready, it * RS + (j + 1))
                            for i in range(2):
                                op = nc.tensor.matmul(acc[:, i * 512:(i + 1) * 512], w["gather"][:, j, :],
                                                      halves(z[:, j % 2, :, :])[i], start=(j == 0), stop=(j == RS - 1))
                            op.then_inc(summed, 1)
                    pe.wait_ge(summed, it * RS + RS)
                    pe.sem_inc(filled, 1)
                    pe.wait_ge(emptied["dve"], units.emptied(it, "wkv"))
                    u = tokens("y")
                    for tc in range(TC):
                        for c in range(KC):
                            op = nc.tensor.transpose(u[:, tc, c * P:(c + 1) * P], yT[:, c, tc * P:(tc + 1) * P],
                                                     w["ident"][:, :])
                    op.then_inc(filled, 1)
                    pe.wait_ge(zn_ready, it + 1)
                    to_channel_layout("zT", zn)
                    pe.wait_ge(emptied["act"], units.emptied(it, "zT"))
                    to_tokens("o", zT, w["Wo"])
                    pe.wait_ge(xhat_ready, 2 * it + 2)
                    to_channel_layout("xcT", xhat)
                    shift_done(2)
                    channels("kk", w["fWk"], xk2)
                    shift_done(3)
                    to_tokens("rr", xr2, w["fWr"])
                    pe.wait_ge(kk_ready, it + 1)
                    to_tokens("kv", kkT, w["fWv"])


def carve(arena, names):
    out, at = {}, 0
    for name, shape in names:
        n = int(np.prod(shape))
        v = arena[:, at:at + n]
        if len(shape) == 2:
            v = v.rearrange("p (a n) -> p a n", n=shape[1])
        out[name] = v
        at += n
    return out


WEIGHTS_A = [("qkv", (KC, 3 * C)), ("kv", (KC, 2 * C)), ("ao", (KC, C)), ("q", (KC, C)), ("co", (KC, C))]
WEIGHTS_C = {"Wk": (KC, C), "Wv": (KC, C), "Wr": (KC, C), "Wg": (KC, C), "maa_w1": (KC, NMIX * DM),
             "maa_w2": (2, C), "decay_w1": (KC, DD), "decay_w2": (C,), "same_head": (P,), "spread": (RS, P),
             "gather": (RS, P)}


def build_program(nc, d, out):
    with ExitStack() as ctx:
        def sb(name, *shape):
            return ctx.enter_context(nc.sbuf_tensor("w_" + name, list(shape), F32))

        arena = sb("arena", P, 8 * C * C // P)
        w = {"ident": sb("ident", P, P), "cols": sb("cols", P, NCOL), "neghalf": sb("neghalf", P, TC)}
        dsem = {n: ctx.enter_context(nc.semaphore("loaded_" + n))
                for n in ("ident", "cols", "kv", "qkv", "ao", "q", "co", "w1", "w2", "c")}
        d["x3"] = nc.dram_tensor("x3", (B, T, C), F32, kind="Internal").ap()
        d["x4"] = nc.dram_tensor("x4", (B, T, C), F32, kind="Internal").ap()
        weights_c = carve(arena, WEIGHTS_C.items())
        with nc.sbuf_tensor("w_w1", [P, KC, FF], F32) as w1, nc.sbuf_tensor("w_w2", [P, FC, C], F32) as w2:
            phase_a(nc, d, {**w, **carve(arena, WEIGHTS_A), "w1": w1, "w2": w2}, dsem)
            phase_b(nc, d, {**w, **weights_c, "w1": w1, "w2": w2}, dsem)
        phase_c(nc, d, out, {**w, **weights_c}, dsem)


def kernel(**inputs):
    import concourse.bacc as bacc
    from concourse.bass_utils import run_bass_kernel_spmd

    g = {k: np.asarray(v) for k, v in inputs.items()}
    L0 = {k[9:]: v for k, v in g.items() if k.startswith("L0_xattn_")}
    L1 = {k[9:]: v for k, v in g.items() if k.startswith("L1_xattn_")}
    vectors = {
        "ln1_s": L0["ln1_s"], "ln1_b": L0["ln1_b"], "b_q": L0["b_qkv"][:C], "b_k": L0["b_qkv"][C:2 * C], "b_v": L0["b_qkv"][2 * C:],
        "ln2_s": L0["ln2_s"], "ln2_b": L0["ln2_b"], "b_qx": L0["b_q"], "b_kx": L0["b_kv"][:C], "b_vx": L0["b_kv"][C:],
        "ln3_s": L0["ln3_s"], "ln3_b": L0["ln3_b"], "b1": L0["b1"], "rln1_w": L1["ln1_w"], "rln1_b": L1["ln1_b"],
        "rln2_w": L1["ln2_w"], "rln2_b": L1["ln2_b"], "maa_x": L1["maa_x"], "maa_w": L1["maa_w"],
        "maa_k": L1["maa_k"], "maa_v": L1["maa_v"], "maa_r": L1["maa_r"], "maa_g": L1["maa_g"],
        "time_decay": L1["time_decay"], "faaaa": L1["faaaa"].reshape(C), "fmaa_k": L1["fmaa_k"],
        "fmaa_r": L1["fmaa_r"]}
    spread = {"b_ao": L0["b_ao"], "b_co": L0["b_co"], "b2": L0["b2"], "gn_w": L1["gn_w"], "gn_b": L1["gn_b"]}
    state = g["ctx_2048"]

    def chunked(m):
        return m.reshape(KC, P, -1).transpose(1, 0, 2)

    mix2 = [L1["maa_w2"][:4].reshape(P, C), np.zeros((P, C), np.float32)]
    mix2[1][:DM] = L1["maa_w2"][4]
    mix2 = np.stack(mix2, axis=1)
    head, chan, j = np.arange(P) // RS, np.arange(P) % RS, np.arange(RS)
    same = (head[:, None] == head[None, :]).astype(np.float32)
    arrays = {
        "x": g["x"], "ctx_2048": state, "mask_self": g["mask_1x1xSxS2_fc1"], "mask_cross": g["mask_Bx1xSxS2_ff1"],
        "cols": np.concatenate([vectors[n].reshape(k, P).T for n, k in COLUMNS], axis=1),
        "rows": np.stack([spread[n] for n in ROWS]).reshape(len(ROWS), 1, C)[:, 0],
        "ident": np.eye(P, dtype=np.float32),
        "w_qkv": L0["w_qkv"], "w_ao": L0["w_ao"], "w_q": L0["w_q"], "w_kv": L0["w_kv"], "w_co": L0["w_co"],
        "w1": L0["w1"], "w2": L0["w2"],
        "state_cols": state[:, :2].reshape(B, 2, KC, P).transpose(0, 3, 1, 2),
        "s0": state[:, 2:2 + RS].reshape(B, KC, P, RS).transpose(0, 2, 1, 3),
        "Wo": L1["Wo"].T, "fWk": L1["fWk"].T, "fWr": L1["fWr"].T, "fWv": L1["fWv"].T,
        "maa_w1": chunked(L1["maa_w1"]), "maa_w2": mix2,
        "decay_w1": chunked(L1["decay_w1"]), "decay_w2": L1["decay_w2"],
        "same_head": same,
        "spread": same[:, None, :] * (chan[:, None, None] == j[None, :, None]),
        "gather": same[:, None, :] * (chan[None, None, :] == j[None, :, None]),
    }
    for n in ("Wk", "Wv", "Wr", "Wg"):
        arrays[n] = chunked(L1[n].T)
    nc = bacc.Bacc("TRN2", target_bir_lowering=False, num_devices=1)
    feed, d = {}, {}
    for name, a in arrays.items():
        a = np.ascontiguousarray(a)
        feed["in_" + name] = a
        d[name] = nc.dram_tensor("in_" + name, a.shape, mybir.dt.from_np(a.dtype), kind="ExternalInput").ap()
    out = nc.dram_tensor("out_0", (B, T, C), F32, kind="ExternalOutput").ap()
    build_program(nc, d, out)
    r = run_bass_kernel_spmd(nc, [feed], core_ids=[0])
    return r.results[0]["out_0"]
```

```python
from contextlib import ExitStack

import concourse.bass as bass
import numpy as np
from concourse import mybir

F32 = mybir.dt.float32
F32R = mybir.dt.float32r
ALU = mybir.AluOpType
ACT = mybir.ActivationFunctionType
AX = mybir.AxisListType.X

P = 128
B, T, C = 16, 256, 512
KC = C // P
TC = T // P
NH, HD = 16, 32
HPC = P // HD
FF = 4 * C
FC = FF // P
RH, RS = 32, 16
DM, NMIX = 32, 5
DD = 64
EPS = 1e-5
SCALE = float(HD) ** -0.5
GELU_A, GELU_B = 0.7978845608028654, 0.044715

COLUMNS = [("ln1_s", KC), ("ln1_b", KC), ("b_q", KC), ("b_k", KC), ("b_v", KC), ("ln2_s", KC), ("ln2_b", KC), ("b_qx", KC),
           ("b_kx", KC), ("b_vx", KC), ("ln3_s", KC), ("ln3_b", KC), ("b1", FC), ("rln1_w", KC), ("rln1_b", KC),
           ("rln2_w", KC), ("rln2_b", KC), ("maa_x", KC), ("maa_w", KC), ("maa_k", KC), ("maa_v", KC),
           ("maa_r", KC), ("maa_g", KC), ("time_decay", KC), ("faaaa", KC), ("gn_w", KC),
           ("gn_b", KC), ("fmaa_k", KC), ("fmaa_r", KC)]
COL_AT, NCOL = {}, 0
for _name, _n in COLUMNS:
    COL_AT[_name] = NCOL
    NCOL += _n
ROWS = ["b_ao", "b_co", "b2"]


class Units:

    def __init__(self, uses):
        self.uses = uses
        self.at = {name: i for i, (name, _, _) in enumerate(uses)}
        self.per = {}
        self.order = {}
        for name, _, reader in uses:
            self.per[reader] = self.per.get(reader, 0) + 1
            self.order[name] = self.per[reader]

    def filled(self, it, name):
        return it * len(self.uses) + (self.at[name] + 1)

    def emptied(self, it, name):
        per = self.per[self.reader(name)]
        return it * per + (per + self.order[name])

    def emptied_last(self, it, name):
        return it * self.per[self.reader(name)] + self.order[name]

    def reader(self, name):
        return self.uses[self.at[name]][2]

    def unit(self, name):
        return self.uses[self.at[name]][1]

    def before(self, it, name):
        here = self.at[name]
        same = [u for u in self.uses if u[1] == self.unit(name)]
        k = same.index(self.uses[here])
        last = same[k - 1]
        per = self.per[last[2]]
        return last[2], it * per + (self.order[last[0]] + (per if k else 0))


def col(cols, name, c):
    return cols[:, COL_AT[name] + c:COL_AT[name] + c + 1]


def layernorm_stats(nc, x, stats, mv, ve):
    for tc in range(TC):
        nc.vector.bn_stats(stats[:, tc, :], x[:, tc, :])
    nc.vector.drain()
    for tc in range(TC):
        nc.vector.bn_aggr(mv[:, tc, :], stats[:, tc, :])
    nc.vector.drain()
    return nc.vector.tensor_scalar(ve[:, :], mv[:, :, 1], EPS, None, ALU.add)


def layernorm_apply(nc, x, mv, rstd, xhat):
    for tc in range(TC):
        last = nc.vector.tensor_scalar(xhat[:, tc, :], x[:, tc, :], mv[:, tc, 0:1], rstd[:, tc:tc + 1],
                                       ALU.subtract, ALU.mult)
    return last


def load_attention_weights(sp, d, w, dsem, cross):
    def load(name, key):
        sp.dma_start(w[name][:, :, :], d["w_" + name].rearrange("(c p) n -> p c n", p=P)).then_inc(dsem[key], 16)

    if cross:
        load("q", "q_x_")
        load("kv", "kv_x_")
        load("co", "o_x_")
    else:
        sp.dma_start(w["ident"][:, :], d["ident"]).then_inc(dsem["ident"], 16)
        sp.dma_start(w["cols"][:, :], d["cols"]).then_inc(dsem["cols"], 16)
        load("qkv", "q_s_")
        sp.sem_inc(dsem["kv_s_"], 16)
        load("ao", "o_s_")


def attention_phase(nc, d, w, dsem, cross):
    tag = "x_" if cross else "s_"
    ln_s, ln_b, b_q, b_k, b_v = ("ln2_s", "ln2_b", "b_qx", "b_kx", "b_vx") if cross else (
        "ln1_s", "ln1_b", "b_q", "b_k", "b_v")
    LT = 3
    FILLS = {0: ["k2", "ctx2"], 1: ["q3"], 2: ["k3"], 4: ["ctx3"], 5: ["v0"], 6: ["v1"], 7: ["out0"],
             8: ["out1", "ctx0"], 9: ["encT0", "encT1"] if cross else [], 10: ["lnT0", "lnT1"], 11: ["q0"],
             12: ["k0", "ctx1"], 13: ["q1"], 14: ["k1"], 15: ["q2"]}
    PART = {"attn": ("k2", "q3", "k3", "v0", "v1", "ctx0", "ctx1"), "lag": ("ctx2", "ctx3", "out0", "out1"),
            "front": ("encT0", "encT1", "lnT0", "lnT1", "q0", "k0", "q1", "k1", "q2")}
    PART_OF = {name: part for part, names in PART.items() for name in names}
    SHIFT = {"attn": 0, "lag": -1, "front": 1}
    BY_VECTOR = ("v0", "v1", "out0", "out1")
    units = Units([(name, i % 4, "dve" if name in BY_VECTOR else "act")
                   for i, name in enumerate(name for n in range(NH) for name in FILLS.get(n, []))])

    with ExitStack() as ctx:
        def sb(name, *shape):
            return ctx.enter_context(nc.sbuf_tensor(tag + name, list(shape), F32))

        def sem(name):
            return ctx.enter_context(nc.semaphore(tag + name))

        x_in = sb("x_in", P, TC, C)
        xb = sb("xb", P, TC, C)
        x_out = sb("x_out", P, TC, C)
        xhat = sb("xhat", P, TC, C)
        lnT = sb("lnT", P, KC, T)
        enc = sb("enc", P, TC, C) if cross else None
        srcT = sb("encT", P, KC, T) if cross else lnT
        qT = sb("qT", P, KC, T)
        kz = sb("kz", P, NH, T)
        v = sb("v", P, TC, C)
        ctxT = sb("ctxT", P, KC, T)
        mask_in = sb("mask_in", P, TC, T)
        mask = sb("mask", P, TC, T)
        mneg = sb("mneg", P, TC, T)
        t = sb("t", P, 2, TC, T)
        prob = sb("prob", P, 4, TC, T)
        probT = sb("probT", P, 2 * HPC, TC, T)
        tmin = sb("tmin", P, NH, TC)
        psums = sb("psums", P, NH, TC)
        rsums = sb("rsums", P, NH, TC)
        stats = sb("stats", P, TC, 6)
        mv = sb("mv", P, TC, 2)
        ve = sb("ve", P, TC)
        rstd = sb("rstd", P, TC)
        row_out = sb("row_out", P, C)
        ps = ctx.enter_context(nc.psum_tensor(tag + "ps", [P, 4, 512], F32))
        ps_s = ctx.enter_context(nc.psum_tensor(tag + "ps_s", [P, 2, TC, T], F32))
        ps_t = ctx.enter_context(nc.psum_tensor(tag + "ps_t", [P, 2, TC, T], F32))

        row_loaded, x_loaded, xb_loaded = sem("row_loaded"), sem("x_loaded"), sem("xb_loaded")
        enc_loaded, mask_loaded, out_stored = sem("enc_loaded"), sem("mask_loaded"), sem("out_stored")
        mask_released = sem("mask_released")
        filled = sem("filled")
        emptied = {"act": sem("emptied_act"), "dve": sem("emptied_dve")}
        stats_ready, rstd_ready, xhat_ready = sem("stats_ready"), sem("rstd_ready"), sem("xhat_ready")
        xb_ready, out_ready, zeros_ready = sem("xb_ready"), sem("out_ready"), sem("zeros_ready")
        s_filled, s_read, t_ready = sem("s_filled"), sem("s_read"), sem("t_ready")
        exp_done, rsum_ready, prob_ready = sem("exp_done"), sem("rsum_ready"), sem("prob_ready")
        pt_filled, pt_copied, pv_done = sem("pt_filled"), sem("pt_copied"), sem("pv_done")

        x_d = d["x2" if cross else "x"].rearrange("b (c p) n -> b p c n", p=P)
        out_d = d["x3" if cross else "x2"].rearrange("b (c p) n -> b p c n", p=P)
        if cross:
            enc_d = d["ctx_2048"].rearrange("b (c p) n -> b p c n", p=P)
            mask_d = d["mask_cross"].rearrange("b o (c p) n -> b p (o c) n", p=P)
        else:
            self_d = d["mask_self"].rearrange("a o (c p) n -> p (a o c) n", p=P)

        def head(k, h):
            return k * NH + (h + 1)

        def behind(k, n, lag):
            return (k, n - lag) if n >= lag else (k - 1, n - lag + NH)

        def first(k):
            return isinstance(k, int) and k == 0

        def iterations(engine, body):
            body(-1, ("front",))
            body(0, ("attn", "front"))
            with engine.Fori(1, B - 1) as k:
                body(k, ("attn", "lag", "front"))
            body(B - 1, ("attn", "lag"))
            body(B, ("lag",))

        with nc.Block() as block:

            @block.sync
            def _(sp):
                sp.sem_inc(out_stored, 16)
                if cross:
                    sp.dma_start(enc[:, :, :], enc_d[0]).then_inc(enc_loaded, 16)
                    sp.dma_start(mask_in[:, :, :], mask_d[0]).then_inc(mask_loaded, 16)
                sp.dma_start(x_in[:, :, :], x_d[0]).then_inc(x_loaded, 16)
                load_attention_weights(sp, d, w, dsem, cross)
                if not cross:
                    sp.dma_start(mask_in[:, :, :], self_d).then_inc(mask_loaded, 16)
                sp.dma_start(row_out[:, :], d["rows"][ROWS.index("b_co" if cross else "b_ao")].partition_broadcast(P)
                             ).then_inc(row_loaded, 16)

                def load_front(k):
                    sp.wait_ge(xhat_ready, k)
                    sp.dma_start(x_in[:, :, :], x_d[k]).then_inc(x_loaded, 16)
                    if cross:
                        sp.wait_ge(filled, units.filled(k - 1, "encT1"))
                        sp.dma_start(enc[:, :, :], enc_d[k]).then_inc(enc_loaded, 16)

                def load_mask(k):
                    if cross:
                        sp.wait_ge(mask_released, k)
                        sp.dma_start(mask_in[:, :, :], mask_d[k]).then_inc(mask_loaded, 16)

                def load_xb(k):
                    if not first(k):
                        sp.wait_ge(emptied["dve"], units.emptied(k + 1, "out1"))
                    sp.dma_start(xb[:, :, :], x_d[k]).then_inc(xb_loaded, 16)

                def store(k):
                    sp.wait_ge(out_ready, k + 1)
                    sp.dma_start(out_d[k], x_out[:, :, :]).then_inc(out_stored, 16)

                load_front(1)
                load_xb(0)
                load_mask(1)
                with sp.Fori(1, B - 1) as k:
                    load_front(k + 1)
                    load_mask(k + 1)
                    load_xb(k)
                    store(k - 1)
                load_xb(B - 1)
                store(B - 2)
                store(B - 1)
                sp.wait_ge(out_stored, (B + 1) * 16)

            @block.gpsimd
            def _(pool):
                nc.gpsimd.memset(kz[:, :, :], 0.0).then_inc(zeros_ready, 1)
                nc.gpsimd.memset(w["neghalf"][:, :], -0.5)
                nc.gpsimd.drain()
                pool.wait_ge(row_loaded, 16)

                def body(k, parts):
                    for n in range(NH):
                        if n == 1 and "lag" in parts:
                            pool.wait_ge(xb_loaded, 16 * k)
                            nc.gpsimd.tensor_tensor(xb[:, :, :], xb[:, :, :],
                                                    row_out[:, :].unsqueeze(1).to_broadcast([P, TC, C]),
                                                    ALU.add).then_inc(xb_ready, 1)
                        kk, h = behind(k, n, 1)
                        if ("lag" if n < 1 else "attn") in parts:
                            pool.wait_ge(rsum_ready, head(kk, h))
                            nc.gpsimd.tensor_tensor(prob[:, h % 4, :, :], prob[:, h % 4, :, :],
                                                    rsums[:, h, :].unsqueeze(2).to_broadcast([P, TC, T]),
                                                    ALU.mult).then_inc(prob_ready, 1)
                        if n == 8 and "front" in parts:
                            pool.wait_ge(stats_ready, k + 2)
                            nc.gpsimd.tensor_tensor(rstd[:, :], ve[:, :], w["neghalf"][:, :],
                                                    ALU.pow).then_inc(rstd_ready, 1)

                iterations(pool, body)

            @block.scalar
            def _(act):
                act.wait_ge(dsem["cols"], 16)
                act.wait_ge(zeros_ready, 1)
                act.sem_inc(emptied["act"], units.per["act"])

                def move(k, name):
                    act.wait_ge(filled, units.filled(k + 1, name))
                    u = ps[:, units.unit(name), :]
                    two = u.rearrange("p (a n) -> p a n", a=2)
                    i = int(name[-1])
                    if name[:-1] == "encT":
                        op = nc.scalar.copy(srcT[:, 2 * i:2 * i + 2, :], two)
                    elif name[:-1] == "lnT":
                        for a in range(2):
                            op = nc.scalar.activation(lnT[:, 2 * i + a, :], two[:, a, :], ACT.Identity,
                                                      bias=col(w["cols"], ln_b, 2 * i + a),
                                                      scale=col(w["cols"], ln_s, 2 * i + a))
                    elif name[0] == "q":
                        op = nc.scalar.activation(qT[:, i, :], u[:, 0:T], ACT.Identity, bias=col(w["cols"], b_q, i))
                    elif name[0] == "k":
                        for g in range(HPC):
                            rows = slice(HD * g, HD * (g + 1))
                            op = nc.scalar.activation(kz[rows, HPC * i + g, :], u[rows, 0:T], ACT.Identity,
                                                      bias=col(w["cols"], b_k, i)[rows, :])
                    else:
                        op = nc.scalar.activation(ctxT[:, i, :], u[:, 0:T], ACT.Identity,
                                                  bias=col(w["cols"], b_v, i))
                    op.then_inc(emptied["act"], 1)

                def body(k, parts):
                    for n in range(NH):
                        if "attn" in parts:
                            act.wait_ge(t_ready, head(k, n))
                            for tc in range(TC):
                                op = nc.scalar.activation(prob[:, n % 4, tc, :], t[:, n % 2, tc, :], ACT.Exp,
                                                          bias=tmin[:, n, tc:tc + 1], scale=-1.0,
                                                          accum_out=psums[:, n, tc:tc + 1])
                            op.then_inc(exp_done, 1)
                        kk, h = behind(k, n, LT)
                        if ("lag" if n < LT else "attn") in parts:
                            act.wait_ge(pt_filled, head(kk, h))
                            g = h // HPC
                            if not first(kk) or g >= 2:
                                act.wait_ge(pv_done, kk * (NH // HPC) + (g - 1))
                            nc.scalar.copy(probT[:, h % (2 * HPC), :, :], ps_t[:, h % 2, :, :]).then_inc(pt_copied, 1)
                        for name in FILLS.get(n, []):
                            if units.reader(name) == "act":
                                if PART_OF[name] in parts:
                                    move(k, name)
                                else:
                                    nc.scalar.drain()
                                    act.sem_inc(emptied["act"], 1)

                iterations(act, body)

            @block.vector
            def _(dve):
                dve.sem_inc(emptied["dve"], units.per["dve"])

                def take_mask(k):
                    nc.vector.drain()
                    dve.wait_ge(mask_loaded, 16 * k + 16)
                    nc.vector.tensor_copy(mask[:, :, :], mask_in[:, :, :])
                    nc.vector.tensor_scalar(mneg[:, :, :], mask_in[:, :, :], -10000.0, 10000.0, ALU.mult, ALU.add)
                    nc.vector.drain()
                    dve.sem_inc(mask_released, 1)

                if not cross:
                    take_mask(0)

                def body(k, parts):
                    if cross and "attn" in parts:
                        take_mask(k)
                    for n in range(NH):
                        if "attn" in parts:
                            dve.wait_ge(s_filled, head(k, n))
                            if not first(k) or n >= 2:
                                dve.wait_ge(exp_done, head(k, n - 2))
                            nc.vector.scalar_tensor_tensor(t[:, n % 2, :, :], ps_s[:, n % 2, :, :], -SCALE,
                                                           mask[:, :, :], ALU.mult, ALU.mult).then_inc(s_read, 1)
                            nc.vector.drain()
                            for tc in range(TC):
                                s = t[:, n % 2, tc, :]
                                op = nc.vector.tensor_tensor_reduce(
                                    out=s, in0=s, in1=mneg[:, tc, :], scale=1.0, scalar=3.0e38,
                                    op0=ALU.add, op1=ALU.min, accum_out=tmin[:, n, tc:tc + 1])
                            op.then_inc(t_ready, 1)
                        kk, h = behind(k, n, 1)
                        if ("lag" if n < 1 else "attn") in parts:
                            dve.wait_ge(exp_done, head(kk, h))
                            nc.vector.reciprocal(rsums[:, h, :], psums[:, h, :]).then_inc(rsum_ready, 1)
                        if n == 7 and "front" in parts:
                            dve.wait_ge(x_loaded, 16 * k + 32)
                            layernorm_stats(nc, x_in, stats, mv, ve).then_inc(stats_ready, 1)
                        if n == 9 and "front" in parts:
                            dve.wait_ge(rstd_ready, k + 2)
                            layernorm_apply(nc, x_in, mv, rstd, xhat).then_inc(xhat_ready, 1)
                        for name in FILLS.get(n - 1, []):
                            if units.reader(name) != "dve":
                                continue
                            if PART_OF[name] not in parts:
                                nc.vector.drain()
                                dve.sem_inc(emptied["dve"], 1)
                                continue
                            i = int(name[-1])
                            if name == "out0":
                                dve.wait_ge(xb_ready, k)
                                dve.wait_ge(out_stored, 16 * k)
                            dve.wait_ge(filled, units.filled(k + 1, name))
                            u = ps[:, units.unit(name), :]
                            if name[0] == "v":
                                op = nc.vector.tensor_copy(v[:, i, :], u)
                            else:
                                op = nc.vector.tensor_tensor(x_out[:, i, :], u, xb[:, i, :], ALU.add)
                            op.then_inc(emptied["dve"], 1)
                            if name == "out1":
                                nc.vector.drain()
                                dve.sem_inc(out_ready, 1)

                iterations(dve, body)

            @block.tensor
            def _(pe):
                wq, nq = (w["q"], 0) if cross else (w["qkv"], 0)
                wk, nk = (w["kv"], 0) if cross else (w["qkv"], C)
                wv, nv = (w["kv"], C) if cross else (w["qkv"], 2 * C)
                wo = w["co" if cross else "ao"]
                pe.wait_ge(dsem["ident"], 16)

                def fill(k, name):
                    u = ps[:, units.unit(name), :]
                    two = u.rearrange("p (a n) -> p a n", a=2)
                    what, i = name[:-1], int(name[-1])
                    if what in ("encT", "lnT"):
                        if what == "lnT":
                            pe.wait_ge(xhat_ready, k + 2)
                        else:
                            pe.wait_ge(enc_loaded, 16 * k + 32)
                        src = xhat if what == "lnT" else enc
                        for a in range(2):
                            for tc in range(TC):
                                op = nc.tensor.transpose(two[:, a, tc * P:(tc + 1) * P],
                                                         src[:, tc, (2 * i + a) * P:(2 * i + a + 1) * P],
                                                         w["ident"][:, :])
                    elif what in ("q", "k"):
                        if name == "q0":
                            pe.wait_ge(dsem["q_" + tag], 16)
                            pe.wait_ge(emptied["act"], units.emptied(k + 1, "lnT1"))
                        if name == "k0":
                            pe.wait_ge(dsem["kv_" + tag], 16)
                        weights, at, src = (wq, nq, lnT) if what == "q" else (wk, nk, srcT)
                        at += i * P
                        for c in range(KC):
                            op = nc.tensor.matmul(u[:, 0:T], weights[:, c, at:at + P], src[:, c, :],
                                                  start=(c == 0), stop=(c == KC - 1))
                    elif what == "v":
                        for c in range(KC):
                            op = nc.tensor.matmul(u, srcT[:, c, i * P:(i + 1) * P], wv[:, c, nv:nv + C],
                                                  start=(c == 0), stop=(c == KC - 1))
                    elif what == "out":
                        if i == 0:
                            pe.wait_ge(dsem["o_" + tag], 16)
                            pe.wait_ge(emptied["act"], units.emptied(k + 1, "ctx3"))
                        for c in range(KC):
                            op = nc.tensor.matmul(u, ctxT[:, c, i * P:(i + 1) * P], wo[:, c, :],
                                                  start=(c == 0), stop=(c == KC - 1))
                    else:
                        kk = k + SHIFT[PART_OF[name]]
                        if i == 0:
                            pe.wait_ge(emptied["dve"], units.emptied(k + 1, "v1"))
                        pe.wait_ge(pt_copied, head(kk, HPC * i + HPC - 1))
                        for kc in range(TC):
                            for g in range(HPC):
                                h = HPC * i + g
                                op = nc.tensor.matmul(u[HD * g:HD * (g + 1), 0:T], v[:, kc, h * HD:(h + 1) * HD],
                                                      probT[:, h % (2 * HPC), kc, :],
                                                      start=(kc == 0), stop=(kc == TC - 1))
                        op.then_inc(pv_done, 1)
                        pe.wait_ge(pv_done, kk * (NH // HPC) + (i + 1))
                        pe.sem_inc(filled, 1)
                        return
                    op.then_inc(filled, 1)

                def body(k, parts):
                    for n in range(NH):
                        if "attn" in parts:
                            m = n // HPC
                            if n % HPC == 0:
                                pe.wait_ge(emptied["act"], units.emptied(k + 1, f"k{m}") if m >= 2
                                           else units.emptied_last(k + 1, f"k{m}"))
                            if not first(k) or n >= 2:
                                pe.wait_ge(s_read, head(k, n - 2))
                            for tc in range(TC):
                                op = nc.tensor.matmul(ps_s[:, n % 2, tc, :], qT[:, m, tc * P:(tc + 1) * P],
                                                      kz[:, n, :], start=True, stop=True)
                            op.then_inc(s_filled, 1)
                        kk, h = behind(k, n, LT)
                        if ("lag" if n < LT else "attn") in parts:
                            pe.wait_ge(prob_ready, head(kk, h))
                            if not first(kk) or h >= 2:
                                pe.wait_ge(pt_copied, head(kk, h - 2))
                            for kc in range(TC):
                                for tc in range(TC):
                                    op = nc.tensor.transpose(ps_t[:, h % 2, kc, tc * P:(tc + 1) * P],
                                                             prob[:, h % 4, tc, kc * P:(kc + 1) * P], w["ident"][:, :])
                            op.then_inc(pt_filled, 1)
                        for name in FILLS.get(n, []):
                            reader, value = units.before(k + 1, name)
                            pe.wait_ge(emptied[reader], value)
                            if PART_OF[name] in parts:
                                fill(k, name)
                            else:
                                nc.tensor.drain()
                                pe.sem_inc(filled, 1)

                iterations(pe, body)


def phase_b(nc, d, w, dsem):
    with ExitStack() as ctx:
        def sb(name, *shape):
            return ctx.enter_context(nc.sbuf_tensor("b_" + name, list(shape), F32))

        def sem(name):
            return ctx.enter_context(nc.semaphore("b_" + name))

        units = Units([("lnT0", 0, "act"), ("lnT1", 1, "act")] +
                      [(f"up{i}", (i + 2) % 6, "act") for i in range(FC // 2)] +
                      [("down0", 6, "dve"), ("down1", 7, "dve")])
        NU = FC // 2

        x_in = sb("x_in", P, TC, C)
        xb = sb("xb", P, TC, C)
        x4 = sb("x4", P, TC, C)
        xhat = sb("xhat", P, TC, C)
        lnT = sb("lnT", P, KC, T)
        h = sb("h", P, 2, 2, T)
        hh = sb("hh", P, 2, 2, T)
        act2 = sb("act2", P, FC, T)
        stats = sb("stats", P, TC, 6)
        mv = sb("mv", P, TC, 2)
        ve = sb("ve", P, TC)
        rstd = sb("rstd", P, TC)
        row_b2 = sb("row_b2", P, C)
        ps = ctx.enter_context(nc.psum_tensor("b_ps", [P, 8, 512], F32))

        row_loaded, x_loaded, x4_stored = sem("row_loaded"), sem("x_loaded"), sem("x4_stored")
        filled = sem("filled")
        emptied = {"act": sem("emptied_act"), "dve": sem("emptied_dve")}
        stats_ready, rstd_ready, xhat_ready = sem("stats_ready"), sem("rstd_ready"), sem("xhat_ready")
        xb_ready, x4_ready = sem("xb_ready"), sem("x4_ready")
        inner_ready, tanh_ready, gelu_ready = sem("inner_ready"), sem("tanh_ready"), sem("gelu_ready")

        x_d = d["x3"].rearrange("b (c p) n -> b p c n", p=P)
        x4_d = d["x4"].rearrange("b (c p) n -> b p c n", p=P)

        with nc.Block() as block:

            @block.sync
            def _(sp):
                sp.sem_inc(x4_stored, 16)
                sp.dma_start(x_in[:, :, :], x_d[0]).then_inc(x_loaded, 16)
                sp.dma_start(row_b2[:, :], d["rows"][ROWS.index("b2")].partition_broadcast(P)).then_inc(row_loaded, 16)
                sp.dma_start(w["w1"][:, :, :], d["w1"].rearrange("(c p) n -> p c n", p=P)).then_inc(dsem["w1"], 16)
                sp.dma_start(w["w2"][:, :, :], d["w2"].rearrange("(c p) n -> p c n", p=P)).then_inc(dsem["w2"], 16)
                for n in WEIGHTS_C:
                    rows = d[n].shape[0]
                    sp.dma_start(w[n][0:rows], d[n]).then_inc(dsem["c"], 16)
                with sp.Fori(0, B - 1) as it:
                    sp.wait_ge(xb_ready, it + 1)
                    sp.dma_start(x_in[:, :, :], x_d[it + 1]).then_inc(x_loaded, 16)
                    sp.wait_ge(x4_ready, it + 1)
                    sp.dma_start(x4_d[it], x4[:, :, :]).then_inc(x4_stored, 16)
                sp.wait_ge(x4_ready, B)
                sp.dma_start(x4_d[B - 1], x4[:, :, :]).then_inc(x4_stored, 16)
                sp.wait_ge(x4_stored, (B + 1) * 16)

            @block.gpsimd
            def _(pool):
                pool.wait_ge(row_loaded, 16)

                def inverse_deviation(k):
                    pool.wait_ge(stats_ready, k)
                    nc.gpsimd.tensor_tensor(rstd[:, :], ve[:, :], w["neghalf"][:, :], ALU.pow).then_inc(rstd_ready, 1)

                def item(it, last):
                    pool.wait_ge(xhat_ready, it + 1)
                    pool.wait_ge(emptied["dve"], units.emptied_last(it, "down1"))
                    nc.gpsimd.tensor_tensor(xb[:, :, :], x_in[:, :, :],
                                            row_b2[:, :].unsqueeze(1).to_broadcast([P, TC, C]),
                                            ALU.add).then_inc(xb_ready, 1)
                    if not last:
                        inverse_deviation(it + 2)

                inverse_deviation(1)
                with pool.Fori(0, B - 1) as it:
                    item(it, False)
                item(B - 1, True)

            @block.scalar
            def _(act):
                act.sem_inc(emptied["act"], units.per["act"])

                def halves(name):
                    return ps[:, units.unit(name), :].rearrange("p (a n) -> p a n", a=2)

                with act.Fori(0, B) as it:
                    for a in range(2):
                        name = f"lnT{a}"
                        act.wait_ge(filled, units.filled(it, name))
                        for c in range(2):
                            op = nc.scalar.activation(lnT[:, 2 * a + c, :], halves(name)[:, c, :], ACT.Identity,
                                                      bias=col(w["cols"], "ln3_b", 2 * a + c),
                                                      scale=col(w["cols"], "ln3_s", 2 * a + c))
                        op.then_inc(emptied["act"], 1)
                    for i in range(NU + 1):
                        if i < NU:
                            name = f"up{i}"
                            act.wait_ge(filled, units.filled(it, name))
                            if i >= 2:
                                act.wait_ge(gelu_ready, it * NU + (i - 1))
                            for c in range(2):
                                bias = col(w["cols"], "b1", 2 * i + c)
                                nc.scalar.activation(h[:, i % 2, c, :], halves(name)[:, c, :], ACT.Identity, bias=bias)
                                op = nc.scalar.activation(hh[:, i % 2, c, :], halves(name)[:, c, :], ACT.Square, bias=bias)
                            op.then_inc(emptied["act"], 1)
                        if i >= 1:
                            act.wait_ge(inner_ready, it * NU + i)
                            s = hh[:, (i - 1) % 2, :, :]
                            nc.scalar.activation(s, s, ACT.Tanh, scale=GELU_A).then_inc(tanh_ready, 1)

            @block.vector
            def _(dve):
                dve.sem_inc(emptied["dve"], units.per["dve"])

                def normalise(k):
                    dve.wait_ge(x_loaded, 16 * k)
                    layernorm_stats(nc, x_in, stats, mv, ve).then_inc(stats_ready, 1)
                    dve.wait_ge(rstd_ready, k)
                    layernorm_apply(nc, x_in, mv, rstd, xhat).then_inc(xhat_ready, 1)

                def gelu(it):
                    for i in range(NU + 1):
                        if i < NU:
                            dve.wait_ge(emptied["act"], units.emptied(it, f"up{i}"))
                            s = hh[:, i % 2, :, :]
                            nc.vector.tensor_scalar(s, s, GELU_B, 1.0, ALU.mult, ALU.add)
                            nc.vector.drain()
                            nc.vector.tensor_tensor(s, s, h[:, i % 2, :, :], ALU.mult).then_inc(inner_ready, 1)
                        if i >= 1:
                            j = i - 1
                            dve.wait_ge(tanh_ready, it * NU + i)
                            nc.vector.scalar_tensor_tensor(act2[:, 2 * j:2 * j + 2, :], hh[:, j % 2, :, :], 1.0,
                                                           h[:, j % 2, :, :], ALU.add, ALU.mult).then_inc(gelu_ready, 1)

                def item(it, last):
                    gelu(it)
                    if not last:
                        normalise(it + 2)
                    dve.wait_ge(xb_ready, it + 1)
                    dve.wait_ge(x4_stored, 16 * it + 16)
                    for tc in range(TC):
                        name = f"down{tc}"
                        dve.wait_ge(filled, units.filled(it, name))
                        nc.vector.scalar_tensor_tensor(x4[:, tc, :], ps[:, units.unit(name), :], 0.5, xb[:, tc, :],
                                                       ALU.mult, ALU.add).then_inc(emptied["dve"], 1)
                    nc.vector.drain()
                    dve.sem_inc(x4_ready, 1)

                normalise(1)
                with dve.Fori(0, B - 1) as it:
                    item(it, False)
                item(B - 1, True)

            @block.tensor
            def _(pe):
                def unit(it, name):
                    reader, value = units.before(it, name)
                    pe.wait_ge(emptied[reader], value)
                    return ps[:, units.unit(name), :]

                with pe.Fori(0, B) as it:
                    pe.wait_ge(xhat_ready, it + 1)
                    for a in range(2):
                        u = unit(it, f"lnT{a}").rearrange("p (a n) -> p a n", a=2)
                        for c in range(2):
                            for tc in range(TC):
                                op = nc.tensor.transpose(u[:, c, tc * P:(tc + 1) * P],
                                                         xhat[:, tc, (2 * a + c) * P:(2 * a + c + 1) * P],
                                                         w["ident"][:, :])
                        op.then_inc(filled, 1)
                    pe.wait_ge(dsem["w1"], 16)
                    pe.wait_ge(emptied["act"], units.emptied(it, "lnT1"))
                    for i in range(NU):
                        u = unit(it, f"up{i}").rearrange("p (a n) -> p a n", a=2)
                        for a in range(2):
                            at = (2 * i + a) * P
                            for c in range(KC):
                                op = nc.tensor.matmul(u[:, a, :], w["w1"][:, c, at:at + P], lnT[:, c, :],
                                                      start=(c == 0), stop=(c == KC - 1))
                        op.then_inc(filled, 1)
                    pe.wait_ge(dsem["w2"], 16)
                    for tc in range(TC):
                        u = unit(it, f"down{tc}")
                        for m in range(FC):
                            if tc == 0 and m % 2 == 0:
                                pe.wait_ge(gelu_ready, it * NU + (m // 2 + 1))
                            op = nc.tensor.matmul(u, act2[:, m, tc * P:(tc + 1) * P], w["w2"][:, m, :],
                                                  start=(m == 0), stop=(m == FC - 1))
                        op.then_inc(filled, 1)


def phase_c(nc, d, out, w, dsem):
    STEPS = RS + 2
    MIX = ("w", "k", "r", "v", "g")
    FILLS = {0: [("g", "dve"), ("y", "dve")], 1: [("xaT", "act")], 2: [("t", "act")], 3: [("mw", "dve"), ("mk", "dve")],
             4: [("dec1", "act")], 5: [("dec2", "act"), ("zT", "act")], 6: [("k", "act")], 7: [("mr", "dve"), ("o", "dve")],
             9: [("r", "act"), ("xcT", "act")], 10: [("mv", "dve"), ("kk", "act")], 11: [("bonus", "act")],
             12: [("v", "dve")], 13: [("mg", "dve"), ("rr", "act")], 15: [("kv", "dve")]}
    PART_OF = {"g": "wkv", "y": "back", "zT": "back", "o": "back", "xcT": "back", "kk": "back", "rr": "back",
               "kv": "back"}
    order = [f for n in range(STEPS) for f in FILLS.get(n, [])]
    units = Units([(name, i % 2, reader) for i, (name, reader) in enumerate(order)])
    STEP_OF = {name: n for n in FILLS for name, _ in FILLS[n]}

    with ExitStack() as ctx:
        def sb(name, *shape, dtype=F32):
            return ctx.enter_context(nc.sbuf_tensor("c_" + name, list(shape), dtype))

        def sem(name):
            return ctx.enter_context(nc.semaphore("c_" + name))

        x_in = sb("x_in", P, TC, C)
        state1 = sb("state1", P, KC)
        xaT = sb("xaT", P, KC, T + 1)
        sx = sb("sx", P, KC, T)
        xmix = sb("xmix", P, 2, KC, T)
        tT = w["tT"]
        decT = sb("decT", DD, T)
        wT = sb("wT", P, 2, KC, T)
        kT, rT = sb("kT", P, 2, KC, T), sb("rT", P, 2, KC, T)
        vh, vl = sb("vh", P, 2, KC, T, dtype=F32R), sb("vl", P, 2, KC, T, dtype=F32R)
        bonusT = sb("bonusT", P, 2, KC, T)
        g2T = sb("g2T", P, 2, KC, T)
        s0 = sb("s0", P, 2, KC, RS)
        S = sb("S", P, 2, KC, T)
        z = sb("z", P, 2, KC, T)
        ba, bb, bc = sb("ba", P, KC, T), sb("bb", P, KC, T), sb("bc", P, KC, T)
        x5 = sb("x5", P, TC, C)
        state0 = sb("state0", P, KC)
        xcT = sb("xcT", P, KC, T + 1)
        yT, sxc, gated = ba, ba, ba
        yc, xhat, xk2, kkT = bb, bb, bb, bb
        sq, zT, xr2, rrt = bc, bc, bc, bc

        def by_token(x):
            return x[:, :, :].rearrange("p (t a) n -> p t (a n)", t=TC)

        norm = {n: (sb(n + "_stats", P, TC, 6), sb(n + "_mv", P, TC, 2), sb(n + "_ve", P, TC), sb(n + "_rstd", P, TC))
                for n in ("ln1", "ln2")}
        NG = TC * RH
        gmean, gvar, grstd = sb("gmean", P, NG), sb("gvar", P, NG), sb("grstd", P, NG)
        spread = sb("spread", P, RS, P, dtype=F32R)
        w = {**w, **{n: sb(n, P, KC, C) for n in LATE_C}}

        acc = ctx.enter_context(nc.psum_tensor("c_acc", [P, KC, T], F32))
        vb = ctx.enter_context(nc.psum_tensor("c_vb", [P, KC, T], F32))
        ps = ctx.enter_context(nc.psum_tensor("c_ps", [P, 2, KC * T], F32))

        spread_loaded, spread_ready = sem("spread_loaded"), sem("spread_ready")
        late_loaded, zeros_ready = sem("late_loaded"), sem("zeros_ready")
        x_loaded, x5_loaded, s0_loaded, out_stored = sem("x_loaded"), sem("x5_loaded"), sem("s0_loaded"), sem("out_stored")
        filled = sem("filled")
        emptied = {"act": sem("emptied_act"), "dve": sem("emptied_dve")}
        stats_ready = {n: sem(n + "_stats_ready") for n in norm}
        rstd_ready = {n: sem(n + "_rstd_ready") for n in norm}
        xhat_ready = {n: sem(n + "_xhat_ready") for n in norm}
        shift_ready, xj_ready, ruk_ready, vh_ready = sem("shift_ready"), sem("xj_ready"), sem("ruk_ready"), sem("vh_ready")
        th_ready, g_used = sem("th_ready"), sem("g_used")
        vb_filled, a_ready, a0_ready, scanned = sem("vb_filled"), sem("a_ready"), sem("a0_ready"), sem("scanned")
        z_ready, summed, acc_read = sem("z_ready"), sem("summed"), sem("acc_read")
        yc_ready, sq_ready, gvar_ready, grstd_ready, zn_ready = (
            sem("yc_ready"), sem("sq_ready"), sem("gvar_ready"), sem("grstd_ready"), sem("zn_ready"))
        shift2_ready, kk_ready, out_ready = sem("shift2_ready"), sem("kk_ready"), sem("out_ready")

        x_d = d["x4"].rearrange("b (c p) n -> b p c n", p=P)
        out_d = out.rearrange("b (c p) n -> b p c n", p=P)

        def channels(name):
            return ps[:, units.unit(name), :].rearrange("p (c n) -> p c n", c=KC)

        def tokens(name):
            return ps[:, units.unit(name), :].rearrange("p (t n) -> p t n", t=TC)

        def flat(x):
            return x.rearrange("p c n -> p (c n)")

        def halves(x):
            return [x[:, 2 * i:2 * i + 2, :].rearrange("p c n -> p (c n)") for i in range(2)]

        def step(k, n):
            return k * RS + (n + 1)

        def first(k):
            return isinstance(k, int) and k == 0

        def iterations(engine, body):
            body(-1, ("front",), 1)
            body(0, ("wkv", "front"), 0)
            with engine.Fori(1, B - 1, 2) as k:
                body(k, ("wkv", "back", "front"), 1)
                body(k + 1, ("wkv", "back", "front"), 0)
            body(B - 1, ("wkv", "back"), 1)
            body(B, ("back",), 0)

        with nc.Block() as block:

            @block.sync
            def _(sp):
                sp.sem_inc(out_stored, 16)

                def load_front(s):
                    sp.dma_start(x_in[:, :, :], x_d[s]).then_inc(x_loaded, 16)
                    sp.dma_start(state1[:, :], d["state_cols"][s][:, 1, :]).then_inc(x_loaded, 16)

                def load_s0(s, par):
                    sp.dma_start(s0[:, par, :, :], d["s0"][s]).then_inc(s0_loaded, 16)

                load_front(0)
                load_s0(0, 0)
                sp.dma_start(z[:, :, :, :].rearrange("p a c n -> p (a c n)"),
                             d["spread"].rearrange("p j m -> p (j m)")).then_inc(spread_loaded, 16)
                for n in LATE_C:
                    sp.dma_start(w[n][:, :, :], d[n].rearrange("(c p) n -> p c n", p=P)).then_inc(late_loaded, 16)

                def body(k, parts, par):
                    if "back" in parts:
                        sp.wait_ge(out_stored, 16 * k)
                        sp.dma_start(x5[:, :, :], x_d[k - 1]).then_inc(x5_loaded, 16)
                        sp.dma_start(state0[:, :], d["state_cols"][k - 1][:, 0, :]).then_inc(x5_loaded, 16)
                    if "front" in parts and not (isinstance(k, int) and k < 0):
                        sp.wait_ge(a0_ready, step(k, 0))
                        load_s0(k + 1, 1 - par)
                    if isinstance(k, int) and k >= B - 2:
                        pass
                    else:
                        sp.wait_ge(emptied["act"], units.emptied(k + 1, "xaT"))
                        load_front(k + 2)
                    if "back" in parts:
                        sp.wait_ge(out_ready, k)
                        sp.dma_start(out_d[k - 1], x5[:, :, :]).then_inc(out_stored, 16)

                body(-1, ("front",), 1)
                body(0, ("wkv", "front"), 0)
                with sp.Fori(1, B - 3, 2) as k:
                    body(k, ("wkv", "back", "front"), 1)
                    body(k + 1, ("wkv", "back", "front"), 0)
                body(B - 3, ("wkv", "back", "front"), 1)
                body(B - 2, ("wkv", "back", "front"), 0)
                body(B - 1, ("wkv", "back"), 1)
                body(B, ("back",), 0)
                sp.wait_ge(out_stored, (B + 1) * 16)

            @block.gpsimd
            def _(pool):
                nc.gpsimd.memset(tT[:, :, :], 0.0)
                nc.gpsimd.memset(wT[:, :, :, 0:1], 0.0).then_inc(zeros_ready, 1)

                def inverse_deviation(name, count):
                    _, _, ve, rstd = norm[name]
                    pool.wait_ge(stats_ready[name], count)
                    nc.gpsimd.tensor_tensor(rstd[:, :], ve[:, :], w["neghalf"][:, 0:TC],
                                            ALU.pow).then_inc(rstd_ready[name], 1)

                def body(k, parts, par):
                    for n in range(STEPS):
                        if n == 0 and "front" in parts:
                            inverse_deviation("ln1", k + 2)
                        if n < RS and "wkv" in parts:
                            pool.wait_ge(scanned, step(k, n))
                            if not first(k) or n >= 2:
                                pool.wait_ge(summed, step(k, n - 2))
                            nc.gpsimd.tensor_tensor(z[:, n % 2, :, :], S[:, n % 2, :, :], rT[:, par, :, :],
                                                    ALU.mult).then_inc(z_ready, 1)
                        if "front" in parts:
                            for i, name in enumerate(MIX):
                                if STEP_OF["m" + name] == n:
                                    pool.wait_ge(emptied["dve"], units.emptied(k + 1, "m" + name))
                                    xj = xmix[:, (i + 1) % 2, :, :]
                                    nc.gpsimd.tensor_tensor(xj, xj, xaT[:, :, 1:T + 1], ALU.add).then_inc(xj_ready, 1)
                        if n == 2 and "back" in parts:
                            pool.wait_ge(gvar_ready, k)
                            nc.gpsimd.tensor_tensor(grstd[:, :], gvar[:, :], w["neghalf"][:, 0:1].to_broadcast([P, NG]),
                                                    ALU.pow).then_inc(grstd_ready, 1)
                        if n == STEP_OF["o"] and "back" in parts:
                            inverse_deviation("ln2", k)

                iterations(pool, body)

            @block.scalar
            def _(act):
                act.wait_ge(zeros_ready, 1)
                act.sem_inc(emptied["act"], units.per["act"])
                act.wait_ge(spread_loaded, 16)
                nc.scalar.copy(spread[:, :, :].rearrange("p j m -> p (j m)"),
                               z[:, :, :, :].rearrange("p a c n -> p (a c n)")).then_inc(spread_ready, 1)

                def shifted(name, dst, state, scale, bias):
                    nc.scalar.copy(dst[:, :, 0], state[:, :])
                    for c in range(KC):
                        op = nc.scalar.activation(dst[:, c, 1:T + 1], channels(name)[:, c, :], ACT.Identity,
                                                  bias=col(w["cols"], bias, c), scale=col(w["cols"], scale, c))
                    return op

                def move(k, name, par):
                    other = 1 - par
                    if name == "g":
                        act.wait_ge(filled, units.filled(k + 1, name))
                        if not first(k):
                            act.wait_ge(g_used, k)
                        nc.scalar.activation(g2T[:, par, :, :], channels(name), ACT.Tanh, scale=0.5).then_inc(th_ready, 1)
                    elif name == "xaT":
                        act.wait_ge(x_loaded, 32 * k + 64)
                        if not (isinstance(k, int) and k < 0):
                            act.wait_ge(xj_ready, NMIX * k + NMIX)
                        act.wait_ge(filled, units.filled(k + 1, name))
                        shifted(name, xaT, state1, "rln1_w", "rln1_b").then_inc(emptied["act"], 1)
                    elif name == "t":
                        act.wait_ge(filled, units.filled(k + 1, name))
                        for j, mix in enumerate(("w", "k", "v", "r", "g")):
                            rows = slice(DM * j % P, DM * j % P + DM)
                            op = nc.scalar.activation(tT[rows, j, :], channels(name)[rows, DM * j // P, :], ACT.Tanh)
                        op.then_inc(emptied["act"], 1)
                    elif name == "dec1":
                        act.wait_ge(filled, units.filled(k + 1, name))
                        nc.scalar.activation(decT[:, :], channels(name)[0:DD, 0, :], ACT.Tanh).then_inc(emptied["act"], 1)
                    elif name == "dec2":
                        if not (isinstance(k, int) and k < 1):
                            act.wait_ge(scanned, k * RS)
                        act.wait_ge(filled, units.filled(k + 1, name))
                        for c in range(KC):
                            nc.scalar.activation(wT[:, other, c, 1:T], channels(name)[:, c, 0:T - 1], ACT.Exp,
                                                 bias=col(w["cols"], "time_decay", c))
                        nc.scalar.drain()
                        nc.scalar.activation(wT[:, other, :, 1:T], wT[:, other, :, 1:T], ACT.Exp,
                                             scale=-1.0).then_inc(emptied["act"], 1)
                    elif name == "k":
                        act.wait_ge(filled, units.filled(k + 1, name))
                        nc.scalar.copy(kT[:, other, :, :], channels(name)).then_inc(emptied["act"], 1)
                    elif name == "r":
                        if not (isinstance(k, int) and k < 1):
                            act.wait_ge(z_ready, k * RS)
                        act.wait_ge(filled, units.filled(k + 1, name))
                        nc.scalar.copy(rT[:, other, :, :], channels(name)).then_inc(emptied["act"], 1)
                    elif name == "bonus":
                        act.wait_ge(filled, units.filled(k + 1, name))
                        nc.scalar.copy(bonusT[:, other, :, :], channels(name)).then_inc(emptied["act"], 1)
                    elif name == "v":
                        act.wait_ge(filled, units.filled(k + 1, name))
                        nc.scalar.copy(vh[:, other, :, :], channels(name)).then_inc(vh_ready, 1)
                    elif name == "y":
                        act.wait_ge(yc_ready, k)
                        nc.scalar.activation(sq[:, :, :], yc[:, :, :], ACT.Square).then_inc(sq_ready, 1)
                    elif name == "zT":
                        act.wait_ge(filled, units.filled(k + 1, name))
                        for c in range(KC):
                            op = nc.scalar.activation(zT[:, c, :], channels(name)[:, c, :], ACT.Identity,
                                                      bias=col(w["cols"], "gn_b", c), scale=col(w["cols"], "gn_w", c))
                        op.then_inc(emptied["act"], 1)
                    elif name == "xcT":
                        act.wait_ge(x5_loaded, 32 * k)
                        act.wait_ge(filled, units.filled(k + 1, name))
                        shifted(name, xcT, state0, "rln2_w", "rln2_b").then_inc(emptied["act"], 1)
                    elif name == "kk":
                        act.wait_ge(filled, units.filled(k + 1, name))
                        nc.scalar.activation(kkT[:, :, :], channels(name), ACT.Relu).then_inc(emptied["act"], 1)
                        nc.scalar.drain()
                        nc.scalar.activation(kkT[:, :, :], kkT[:, :, :], ACT.Square).then_inc(kk_ready, 1)
                    elif name == "rr":
                        act.wait_ge(filled, units.filled(k + 1, name))
                        nc.scalar.activation(by_token(rrt), tokens(name), ACT.Tanh, scale=0.5).then_inc(emptied["act"], 1)

                def body(k, parts, par):
                    for n in range(STEPS):
                        if n < RS and "wkv" in parts:
                            if n == 0:
                                act.wait_ge(s0_loaded, 16 * k + 16)
                            if not first(k) or n >= 2:
                                act.wait_ge(z_ready, step(k, n - 2))
                            nc.scalar.copy(S[:, n % 2, :, 0], s0[:, par, :, n]).then_inc(a0_ready, 1)
                        for name, reader in FILLS.get(n, []):
                            if PART_OF.get(name, "front") in parts:
                                move(k, name, par)
                            elif reader == "act":
                                nc.scalar.drain()
                                act.sem_inc(emptied["act"], 1)

                iterations(act, body)

            @block.vector
            def _(dve):
                dve.sem_inc(emptied["dve"], units.per["dve"])
                dve.sem_inc(g_used, 1)

                def groups(x):
                    return x.rearrange("p t (h s) -> p (t h) s", s=RS)

                def over_group(x):
                    return x[:, :].unsqueeze(2).to_broadcast([P, NG, RS])

                def shift(src, dst, mixes):
                    nc.vector.tensor_tensor(dst[:, :, :], src[:, :, 0:T], src[:, :, 1:T + 1], ALU.subtract)
                    nc.vector.drain()
                    for x, mix, ready in mixes:
                        for c in range(KC):
                            op = nc.vector.scalar_tensor_tensor(x[:, c, :], dst[:, c, :], col(w["cols"], mix, c),
                                                                src[:, c, 1:T + 1], ALU.mult, ALU.add)
                        op.then_inc(ready, 1)

                def mix(k, name):
                    dve.wait_ge(filled, units.filled(k + 1, "m" + name))
                    for c in range(KC):
                        op = nc.vector.scalar_tensor_tensor(xmix[:, (MIX.index(name) + 1) % 2, c, :],
                                                            channels("m" + name)[:, c, :],
                                                            col(w["cols"], "maa_" + name, c), sx[:, c, :], ALU.add, ALU.mult)
                    op.then_inc(emptied["dve"], 1)

                def front(k, n, other):
                    if n == 1:
                        dve.wait_ge(emptied["act"], units.emptied(k + 1, "xaT"))
                        if not (isinstance(k, int) and k < 0):
                            dve.wait_ge(filled, units.filled(k, "v"))
                        shift(xaT, sx, [(xmix[:, 0, :, :], "maa_x", shift_ready)])
                    for name in MIX:
                        if n == STEP_OF["m" + name]:
                            mix(k, name)
                    if n == STEP_OF["r"]:
                        dve.wait_ge(emptied["act"], units.emptied(k + 1, "r"))
                        for c in range(KC):
                            op = nc.vector.scalar_tensor_tensor(bonusT[:, other, c, :], rT[:, other, c, :],
                                                                col(w["cols"], "faaaa", c), kT[:, other, c, :],
                                                                ALU.mult, ALU.mult)
                        op.then_inc(ruk_ready, 1)
                    if n == STEP_OF["v"]:
                        dve.wait_ge(vh_ready, k + 2)
                        dve.wait_ge(emptied["act"], units.emptied(k + 1, "bonus"))
                        nc.vector.tensor_tensor(vl[:, other, :, :], channels("v"), vh[:, other, :, :], ALU.subtract)
                        nc.vector.tensor_tensor(bonusT[:, other, :, :], channels("v"), bonusT[:, other, :, :],
                                                ALU.mult)
                        nc.vector.drain()
                        dve.sem_inc(emptied["dve"], 1)

                def back(k, n, other):
                    ln2 = norm["ln2"]
                    if n == 0:
                        dve.wait_ge(filled, units.filled(k + 1, "y"))
                        nc.vector.reduce_sum(gmean[:, :], groups(tokens("y")), axis=AX)
                        nc.vector.drain()
                        nc.vector.tensor_scalar(gmean[:, :], gmean[:, :], 1.0 / RS, None, ALU.mult)
                        nc.vector.drain()
                        nc.vector.tensor_tensor(groups(by_token(yc)), groups(tokens("y")), over_group(gmean),
                                                ALU.subtract)
                        nc.vector.drain()
                        dve.sem_inc(emptied["dve"], 1)
                        dve.sem_inc(yc_ready, 1)
                    if n == 1:
                        dve.wait_ge(sq_ready, k)
                        nc.vector.reduce_sum(gvar[:, :], groups(by_token(sq)), axis=AX)
                        nc.vector.drain()
                        nc.vector.tensor_scalar(gvar[:, :], gvar[:, :], 1.0 / RS, EPS, ALU.mult,
                                                ALU.add).then_inc(gvar_ready, 1)
                    if n == 4:
                        dve.wait_ge(grstd_ready, k)
                        nc.vector.tensor_tensor(groups(by_token(yc)), groups(by_token(yc)), over_group(grstd),
                                                ALU.mult).then_inc(zn_ready, 1)
                    if n == STEP_OF["zT"]:
                        dve.wait_ge(emptied["act"], units.emptied(k + 1, "zT"))
                        nc.vector.tensor_tensor(zT[:, :, :], zT[:, :, :], g2T[:, other, :, :], ALU.mult).then_inc(g_used, 1)
                    if n == STEP_OF["o"]:
                        dve.wait_ge(x5_loaded, 32 * k)
                        dve.wait_ge(filled, units.filled(k + 1, "o"))
                        nc.vector.scalar_tensor_tensor(x5[:, :, :], tokens("o"), 0.5, x5[:, :, :], ALU.mult,
                                                       ALU.add).then_inc(emptied["dve"], 1)
                        nc.vector.drain()
                        layernorm_stats(nc, x5, *ln2[:3]).then_inc(stats_ready["ln2"], 1)
                    if n == STEP_OF["o"] + 1:
                        dve.wait_ge(rstd_ready["ln2"], k)
                        layernorm_apply(nc, x5, ln2[1], ln2[3], by_token(xhat)).then_inc(xhat_ready["ln2"], 1)
                    if n == STEP_OF["xcT"]:
                        dve.wait_ge(emptied["act"], units.emptied(k + 1, "xcT"))
                        shift(xcT, sxc, [(xk2, "fmaa_k", shift2_ready), (xr2, "fmaa_r", shift2_ready)])
                    if n == STEP_OF["kv"]:
                        dve.wait_ge(emptied["act"], units.emptied(k + 1, "rr"))
                        dve.wait_ge(filled, units.filled(k + 1, "kv"))
                        nc.vector.scalar_tensor_tensor(by_token(gated), by_token(rrt), 1.0, tokens("kv"), ALU.add,
                                                       ALU.mult).then_inc(emptied["dve"], 1)
                        nc.vector.drain()
                        nc.vector.scalar_tensor_tensor(x5[:, :, :], by_token(gated), 0.5, x5[:, :, :], ALU.mult,
                                                       ALU.add).then_inc(out_ready, 1)

                def body(k, parts, par):
                    other = 1 - par
                    ln1 = norm["ln1"]
                    for n in range(STEPS):
                        if n == 0 and "back" in parts:
                            nc.vector.drain()
                            dve.wait_ge(summed, k * RS)
                            nc.vector.tensor_tensor(yT[:, :, :], acc[:, :, :], bonusT[:, other, :, :],
                                                    ALU.add).then_inc(acc_read, 1)
                        if n == 0 and "front" in parts:
                            nc.vector.drain()
                            dve.wait_ge(x_loaded, 32 * k + 64)
                            layernorm_stats(nc, x_in, *ln1[:3]).then_inc(stats_ready["ln1"], 1)
                        if n == 1 and "front" in parts:
                            dve.wait_ge(rstd_ready["ln1"], k + 2)
                            layernorm_apply(nc, x_in, ln1[1], ln1[3], x_in).then_inc(xhat_ready["ln1"], 1)
                        if n < RS and "wkv" in parts:
                            dve.wait_ge(vb_filled, step(k, n))
                            if not first(k) or n >= 2:
                                dve.wait_ge(z_ready, step(k, n - 2))
                            nc.vector.tensor_tensor(S[:, n % 2, :, 1:T], kT[:, par, :, 0:T - 1], vb[:, :, 0:T - 1],
                                                    ALU.mult).then_inc(a_ready, 1)
                            nc.vector.drain()
                            dve.wait_ge(a0_ready, step(k, n))
                            nc.vector.tensor_tensor_scan(flat(S[:, n % 2, :, :]), flat(wT[:, par, :, :]),
                                                         flat(S[:, n % 2, :, :]), 0.0, ALU.mult,
                                                         ALU.add).then_inc(scanned, 1)
                        if n == 0 and "wkv" in parts:
                            dve.wait_ge(th_ready, k + 1)
                            nc.vector.scalar_tensor_tensor(g2T[:, par, :, :], g2T[:, par, :, :], 1.0, channels("g"),
                                                           ALU.add, ALU.mult).then_inc(emptied["dve"], 1)
                        if "front" in parts:
                            front(k, n, other)
                        if "back" in parts:
                            back(k, n, other)
                        for name, reader in FILLS.get(n, []):
                            if reader == "dve" and PART_OF.get(name, "front") not in parts:
                                nc.vector.drain()
                                dve.sem_inc(emptied["dve"], 1)

                iterations(dve, body)

            @block.tensor
            def _(pe):
                pe.wait_ge(dsem["c"], 16 * len(WEIGHTS_C))
                pe.wait_ge(zeros_ready, 1)

                def to_channel_layout(name, src):
                    for c in range(KC):
                        for tc in range(TC):
                            op = nc.tensor.transpose(channels(name)[:, c, tc * P:(tc + 1) * P],
                                                     src[:, tc, c * P:(c + 1) * P], w["ident"][:, :])
                    return op

                def project(name, weights, src):
                    for m in range(KC):
                        for c in range(KC):
                            op = nc.tensor.matmul(channels(name)[:, m, :], weights[:, c, m * P:(m + 1) * P],
                                                  src[:, c, :], start=(c == 0), stop=(c == KC - 1))
                    return op

                def project_to_tokens(name, src, weights):
                    for tc in range(TC):
                        for c in range(KC):
                            op = nc.tensor.matmul(tokens(name)[:, tc, :], src[:, c, tc * P:(tc + 1) * P],
                                                  weights[:, c, :], start=(c == 0), stop=(c == KC - 1))
                    return op

                def mixed(k, i, name):
                    pe.wait_ge(xj_ready, NMIX * k + (NMIX + i + 1))
                    return project(name, w["W" + name], xmix[:, (i + 1) % 2, :, :])

                def fill(k, name, other):
                    u = channels(name)
                    if name == "g":
                        pe.wait_ge(xj_ready, NMIX * k + NMIX)
                        op = project(name, w["Wg"], xmix[:, 1, :, :])
                    elif name == "xaT":
                        pe.wait_ge(xhat_ready["ln1"], k + 2)
                        op = to_channel_layout(name, x_in)
                    elif name == "t":
                        pe.wait_ge(shift_ready, k + 2)
                        for n0, n in ((0, P), (P, DM)):
                            for c in range(KC):
                                op = nc.tensor.matmul(u[0:n, n0 // P, :], w["maa_w1"][:, c, n0:n0 + n],
                                                      xmix[:, 0, c, :], start=(c == 0), stop=(c == KC - 1))
                    elif name in ("mw", "mk", "mr", "mv", "mg"):
                        if name == "mw":
                            pe.wait_ge(emptied["act"], units.emptied(k + 1, "t"))
                        j = "wkvrg".index(name[1])
                        for c in range(KC):
                            op = nc.tensor.matmul(u[:, c, :], w["maa_w2"][:, DM * j // P, c * P:(c + 1) * P],
                                                  tT[:, j, :], start=True, stop=True)
                    elif name == "dec1":
                        pe.wait_ge(xj_ready, NMIX * k + (NMIX + 1))
                        for c in range(KC):
                            op = nc.tensor.matmul(u[0:DD, 0, :], w["decay_w1"][:, c, :], xmix[:, 1, c, :],
                                                  start=(c == 0), stop=(c == KC - 1))
                    elif name == "dec2":
                        pe.wait_ge(emptied["act"], units.emptied(k + 1, "dec1"))
                        for c in range(KC):
                            op = nc.tensor.matmul(u[:, c, :], w["decay_w2"][0:DD, c * P:(c + 1) * P], decT[:, :],
                                                  start=True, stop=True)
                    elif name == "k":
                        op = mixed(k, 1, name)
                    elif name == "r":
                        op = mixed(k, 2, name)
                    elif name == "v":
                        op = mixed(k, 3, name)
                    elif name == "bonus":
                        pe.wait_ge(ruk_ready, k + 2)
                        for to, src in zip(halves(u), halves(bonusT[:, other, :, :])):
                            op = nc.tensor.matmul(to, w["same_head"][:, :], src, start=True, stop=True)
                    elif name == "y":
                        pe.wait_ge(acc_read, k)
                        for tc in range(TC):
                            for c in range(KC):
                                op = nc.tensor.transpose(tokens(name)[:, tc, c * P:(c + 1) * P],
                                                         yT[:, c, tc * P:(tc + 1) * P], w["ident"][:, :])
                    elif name == "zT":
                        pe.wait_ge(zn_ready, k)
                        op = to_channel_layout(name, by_token(yc))
                    elif name == "o":
                        pe.wait_ge(late_loaded, 16 * len(LATE_C))
                        pe.wait_ge(g_used, k + 1)
                        op = project_to_tokens(name, zT, w["Wo"])
                    elif name == "xcT":
                        pe.wait_ge(xhat_ready["ln2"], k)
                        op = to_channel_layout(name, by_token(xhat))
                    elif name == "kk":
                        pe.wait_ge(shift2_ready, 2 * k - 1)
                        op = project(name, w["fWk"], xk2)
                    elif name == "rr":
                        pe.wait_ge(shift2_ready, 2 * k)
                        op = project_to_tokens(name, xr2, w["fWr"])
                    else:
                        pe.wait_ge(kk_ready, k)
                        op = project_to_tokens(name, kkT, w["fWv"])
                    op.then_inc(filled, 1)

                def body(k, parts, par):
                    for n in range(STEPS):
                        if n < RS and "wkv" in parts:
                            if n == 0:
                                pe.wait_ge(spread_ready, 1)
                                pe.wait_ge(emptied["dve"], units.emptied_last(k + 1, "v"))
                            if not first(k) or n >= 1:
                                pe.wait_ge(a_ready, step(k, n - 1))
                            for to, high, low in zip(halves(vb), halves(vh[:, par, :, :]), halves(vl[:, par, :, :])):
                                nc.tensor.matmul(to, spread[:, n, :], high, start=True, stop=False)
                                op = nc.tensor.matmul(to, spread[:, n, :], low, start=False, stop=True)
                            op.then_inc(vb_filled, 1)
                        j = n - 2
                        if j >= 0 and "wkv" in parts:
                            pe.wait_ge(z_ready, step(k, j))
                            if j == 0 and not first(k):
                                pe.wait_ge(acc_read, k)
                            for to, src in zip(halves(acc), halves(z[:, j % 2, :, :])):
                                op = nc.tensor.matmul(to, w["gather"][:, RS - 1 - j:RS - 1 - j + P], src,
                                                      start=(j == 0), stop=(j == RS - 1))
                            op.then_inc(summed, 1)
                        for name, _ in FILLS.get(n, []):
                            reader, value = units.before(k + 1, name)
                            pe.wait_ge(emptied[reader], value)
                            if PART_OF.get(name, "front") in parts:
                                fill(k, name, 1 - par)
                            else:
                                nc.tensor.drain()
                                pe.sem_inc(filled, 1)

                iterations(pe, body)


def carve(arena, names):
    out, at = {}, 0
    for name, shape in names:
        n = int(np.prod(shape))
        v = arena[:, at:at + n]
        if len(shape) == 2:
            v = v.rearrange("p (a n) -> p a n", n=shape[1])
        out[name] = v
        at += n
    return out


WEIGHTS_A = [("qkv", (KC, 3 * C)), ("kv", (KC, 2 * C)), ("ao", (KC, C)), ("q", (KC, C)), ("co", (KC, C))]
WEIGHTS_C = {"Wk": (KC, C), "Wv": (KC, C), "Wr": (KC, C), "Wg": (KC, C), "maa_w1": (KC, NMIX * DM),
             "maa_w2": (2, C), "decay_w1": (KC, DD), "decay_w2": (C,), "same_head": (P,), "gather": (P + RS - 1,),
             "Wo": (KC, C), "fWk": (KC, C)}
LATE_C = ("fWr", "fWv")


def build_program(nc, d, out):
    with ExitStack() as ctx:
        def sb(name, *shape):
            return ctx.enter_context(nc.sbuf_tensor("w_" + name, list(shape), F32))

        arena = sb("arena", P, 8 * C * C // P)
        w = {"ident": sb("ident", P, P), "cols": sb("cols", P, NCOL), "neghalf": sb("neghalf", P, TC)}
        dsem = {n: ctx.enter_context(nc.semaphore("loaded_" + n))
                for n in ("ident", "cols", "q_s_", "kv_s_", "o_s_", "q_x_", "kv_x_", "o_x_", "w1", "w2", "c")}
        d["x2"] = nc.dram_tensor("x2", (B, T, C), F32, kind="Internal").ap()
        d["x3"] = nc.dram_tensor("x3", (B, T, C), F32, kind="Internal").ap()
        d["x4"] = nc.dram_tensor("x4", (B, T, C), F32, kind="Internal").ap()
        weights_c = carve(arena, list(WEIGHTS_C.items()) + [("tT", (NMIX, T))])
        weights = {**w, **carve(arena, WEIGHTS_A)}
        attention_phase(nc, d, weights, dsem, cross=False)
        attention_phase(nc, d, weights, dsem, cross=True)
        with nc.sbuf_tensor("w_w1", [P, KC, FF], F32) as w1, nc.sbuf_tensor("w_w2", [P, FC, C], F32) as w2:
            phase_b(nc, d, {**w, **weights_c, "w1": w1, "w2": w2}, dsem)
        phase_c(nc, d, out, {**w, **weights_c}, dsem)


def kernel(**inputs):
    import concourse.bacc as bacc
    from concourse.bass_utils import run_bass_kernel_spmd

    g = {k: np.asarray(v) for k, v in inputs.items()}
    L0 = {k[9:]: v for k, v in g.items() if k.startswith("L0_xattn_")}
    L1 = {k[9:]: v for k, v in g.items() if k.startswith("L1_xattn_")}
    vectors = {
        "ln1_s": L0["ln1_s"], "ln1_b": L0["ln1_b"], "b_q": L0["b_qkv"][:C], "b_k": L0["b_qkv"][C:2 * C], "b_v": L0["b_qkv"][2 * C:],
        "ln2_s": L0["ln2_s"], "ln2_b": L0["ln2_b"], "b_qx": L0["b_q"], "b_kx": L0["b_kv"][:C], "b_vx": L0["b_kv"][C:],
        "ln3_s": L0["ln3_s"], "ln3_b": L0["ln3_b"], "b1": L0["b1"], "rln1_w": L1["ln1_w"], "rln1_b": L1["ln1_b"],
        "rln2_w": L1["ln2_w"], "rln2_b": L1["ln2_b"], "maa_x": L1["maa_x"], "maa_w": L1["maa_w"],
        "maa_k": L1["maa_k"], "maa_v": L1["maa_v"], "maa_r": L1["maa_r"], "maa_g": L1["maa_g"],
        "time_decay": L1["time_decay"], "faaaa": L1["faaaa"].reshape(C), "gn_w": L1["gn_w"], "gn_b": L1["gn_b"], "fmaa_k": L1["fmaa_k"],
        "fmaa_r": L1["fmaa_r"]}
    spread = {"b_ao": L0["b_ao"], "b_co": L0["b_co"], "b2": L0["b2"]}
    state = g["ctx_2048"]

    def chunked(m):
        return m.reshape(KC, P, -1).transpose(1, 0, 2)

    mix2 = [L1["maa_w2"][:4].reshape(P, C), np.zeros((P, C), np.float32)]
    mix2[1][:DM] = L1["maa_w2"][4]
    mix2 = np.stack(mix2, axis=1)
    head, chan, j = np.arange(P) // RS, np.arange(P) % RS, np.arange(RS)
    same = (head[:, None] == head[None, :]).astype(np.float32)
    arrays = {
        "x": g["x"], "ctx_2048": state, "mask_self": g["mask_1x1xSxS2_fc1"], "mask_cross": g["mask_Bx1xSxS2_ff1"],
        "cols": np.concatenate([vectors[n].reshape(k, P).T for n, k in COLUMNS], axis=1),
        "rows": np.stack([spread[n] for n in ROWS]).reshape(len(ROWS), 1, C)[:, 0],
        "ident": np.eye(P, dtype=np.float32),
        "w_qkv": L0["w_qkv"], "w_ao": L0["w_ao"], "w_q": L0["w_q"], "w_kv": L0["w_kv"], "w_co": L0["w_co"],
        "w1": L0["w1"], "w2": L0["w2"],
        "state_cols": state[:, :2].reshape(B, 2, KC, P).transpose(0, 3, 1, 2),
        "s0": state[:, 2:2 + RS].reshape(B, KC, P, RS).transpose(0, 2, 1, 3),
        "fWr": L1["fWr"].T, "fWv": L1["fWv"].T,
        "maa_w1": chunked(L1["maa_w1"]), "maa_w2": mix2,
        "decay_w1": chunked(L1["decay_w1"]), "decay_w2": L1["decay_w2"],
        "same_head": same,
        "spread": same[:, None, :] * (chan[:, None, None] == j[None, :, None]),
        "gather": (np.arange(P + RS - 1)[None, :] == (RS * head + RS - 1)[:, None]).astype(np.float32),
    }
    for n in ("Wk", "Wv", "Wr", "Wg", "Wo", "fWk"):
        arrays[n] = chunked(L1[n].T)
    nc = bacc.Bacc("TRN2", target_bir_lowering=False, num_devices=1)
    feed, d = {}, {}
    for name, a in arrays.items():
        a = np.ascontiguousarray(a)
        feed["in_" + name] = a
        d[name] = nc.dram_tensor("in_" + name, a.shape, mybir.dt.from_np(a.dtype), kind="ExternalInput").ap()
    out = nc.dram_tensor("out_0", (B, T, C), F32, kind="ExternalOutput").ap()
    build_program(nc, d, out)
    r = run_bass_kernel_spmd(nc, [feed], core_ids=[0])
    return r.results[0]["out_0"]
```

```python
from contextlib import ExitStack

import concourse.bass as bass
import numpy as np
from concourse import mybir

F32 = mybir.dt.float32
F32R = mybir.dt.float32r
ALU = mybir.AluOpType
ACT = mybir.ActivationFunctionType
AX = mybir.AxisListType.X

P = 128
B, T, C = 16, 256, 512
KC = C // P
TC = T // P
NH, HD = 16, 32
HPC = P // HD
FF = 4 * C
FC = FF // P
RH, RS = 32, 16
DM, NMIX = 32, 5
DD = 64
EPS = 1e-5
SCALE = float(HD) ** -0.5
GELU_A, GELU_B = 0.7978845608028654, 0.044715

COLUMNS = [("ln1_s", KC), ("ln1_b", KC), ("b_q", KC), ("b_k", KC), ("b_v", KC), ("ln2_s", KC), ("ln2_b", KC), ("b_qx", KC),
           ("b_kx", KC), ("b_vx", KC), ("ln3_s", KC), ("ln3_b", KC), ("b1", FC), ("rln1_w", KC), ("rln1_b", KC),
           ("rln2_w", KC), ("rln2_b", KC), ("maa_x", KC), ("maa_w", KC), ("maa_k", KC), ("maa_v", KC),
           ("maa_r", KC), ("maa_g", KC), ("time_decay", KC), ("faaaa", KC), ("gn_w", KC),
           ("gn_b", KC), ("fmaa_k", KC), ("fmaa_r", KC)]
COL_AT, NCOL = {}, 0
for _name, _n in COLUMNS:
    COL_AT[_name] = NCOL
    NCOL += _n
ROWS = ["b_ao", "b_co", "b2"]


class Units:

    def __init__(self, uses):
        self.uses = uses
        self.at = {name: i for i, (name, _, _) in enumerate(uses)}
        self.per = {}
        self.order = {}
        for name, _, reader in uses:
            self.per[reader] = self.per.get(reader, 0) + 1
            self.order[name] = self.per[reader]

    def filled(self, it, name):
        return it * len(self.uses) + (self.at[name] + 1)

    def emptied(self, it, name):
        per = self.per[self.reader(name)]
        return it * per + (per + self.order[name])

    def emptied_last(self, it, name):
        return it * self.per[self.reader(name)] + self.order[name]

    def reader(self, name):
        return self.uses[self.at[name]][2]

    def unit(self, name):
        return self.uses[self.at[name]][1]

    def before(self, it, name):
        here = self.at[name]
        same = [u for u in self.uses if u[1] == self.unit(name)]
        k = same.index(self.uses[here])
        last = same[k - 1]
        per = self.per[last[2]]
        return last[2], it * per + (self.order[last[0]] + (per if k else 0))


def col(cols, name, c):
    return cols[:, COL_AT[name] + c:COL_AT[name] + c + 1]


def layernorm_stats(nc, x, stats, mv, ve):
    for tc in range(TC):
        nc.vector.bn_stats(stats[:, tc, :], x[:, tc, :])
    nc.vector.drain()
    for tc in range(TC):
        nc.vector.bn_aggr(mv[:, tc, :], stats[:, tc, :])
    nc.vector.drain()
    return nc.vector.tensor_scalar(ve[:, :], mv[:, :, 1], EPS, None, ALU.add)


def layernorm_apply(nc, x, mv, rstd, xhat):
    for tc in range(TC):
        last = nc.vector.tensor_scalar(xhat[:, tc, :], x[:, tc, :], mv[:, tc, 0:1], rstd[:, tc:tc + 1],
                                       ALU.subtract, ALU.mult)
    return last


def attention_phase(nc, d, w, dsem, cross):
    tag = "x_" if cross else "s_"
    ln_s, ln_b, b_q, b_k, b_v = ("ln2_s", "ln2_b", "b_qx", "b_kx", "b_vx") if cross else (
        "ln1_s", "ln1_b", "b_q", "b_k", "b_v")
    LT = 3
    FILLS = {0: ["k2", "ctx2"], 1: ["q3"], 2: ["k3"], 4: ["ctx3"], 5: ["v0"], 
             6: ["v1"] + (["encT0", "encT1"] if cross else []), 7: ["lnT0", "lnT1", "out0"], 8: ["out1", "ctx0"], 9: ["q0"],
             10: ["k0"], 11: ["q1"], 12: ["k1", "ctx1"], 15: ["q2"]}
    PART = {"attn": ("k2", "q3", "k3", "v0", "v1", "ctx0", "ctx1"), "lag": ("ctx2", "ctx3", "out0", "out1"),
            "front": ("encT0", "encT1", "lnT0", "lnT1", "q0", "k0", "q1", "k1", "q2")}
    PART_OF = {name: part for part, names in PART.items() for name in names}
    SHIFT = {"attn": 0, "lag": -1, "front": 1}
    units = Units([(name, i % 4, "act" if name in ("lnT0", "lnT1") else "dve")
                   for i, name in enumerate(name for n in range(NH) for name in FILLS.get(n, []))])

    with ExitStack() as ctx:
        def sb(name, *shape, dtype=F32):
            return ctx.enter_context(nc.sbuf_tensor(tag + name, list(shape), dtype))

        def split(name, *shape):
            return sb(name + "_high", *shape, dtype=F32R), sb(name + "_low", *shape, dtype=F32R)

        def sem(name):
            return ctx.enter_context(nc.semaphore(tag + name))

        x_in = sb("x_in", P, TC, C)
        xb = sb("xb", P, TC, C)
        x_out = sb("x_out", P, TC, C)
        lnT = sb("lnT", P, KC, T)
        ln_parts = split("ln", P, KC, T)
        enc = sb("enc", P, TC, C) if cross else None
        src_parts = split("enc", P, KC, T) if cross else ln_parts
        parts_qk = sb("parts_qk", P, 2, 4, 2, T, dtype=F32R)
        HIGH, LOW = {"q": 1, "k": 2}, {"q": 0, "k": 3}
        SLOTS = (slice(1, 3), slice(1, 4, 2), slice(0, 3, 2))
        stack = sb("stack", 3 * HD, 2, HPC, KC, T, dtype=F32R)
        v = sb("v", P, TC, C)
        ctx_parts = split("ctx", P, KC, T)
        weights = {n: split("w_" + n, P, KC, C) for n in ("q", "k", "v", "o")}
        mask_in = sb("mask_in", P, TC, T)
        mask = sb("mask", P, TC, T)
        mneg = sb("mneg", P, TC, T)
        t = sb("t", P, 2, TC, T)
        prob = sb("prob", P, 4, TC, T)
        probT = sb("probT", P, 2 * HPC, TC, T)
        stage = probT[:, :, :, :].rearrange("p (s h) c n -> p s (h c n)", s=2)
        tmin = sb("tmin", P, NH, TC)
        psums = sb("psums", P, NH, TC)
        rsums = sb("rsums", P, NH, TC)
        stats = sb("stats", P, TC, 6)
        mv = sb("mv", P, TC, 2)
        ve = sb("ve", P, TC)
        rstd = sb("rstd", P, TC)
        row_out = sb("row_out", P, C)
        ps = ctx.enter_context(nc.psum_tensor(tag + "ps", [P, 4, 512], F32))
        ps_s = ctx.enter_context(nc.psum_tensor(tag + "ps_s", [P, 2, TC, T], F32))
        ps_t = ctx.enter_context(nc.psum_tensor(tag + "ps_t", [P, 2, TC, T], F32))

        row_loaded, x_loaded, xb_loaded = sem("row_loaded"), sem("x_loaded"), sem("xb_loaded")
        enc_loaded, mask_loaded, out_stored = sem("enc_loaded"), sem("mask_loaded"), sem("out_stored")
        mask_released = sem("mask_released")
        filled = sem("filled")
        emptied = {"act": sem("emptied_act"), "dve": sem("emptied_dve")}
        stats_ready, rstd_ready, xhat_ready = sem("stats_ready"), sem("rstd_ready"), sem("xhat_ready")
        xb_ready, out_ready = sem("xb_ready"), sem("out_ready")
        weights_loaded = [sem("weights_loaded_0"), sem("weights_loaded_1")]
        weight_high, weight_split = sem("weight_high"), sem("weight_split")
        high_ready, ln_split, qk_split = sem("high_ready"), sem("ln_split"), sem("qk_split")
        stacked = [sem(f"stacked_{g}") for g in range(HPC)]
        s_filled, s_read, t_ready = sem("s_filled"), sem("s_read"), sem("t_ready")
        exp_done, rsum_ready, prob_ready = sem("exp_done"), sem("rsum_ready"), sem("prob_ready")
        pt_filled, pt_copied, pv_done = sem("pt_filled"), sem("pt_copied"), sem("pv_done")

        x_d = d["x2" if cross else "x"].rearrange("b (c p) n -> b p c n", p=P)
        out_d = d["x3" if cross else "x2"].rearrange("b (c p) n -> b p c n", p=P)
        qkv_d = [(d["w_kv"], 0), (d["w_kv"], 1)] if cross else [(d["w_qkv"], 1), (d["w_qkv"], 2)]
        weights_d = [(d["w_q"] if cross else d["w_qkv"], 0)] + qkv_d + [(d["w_co" if cross else "w_ao"], 0)]
        if cross:
            enc_d = d["ctx_2048"].rearrange("b (c p) n -> b p c n", p=P)
            mask_d = d["mask_cross"].rearrange("b o (c p) n -> b p (o c) n", p=P)
        else:
            self_d = d["mask_self"].rearrange("a o (c p) n -> p (a o c) n", p=P)

        def head(k, h):
            return k * NH + (h + 1)

        def behind(k, n, lag):
            return (k, n - lag) if n >= lag else (k - 1, n - lag + NH)

        def first(k):
            return isinstance(k, int) and k == 0

        SPLIT = [name for n in range(NH) for name in FILLS.get(n, []) if name[:-1] in ("q", "k", "ctx", "encT")]

        QK = [name for name in SPLIT if name[0] in "qk"]
        LATE = len([name for name in QK if PART_OF[name] == "attn"])

        def high_done(k, name):
            return (k + 1) * len(SPLIT) + (SPLIT.index(name) + 1)

        def iterations(engine, body):
            body(-1, ("front",))
            body(0, ("attn", "front"))
            with engine.Fori(1, B - 1) as k:
                body(k, ("attn", "lag", "front"))
            body(B - 1, ("attn", "lag"))
            body(B, ("lag",))

        with nc.Block() as block:

            @block.sync
            def _(sp):
                sp.sem_inc(out_stored, 16)
                if cross:
                    sp.dma_start(enc[:, :, :], enc_d[0]).then_inc(enc_loaded, 16)
                    sp.dma_start(mask_in[:, :, :], mask_d[0]).then_inc(mask_loaded, 16)
                sp.dma_start(x_in[:, :, :], x_d[0]).then_inc(x_loaded, 16)
                if not cross:
                    sp.dma_start(w["ident"][:, :], d["ident"]).then_inc(dsem["ident"], 16)
                    sp.dma_start(w["cols"][:, :], d["cols"]).then_inc(dsem["cols"], 16)
                    sp.dma_start(mask_in[:, :, :], self_d).then_inc(mask_loaded, 16)
                for i, (src, third) in enumerate(weights_d):
                    if i >= 2:
                        sp.wait_ge(weight_split, i - 1)
                    sp.dma_start(stage[:, i % 2, :].rearrange("p (c n) -> p c n", c=KC),
                                 src.rearrange("(c p) n -> p c n", p=P)[:, :, third * C:(third + 1) * C]
                                 ).then_inc(weights_loaded[i % 2], 16)
                sp.dma_start(row_out[:, :], d["rows"][ROWS.index("b_co" if cross else "b_ao")].partition_broadcast(P)
                             ).then_inc(row_loaded, 16)

                def stack_up(split, pair):
                    sp.wait_ge(qk_split, split)
                    for g in range(HPC):
                        for slot, pick in enumerate(SLOTS):
                            sp.dma_start(
                                stack[slot * HD:(slot + 1) * HD, :, g, 2 * pair:2 * pair + 2, :]
                                .rearrange("p s i t -> p s (i t)").bitcast(F32),
                                parts_qk[g * HD:(g + 1) * HD, pair, pick, :, :]
                                .rearrange("p s i t -> p s (i t)").bitcast(F32)).then_inc(stacked[g], 16)

                def first_pair(k):
                    stack_up((k + 1) * 2 * KC + (QK.index("k1") + 1 - LATE - 2 * KC), 0)

                def second_pair(k):
                    stack_up((k + 1) * 2 * KC, 1)

                def load_front(k):
                    sp.wait_ge(filled, units.filled(k - 1, "lnT1"))
                    sp.dma_start(x_in[:, :, :], x_d[k]).then_inc(x_loaded, 16)
                    if cross:
                        sp.wait_ge(filled, units.filled(k - 1, "encT1"))
                        sp.dma_start(enc[:, :, :], enc_d[k]).then_inc(enc_loaded, 16)

                def load_mask(k):
                    if cross:
                        sp.wait_ge(mask_released, k)
                        sp.dma_start(mask_in[:, :, :], mask_d[k]).then_inc(mask_loaded, 16)

                def load_xb(k):
                    if not first(k):
                        sp.wait_ge(emptied["dve"], units.emptied(k + 1, "out1"))
                    sp.dma_start(xb[:, :, :], x_d[k]).then_inc(xb_loaded, 16)

                def store(k):
                    sp.wait_ge(out_ready, k + 1)
                    sp.dma_start(out_d[k], x_out[:, :, :]).then_inc(out_stored, 16)

                first_pair(0)
                load_front(1)
                second_pair(0)
                load_xb(0)
                load_mask(1)
                first_pair(1)
                with sp.Fori(1, B - 1) as k:
                    load_front(k + 1)
                    second_pair(k)
                    load_mask(k + 1)
                    load_xb(k)
                    store(k - 1)
                    first_pair(k + 1)
                second_pair(B - 1)
                load_xb(B - 1)
                store(B - 2)
                store(B - 1)
                sp.wait_ge(out_stored, (B + 1) * 16)

            @block.gpsimd
            def _(pool):
                nc.gpsimd.memset(w["neghalf"][:, :], -0.5)
                nc.gpsimd.drain()
                pool.wait_ge(row_loaded, 16)

                def body(k, parts):
                    for n in range(NH):
                        if n == 1 and "lag" in parts:
                            pool.wait_ge(xb_loaded, 16 * k)
                            nc.gpsimd.tensor_tensor(xb[:, :, :], xb[:, :, :],
                                                    row_out[:, :].unsqueeze(1).to_broadcast([P, TC, C]),
                                                    ALU.add).then_inc(xb_ready, 1)
                        kk, h = behind(k, n, 1)
                        if ("lag" if n < 1 else "attn") in parts:
                            pool.wait_ge(rsum_ready, head(kk, h))
                            nc.gpsimd.tensor_tensor(prob[:, h % 4, :, :], prob[:, h % 4, :, :],
                                                    rsums[:, h, :].unsqueeze(2).to_broadcast([P, TC, T]),
                                                    ALU.mult).then_inc(prob_ready, 1)
                        if n == 5 and "front" in parts:
                            pool.wait_ge(stats_ready, k + 2)
                            nc.gpsimd.tensor_tensor(rstd[:, :], ve[:, :], w["neghalf"][:, :],
                                                    ALU.pow).then_inc(rstd_ready, 1)

                iterations(pool, body)

            @block.scalar
            def _(act):
                act.wait_ge(dsem["cols"], 16)
                act.sem_inc(emptied["act"], units.per["act"])
                for i, n in enumerate(weights):
                    act.wait_ge(weights_loaded[i % 2], 16 * (i // 2 + 1))
                    nc.scalar.copy(weights[n][0][:, :, :].rearrange("p c n -> p (c n)"),
                                   stage[:, i % 2, :]).then_inc(weight_high, 1)
                act.wait_ge(weight_split, 4)

                def move(k, name):
                    u = ps[:, units.unit(name), :]
                    two = u.rearrange("p (a n) -> p a n", a=2)
                    i = int(name[-1])
                    if name[:-1] == "encT":
                        act.wait_ge(filled, units.filled(k + 1, name))
                        nc.scalar.copy(src_parts[0][:, 2 * i:2 * i + 2, :], two).then_inc(high_ready, 1)
                    elif name[:-1] == "lnT":
                        act.wait_ge(filled, units.filled(k + 1, name))
                        for a in range(2):
                            nc.scalar.activation(lnT[:, 2 * i + a, :], two[:, a, :], ACT.Identity,
                                                 bias=col(w["cols"], ln_b, 2 * i + a),
                                                 scale=col(w["cols"], ln_s, 2 * i + a))
                        nc.scalar.drain()
                        nc.scalar.copy(ln_parts[0][:, 2 * i:2 * i + 2, :],
                                       lnT[:, 2 * i:2 * i + 2, :]).then_inc(emptied["act"], 1)
                    elif name[0] in "qk":
                        act.wait_ge(filled, units.filled(k + 1, name))
                        nc.scalar.activation(parts_qk[:, i // 2, HIGH[name[0]], i % 2, :], u[:, 0:T], ACT.Identity,
                                             bias=col(w["cols"], b_q if name[0] == "q" else b_k, i)
                                             ).then_inc(high_ready, 1)
                    else:
                        act.wait_ge(filled, units.filled(k + 1, name))
                        nc.scalar.activation(ctx_parts[0][:, i, :], u[:, 0:T], ACT.Identity,
                                             bias=col(w["cols"], b_v, i)).then_inc(high_ready, 1)

                def body(k, parts):
                    for n in range(NH):
                        if "attn" in parts:
                            act.wait_ge(t_ready, head(k, n))
                            for tc in range(TC):
                                op = nc.scalar.activation(prob[:, n % 4, tc, :], t[:, n % 2, tc, :], ACT.Exp,
                                                          bias=tmin[:, n, tc:tc + 1], scale=-1.0,
                                                          accum_out=psums[:, n, tc:tc + 1])
                            op.then_inc(exp_done, 1)
                        kk, h = behind(k, n, LT)
                        if ("lag" if n < LT else "attn") in parts:
                            act.wait_ge(pt_filled, head(kk, h))
                            g = h // HPC
                            if not first(kk) or g >= 2:
                                act.wait_ge(pv_done, kk * (NH // HPC) + (g - 1))
                            nc.scalar.copy(probT[:, h % (2 * HPC), :, :], ps_t[:, h % 2, :, :]).then_inc(pt_copied, 1)
                        for name in FILLS.get(n, []):
                            if name not in SPLIT and units.reader(name) == "dve":
                                continue
                            if PART_OF[name] in parts:
                                move(k, name)
                            else:
                                nc.scalar.drain()
                                act.sem_inc(high_ready if name in SPLIT else emptied["act"], 1)

                iterations(act, body)

            @block.vector
            def _(dve):
                dve.sem_inc(emptied["dve"], units.per["dve"])

                for i, n in enumerate(weights):
                    dve.wait_ge(weight_high, i + 1)
                    nc.vector.tensor_tensor(weights[n][1][:, :, :].rearrange("p c n -> p (c n)"), stage[:, i % 2, :],
                                            weights[n][0][:, :, :].rearrange("p c n -> p (c n)"),
                                            ALU.subtract).then_inc(weight_split, 1)

                def take_mask(k):
                    nc.vector.drain()
                    dve.wait_ge(mask_loaded, 16 * k + 16)
                    nc.vector.tensor_copy(mask[:, :, :], mask_in[:, :, :])
                    nc.vector.tensor_scalar(mneg[:, :, :], mask_in[:, :, :], -10000.0, 10000.0, ALU.mult, ALU.add)
                    nc.vector.drain()
                    dve.sem_inc(mask_released, 1)

                if not cross:
                    take_mask(0)

                def move(k, name, parts):
                    if PART_OF[name] not in parts:
                        if units.reader(name) == "dve":
                            nc.vector.drain()
                            dve.sem_inc(emptied["dve"], 1)
                        return
                    i = int(name[-1])
                    u = ps[:, units.unit(name), :]
                    if name[:-1] == "lnT":
                        dve.wait_ge(emptied["act"], units.emptied(k + 1, name))
                        high, low = [x[:, 2 * i:2 * i + 2, :] for x in ln_parts]
                        nc.vector.tensor_tensor(low, lnT[:, 2 * i:2 * i + 2, :], high, ALU.subtract).then_inc(ln_split, 1)
                    elif name[:-1] == "encT":
                        dve.wait_ge(high_ready, high_done(k, name))
                        high, low = [x[:, 2 * i:2 * i + 2, :] for x in src_parts]
                        nc.vector.tensor_tensor(low, u.rearrange("p (a n) -> p a n", a=2), high,
                                                ALU.subtract).then_inc(emptied["dve"], 1)
                    elif name[0] == "v":
                        dve.wait_ge(filled, units.filled(k + 1, name))
                        nc.vector.tensor_copy(v[:, i, :], u).then_inc(emptied["dve"], 1)
                    elif name[:-1] == "out":
                        if i == 0:
                            dve.wait_ge(xb_ready, k)
                            dve.wait_ge(out_stored, 16 * k)
                        dve.wait_ge(filled, units.filled(k + 1, name))
                        nc.vector.tensor_tensor(x_out[:, i, :], u, xb[:, i, :], ALU.add).then_inc(emptied["dve"], 1)
                        if i == 1:
                            nc.vector.drain()
                            dve.sem_inc(out_ready, 1)
                    else:
                        dve.wait_ge(high_ready, high_done(k, name))
                        if name[:-1] == "ctx":
                            (high, low), bias = [x[:, i, :] for x in ctx_parts], b_v
                        else:
                            high, low = [parts_qk[:, i // 2, x[name[0]], i % 2, :] for x in (HIGH, LOW)]
                            bias = b_q if name[0] == "q" else b_k
                        nc.vector.scalar_tensor_tensor(low, u[:, 0:T], col(w["cols"], bias, i), high, ALU.add,
                                                       ALU.subtract).then_inc(emptied["dve"], 1)
                        if name in QK:
                            nc.vector.drain()
                            dve.sem_inc(qk_split, 1)

                def body(k, parts):
                    if cross and "attn" in parts:
                        take_mask(k)
                    for n in range(NH):
                        if "attn" in parts:
                            dve.wait_ge(s_filled, head(k, n))
                            if not first(k) or n >= 2:
                                dve.wait_ge(exp_done, head(k, n - 2))
                            nc.vector.scalar_tensor_tensor(t[:, n % 2, :, :], ps_s[:, n % 2, :, :], -SCALE,
                                                           mask[:, :, :], ALU.mult, ALU.mult).then_inc(s_read, 1)
                            nc.vector.drain()
                            for tc in range(TC):
                                s = t[:, n % 2, tc, :]
                                op = nc.vector.tensor_tensor_reduce(
                                    out=s, in0=s, in1=mneg[:, tc, :], scale=1.0, scalar=3.0e38,
                                    op0=ALU.add, op1=ALU.min, accum_out=tmin[:, n, tc:tc + 1])
                            op.then_inc(t_ready, 1)
                        kk, h = behind(k, n, 1)
                        if ("lag" if n < 1 else "attn") in parts:
                            dve.wait_ge(exp_done, head(kk, h))
                            nc.vector.reciprocal(rsums[:, h, :], psums[:, h, :]).then_inc(rsum_ready, 1)
                        if n == 4 and "front" in parts:
                            dve.wait_ge(x_loaded, 16 * k + 32)
                            layernorm_stats(nc, x_in, stats, mv, ve).then_inc(stats_ready, 1)
                        if n == 6 and "front" in parts:
                            dve.wait_ge(rstd_ready, k + 2)
                            layernorm_apply(nc, x_in, mv, rstd, x_in).then_inc(xhat_ready, 1)
                        for name in FILLS.get(n - 1, []):
                            move(k, name, parts)
                    for name in FILLS.get(NH - 1, []):
                        move(k, name, parts)

                iterations(dve, body)

            @block.tensor
            def _(pe):
                pe.wait_ge(dsem["ident"], 16)

                def product(out, stationary, moving):
                    (sh, sl), (mh, ml) = stationary, moving
                    for c in range(KC):
                        nc.tensor.matmul(out, sh[:, c, :], mh[:, c, :], start=(c == 0), stop=False)
                        nc.tensor.matmul(out, sh[:, c, :], ml[:, c, :], start=False, stop=False)
                        op = nc.tensor.matmul(out, sl[:, c, :], mh[:, c, :], start=False, stop=(c == KC - 1))
                    return op

                def fill(k, name):
                    u = ps[:, units.unit(name), :]
                    two = u.rearrange("p (a n) -> p a n", a=2)
                    what, i = name[:-1], int(name[-1])
                    if what in ("encT", "lnT"):
                        if what == "lnT":
                            pe.wait_ge(xhat_ready, k + 2)
                        else:
                            pe.wait_ge(enc_loaded, 16 * k + 32)
                        src = x_in if what == "lnT" else enc
                        for a in range(2):
                            for tc in range(TC):
                                op = nc.tensor.transpose(two[:, a, tc * P:(tc + 1) * P],
                                                         src[:, tc, (2 * i + a) * P:(2 * i + a + 1) * P],
                                                         w["ident"][:, :])
                    elif what in ("q", "k"):
                        if name == "q0":
                            pe.wait_ge(weight_split, 2)
                            pe.wait_ge(ln_split, 2 * k + 4)
                        if name == "k0" and cross:
                            pe.wait_ge(emptied["dve"], units.emptied(k + 1, "encT1"))
                        op = product(u[:, 0:T], [x[:, :, i * P:(i + 1) * P] for x in weights[what]],
                                     ln_parts if what == "q" else src_parts)
                    elif what == "v":
                        pe.wait_ge(weight_split, 3)
                        op = product(u, [x[:, :, i * P:(i + 1) * P] for x in src_parts], weights["v"])
                    elif what == "out":
                        if i == 0:
                            pe.wait_ge(weight_split, 4)
                            pe.wait_ge(emptied["dve"], units.emptied(k + 1, "ctx3"))
                        op = product(u, [x[:, :, i * P:(i + 1) * P] for x in ctx_parts], weights["o"])
                    else:
                        kk = k + SHIFT[PART_OF[name]]
                        if i == 0:
                            pe.wait_ge(emptied["dve"], units.emptied(k + 1, "v1"))
                        pe.wait_ge(pt_copied, head(kk, HPC * i + HPC - 1))
                        for kc in range(TC):
                            for g in range(HPC):
                                h = HPC * i + g
                                op = nc.tensor.matmul(u[HD * g:HD * (g + 1), 0:T], v[:, kc, h * HD:(h + 1) * HD],
                                                      probT[:, h % (2 * HPC), kc, :],
                                                      start=(kc == 0), stop=(kc == TC - 1))
                        op.then_inc(pv_done, 1)
                        pe.wait_ge(pv_done, kk * (NH // HPC) + (i + 1))
                        pe.sem_inc(filled, 1)
                        return
                    op.then_inc(filled, 1)

                def body(k, parts):
                    for n in range(NH):
                        if "attn" in parts:
                            m, g = n // HPC, n % HPC
                            if m % 2 == 0:
                                pe.wait_ge(stacked[g], 16 * 3 * (k * 2 + (m // 2 + 1)))
                            if not first(k) or n >= 2:
                                pe.wait_ge(s_read, head(k, n - 2))
                            for tc in range(TC):
                                op = nc.tensor.matmul(ps_s[:, n % 2, tc, :], stack[:, 0, g, m, tc * P:(tc + 1) * P],
                                                      stack[:, 1, g, m, :], start=True, stop=True)
                            op.then_inc(s_filled, 1)
                        kk, h = behind(k, n, LT)
                        if ("lag" if n < LT else "attn") in parts:
                            pe.wait_ge(prob_ready, head(kk, h))
                            if not first(kk) or h >= 2:
                                pe.wait_ge(pt_copied, head(kk, h - 2))
                            for kc in range(TC):
                                for tc in range(TC):
                                    op = nc.tensor.transpose(ps_t[:, h % 2, kc, tc * P:(tc + 1) * P],
                                                             prob[:, h % 4, tc, kc * P:(kc + 1) * P], w["ident"][:, :])
                            op.then_inc(pt_filled, 1)
                        for name in FILLS.get(n, []):
                            reader, value = units.before(k + 1, name)
                            pe.wait_ge(emptied[reader], value)
                            if PART_OF[name] in parts:
                                fill(k, name)
                            else:
                                nc.tensor.drain()
                                pe.sem_inc(filled, 1)

                iterations(pe, body)


def phase_b(nc, d, w, dsem):
    with ExitStack() as ctx:
        def sb(name, *shape):
            return ctx.enter_context(nc.sbuf_tensor("b_" + name, list(shape), F32))

        def sem(name):
            return ctx.enter_context(nc.semaphore("b_" + name))

        units = Units([("lnT0", 0, "act"), ("lnT1", 1, "act")] +
                      [(f"up{i}", (i + 2) % 6, "act") for i in range(FC // 2)] +
                      [("down0", 6, "dve"), ("down1", 7, "dve")])
        NU = FC // 2

        x_in = sb("x_in", P, TC, C)
        xb = sb("xb", P, TC, C)
        x4 = sb("x4", P, TC, C)
        xhat = sb("xhat", P, TC, C)
        lnT = sb("lnT", P, KC, T)
        h = sb("h", P, 2, 2, T)
        hh = sb("hh", P, 2, 2, T)
        act2 = sb("act2", P, FC, T)
        stats = sb("stats", P, TC, 6)
        mv = sb("mv", P, TC, 2)
        ve = sb("ve", P, TC)
        rstd = sb("rstd", P, TC)
        row_b2 = sb("row_b2", P, C)
        ps = ctx.enter_context(nc.psum_tensor("b_ps", [P, 8, 512], F32))

        row_loaded, x_loaded, x4_stored = sem("row_loaded"), sem("x_loaded"), sem("x4_stored")
        filled = sem("filled")
        emptied = {"act": sem("emptied_act"), "dve": sem("emptied_dve")}
        stats_ready, rstd_ready, xhat_ready = sem("stats_ready"), sem("rstd_ready"), sem("xhat_ready")
        xb_ready, x4_ready = sem("xb_ready"), sem("x4_ready")
        inner_ready, tanh_ready, gelu_ready = sem("inner_ready"), sem("tanh_ready"), sem("gelu_ready")

        x_d = d["x3"].rearrange("b (c p) n -> b p c n", p=P)
        x4_d = d["x4"].rearrange("b (c p) n -> b p c n", p=P)

        with nc.Block() as block:

            @block.sync
            def _(sp):
                sp.sem_inc(x4_stored, 16)
                sp.dma_start(x_in[:, :, :], x_d[0]).then_inc(x_loaded, 16)
                sp.dma_start(row_b2[:, :], d["rows"][ROWS.index("b2")].partition_broadcast(P)).then_inc(row_loaded, 16)
                sp.dma_start(w["w1"][:, :, :], d["w1"].rearrange("(c p) n -> p c n", p=P)).then_inc(dsem["w1"], 16)
                sp.dma_start(w["w2"][:, :, :], d["w2"].rearrange("(c p) n -> p c n", p=P)).then_inc(dsem["w2"], 16)
                for n in WEIGHTS_C:
                    rows = d[n].shape[0]
                    sp.dma_start(w[n][0:rows], d[n]).then_inc(dsem["c"], 16)
                with sp.Fori(0, B - 1) as it:
                    sp.wait_ge(xb_ready, it + 1)
                    sp.dma_start(x_in[:, :, :], x_d[it + 1]).then_inc(x_loaded, 16)
                    sp.wait_ge(x4_ready, it + 1)
                    sp.dma_start(x4_d[it], x4[:, :, :]).then_inc(x4_stored, 16)
                sp.wait_ge(x4_ready, B)
                sp.dma_start(x4_d[B - 1], x4[:, :, :]).then_inc(x4_stored, 16)
                sp.wait_ge(x4_stored, (B + 1) * 16)

            @block.gpsimd
            def _(pool):
                pool.wait_ge(row_loaded, 16)

                def inverse_deviation(k):
                    pool.wait_ge(stats_ready, k)
                    nc.gpsimd.tensor_tensor(rstd[:, :], ve[:, :], w["neghalf"][:, :], ALU.pow).then_inc(rstd_ready, 1)

                def item(it, last):
                    pool.wait_ge(xhat_ready, it + 1)
                    pool.wait_ge(emptied["dve"], units.emptied_last(it, "down1"))
                    nc.gpsimd.tensor_tensor(xb[:, :, :], x_in[:, :, :],
                                            row_b2[:, :].unsqueeze(1).to_broadcast([P, TC, C]),
                                            ALU.add).then_inc(xb_ready, 1)
                    if not last:
                        inverse_deviation(it + 2)

                inverse_deviation(1)
                with pool.Fori(0, B - 1) as it:
                    item(it, False)
                item(B - 1, True)

            @block.scalar
            def _(act):
                act.sem_inc(emptied["act"], units.per["act"])

                def halves(name):
                    return ps[:, units.unit(name), :].rearrange("p (a n) -> p a n", a=2)

                with act.Fori(0, B) as it:
                    for a in range(2):
                        name = f"lnT{a}"
                        act.wait_ge(filled, units.filled(it, name))
                        for c in range(2):
                            op = nc.scalar.activation(lnT[:, 2 * a + c, :], halves(name)[:, c, :], ACT.Identity,
                                                      bias=col(w["cols"], "ln3_b", 2 * a + c),
                                                      scale=col(w["cols"], "ln3_s", 2 * a + c))
                        op.then_inc(emptied["act"], 1)
                    for i in range(NU + 1):
                        if i < NU:
                            name = f"up{i}"
                            act.wait_ge(filled, units.filled(it, name))
                            if i >= 2:
                                act.wait_ge(gelu_ready, it * NU + (i - 1))
                            for c in range(2):
                                bias = col(w["cols"], "b1", 2 * i + c)
                                nc.scalar.activation(h[:, i % 2, c, :], halves(name)[:, c, :], ACT.Identity, bias=bias)
                                op = nc.scalar.activation(hh[:, i % 2, c, :], halves(name)[:, c, :], ACT.Square, bias=bias)
                            op.then_inc(emptied["act"], 1)
                        if i >= 1:
                            act.wait_ge(inner_ready, it * NU + i)
                            s = hh[:, (i - 1) % 2, :, :]
                            nc.scalar.activation(s, s, ACT.Tanh, scale=GELU_A).then_inc(tanh_ready, 1)

            @block.vector
            def _(dve):
                dve.sem_inc(emptied["dve"], units.per["dve"])

                def normalise(k):
                    dve.wait_ge(x_loaded, 16 * k)
                    layernorm_stats(nc, x_in, stats, mv, ve).then_inc(stats_ready, 1)
                    dve.wait_ge(rstd_ready, k)
                    layernorm_apply(nc, x_in, mv, rstd, xhat).then_inc(xhat_ready, 1)

                def gelu(it):
                    for i in range(NU + 1):
                        if i < NU:
                            dve.wait_ge(emptied["act"], units.emptied(it, f"up{i}"))
                            s = hh[:, i % 2, :, :]
                            nc.vector.tensor_scalar(s, s, GELU_B, 1.0, ALU.mult, ALU.add)
                            nc.vector.drain()
                            nc.vector.tensor_tensor(s, s, h[:, i % 2, :, :], ALU.mult).then_inc(inner_ready, 1)
                        if i >= 1:
                            j = i - 1
                            dve.wait_ge(tanh_ready, it * NU + i)
                            nc.vector.scalar_tensor_tensor(act2[:, 2 * j:2 * j + 2, :], hh[:, j % 2, :, :], 1.0,
                                                           h[:, j % 2, :, :], ALU.add, ALU.mult).then_inc(gelu_ready, 1)

                def item(it, last):
                    gelu(it)
                    if not last:
                        normalise(it + 2)
                    dve.wait_ge(xb_ready, it + 1)
                    dve.wait_ge(x4_stored, 16 * it + 16)
                    for tc in range(TC):
                        name = f"down{tc}"
                        dve.wait_ge(filled, units.filled(it, name))
                        nc.vector.scalar_tensor_tensor(x4[:, tc, :], ps[:, units.unit(name), :], 0.5, xb[:, tc, :],
                                                       ALU.mult, ALU.add).then_inc(emptied["dve"], 1)
                    nc.vector.drain()
                    dve.sem_inc(x4_ready, 1)

                normalise(1)
                with dve.Fori(0, B - 1) as it:
                    item(it, False)
                item(B - 1, True)

            @block.tensor
            def _(pe):
                def unit(it, name):
                    reader, value = units.before(it, name)
                    pe.wait_ge(emptied[reader], value)
                    return ps[:, units.unit(name), :]

                with pe.Fori(0, B) as it:
                    pe.wait_ge(xhat_ready, it + 1)
                    for a in range(2):
                        u = unit(it, f"lnT{a}").rearrange("p (a n) -> p a n", a=2)
                        for c in range(2):
                            for tc in range(TC):
                                op = nc.tensor.transpose(u[:, c, tc * P:(tc + 1) * P],
                                                         xhat[:, tc, (2 * a + c) * P:(2 * a + c + 1) * P],
                                                         w["ident"][:, :])
                        op.then_inc(filled, 1)
                    pe.wait_ge(dsem["w1"], 16)
                    pe.wait_ge(emptied["act"], units.emptied(it, "lnT1"))
                    for i in range(NU):
                        u = unit(it, f"up{i}").rearrange("p (a n) -> p a n", a=2)
                        for a in range(2):
                            at = (2 * i + a) * P
                            for c in range(KC):
                                op = nc.tensor.matmul(u[:, a, :], w["w1"][:, c, at:at + P], lnT[:, c, :],
                                                      start=(c == 0), stop=(c == KC - 1))
                        op.then_inc(filled, 1)
                    pe.wait_ge(dsem["w2"], 16)
                    for tc in range(TC):
                        u = unit(it, f"down{tc}")
                        for m in range(FC):
                            if tc == 0 and m % 2 == 0:
                                pe.wait_ge(gelu_ready, it * NU + (m // 2 + 1))
                            op = nc.tensor.matmul(u, act2[:, m, tc * P:(tc + 1) * P], w["w2"][:, m, :],
                                                  start=(m == 0), stop=(m == FC - 1))
                        op.then_inc(filled, 1)


def phase_c(nc, d, out, w, dsem):
    STEPS = RS + 2
    MIX = ("w", "k", "r", "v", "g")
    FILLS = {0: [("y", "dve")], 1: [("g", "dve"), ("mw", "dve")], 2: [("mk", "dve")], 3: [("dec1", "act")],
             4: [("k", "act"), ("zT", "act"), ("dec2", "act")], 5: [("mr", "dve")], 6: [("o", "dve")],
             8: [("r", "act"), ("mv", "dve")], 9: [("xcT", "act"), ("bonus", "act")], 11: [("v", "dve")],
             12: [("kk", "act"), ("mg", "dve")], 14: [("rr", "act")], 15: [("xaT", "act")], 16: [("kv", "dve")],
             17: [("t", "act")]}
    BEGUN = {0: "g", 3: "k", 5: "o", 7: "r", 10: "v", 11: "kk", 13: "rr", 15: "kv"}
    PART_OF = {"g": "wkv", "y": "back", "zT": "back", "o": "back", "xcT": "back", "kk": "back", "rr": "back",
               "kv": "back", "xaT": "norm", "t": "norm"}
    order = [f for n in range(STEPS) for f in FILLS.get(n, [])]
    units = Units([(name, i % 2, reader) for i, (name, reader) in enumerate(order)])
    STEP_OF = {name: n for n in FILLS for name, _ in FILLS[n]}
    LN1 = 13

    with ExitStack() as ctx:
        def sb(name, *shape, dtype=F32):
            return ctx.enter_context(nc.sbuf_tensor("c_" + name, list(shape), dtype))

        def sem(name):
            return ctx.enter_context(nc.semaphore("c_" + name))

        state1 = sb("state1", P, KC)
        xaT = sb("xaT", P, KC, T + 1)
        sx = sb("sx", P, KC, T)
        xmix = sb("xmix", P, 2, KC, T)
        x_in = xmix[:, 0, :, :].rearrange("p (t a) n -> p t (a n)", t=TC)
        tT = sb("tT", P, NMIX, T)
        decT = sb("decT", DD, T)
        wT = sb("wT", P, 2, KC, T)
        kT, rT = sb("kT", P, 2, KC, T), sb("rT", P, 2, KC, T)
        vh, vl = sb("vh", P, 2, KC, T, dtype=F32R), sb("vl", P, 2, KC, T, dtype=F32R)
        bonusT = sb("bonusT", P, 2, KC, T)
        g2T = sb("g2T", P, 2, KC, T)
        s0 = sb("s0", P, 2, KC, RS)
        S = sb("S", P, 2, KC, T)
        zh, zl = sb("zh", P, 2, KC, T, dtype=F32R), sb("zl", P, 2, KC, T, dtype=F32R)
        ba, bb, bc = sb("ba", P, KC, T), sb("bb", P, KC, T), sb("bc", P, KC, T)
        x5 = sb("x5", P, TC, C)
        state0 = sb("state0", P, KC)
        xcT = sb("xcT", P, KC, T + 1)
        yT, sxc = ba, ba
        yc, xhat, xk2, kkT, gated = bb, bb, bb, bb, bb
        sq, zT, xr2, rrt = bc, bc, bc, bc

        def by_token(x):
            return x[:, :, :].rearrange("p (t a) n -> p t (a n)", t=TC)

        norm = {n: (sb(n + "_stats", P, TC, 6), sb(n + "_mv", P, TC, 2), sb(n + "_ve", P, TC), sb(n + "_rstd", P, TC))
                for n in ("ln1", "ln2")}
        NG = TC * RH
        gmean, gvar, grstd, gtmp = sb("gmean", P, NG), sb("gvar", P, NG), sb("grstd", P, NG), sb("gtmp", P, NG)
        spread, gather = sb("spread", P, RS, P, dtype=F32R), sb("gather", P, P + RS - 1, dtype=F32R)
        w = {**w, **{n: sb(n, P, KC, C) for n in LATE_C}}

        acc = ctx.enter_context(nc.psum_tensor("c_acc", [P, KC, T], F32))
        vb = ctx.enter_context(nc.psum_tensor("c_vb", [P, KC, T], F32))
        ps = ctx.enter_context(nc.psum_tensor("c_ps", [P, 2, KC * T], F32))

        spread_loaded, spread_ready = sem("spread_loaded"), sem("spread_ready")
        late_loaded, zeros_ready = sem("late_loaded"), sem("zeros_ready")
        x_loaded, x5_loaded, s0_loaded, out_stored = sem("x_loaded"), sem("x5_loaded"), sem("s0_loaded"), sem("out_stored")
        filled = sem("filled")
        emptied = {"act": sem("emptied_act"), "dve": sem("emptied_dve")}
        stats_ready = {n: sem(n + "_stats_ready") for n in norm}
        rstd_ready = {n: sem(n + "_rstd_ready") for n in norm}
        xhat_ready = {n: sem(n + "_xhat_ready") for n in norm}
        shift_ready, xj_ready, ruk_ready, vh_ready = sem("shift_ready"), sem("xj_ready"), sem("ruk_ready"), sem("vh_ready")
        th_ready, g_used = sem("th_ready"), sem("g_used")
        vb_filled, a_ready, a0_ready, scanned = sem("vb_filled"), sem("a_ready"), sem("a0_ready"), sem("scanned")
        z_ready, zh_ready, zl_ready = sem("z_ready"), sem("zh_ready"), sem("zl_ready")
        summed, acc_read = sem("summed"), sem("acc_read")
        yc_ready, sq_ready, gvar_ready, gdev_ready, zn_ready = (
            sem("yc_ready"), sem("sq_ready"), sem("gvar_ready"), sem("gdev_ready"), sem("zn_ready"))
        shift2_ready, kk_ready, out_ready = sem("shift2_ready"), sem("kk_ready"), sem("out_ready")

        x_d = d["x4"].rearrange("b (c p) n -> b p c n", p=P)
        out_d = out.rearrange("b (c p) n -> b p c n", p=P)

        def channels(name):
            return ps[:, units.unit(name), :].rearrange("p (c n) -> p c n", c=KC)

        def tokens(name):
            return ps[:, units.unit(name), :].rearrange("p (t n) -> p t n", t=TC)

        def flat(x):
            return x.rearrange("p c n -> p (c n)")

        def halves(x):
            return [x[:, 2 * i:2 * i + 2, :].rearrange("p c n -> p (c n)") for i in range(2)]

        def step(k, n):
            return k * RS + (n + 1)

        def first(k):
            return isinstance(k, int) and k == 0

        def iterations(engine, body):
            body(-2, ("norm",), 0)
            body(-1, ("front", "norm"), 1)
            body(0, ("wkv", "front", "norm"), 0)
            with engine.Fori(1, B - 3, 2) as k:
                body(k, ("wkv", "back", "front", "norm"), 1)
                body(k + 1, ("wkv", "back", "front", "norm"), 0)
            body(B - 3, ("wkv", "back", "front", "norm"), 1)
            body(B - 2, ("wkv", "back", "front"), 0)
            body(B - 1, ("wkv", "back"), 1)
            body(B, ("back",), 0)

        with nc.Block() as block:

            @block.sync
            def _(sp):
                sp.sem_inc(out_stored, 16)

                def load_front(s):
                    sp.dma_start(x_in[:, :, :], x_d[s]).then_inc(x_loaded, 16)
                    sp.dma_start(state1[:, :], d["state_cols"][s][:, 1, :]).then_inc(x_loaded, 16)

                def load_s0(s, par):
                    sp.dma_start(s0[:, par, :, :], d["s0"][s]).then_inc(s0_loaded, 16)

                load_s0(0, 0)
                sp.dma_start(xcT[:, 0, 0:P + RS - 1], d["gather"]).then_inc(spread_loaded, 16)
                sp.dma_start(S[:, :, :, :].rearrange("p a c n -> p (a c n)"),
                             d["spread"].rearrange("p j m -> p (j m)")).then_inc(spread_loaded, 16)
                for n in LATE_C:
                    sp.dma_start(w[n][:, :, :], d[n].rearrange("(c p) n -> p c n", p=P)).then_inc(late_loaded, 16)

                def body(k, parts, par):
                    if "back" in parts:
                        sp.wait_ge(out_stored, 16 * k)
                        sp.dma_start(x5[:, :, :], x_d[k - 1]).then_inc(x5_loaded, 16)
                        sp.dma_start(state0[:, :], d["state_cols"][k - 1][:, 0, :]).then_inc(x5_loaded, 16)
                    if "front" in parts and not (isinstance(k, int) and k < 0):
                        sp.wait_ge(a0_ready, step(k, 0))
                        load_s0(k + 1, 1 - par)
                    if "norm" in parts:
                        sp.wait_ge(filled, units.filled(k + 2, "v"))
                        load_front(k + 2)
                    if "back" in parts:
                        sp.wait_ge(out_ready, k)
                        sp.dma_start(out_d[k - 1], x5[:, :, :]).then_inc(out_stored, 16)

                iterations(sp, body)
                sp.wait_ge(out_stored, (B + 1) * 16)

            @block.gpsimd
            def _(pool):
                nc.gpsimd.memset(tT[:, :, :], 0.0)
                nc.gpsimd.memset(wT[:, :, :, 0:1], 0.0).then_inc(zeros_ready, 1)

                def inverse_deviation(name, count):
                    _, _, ve, rstd = norm[name]
                    pool.wait_ge(stats_ready[name], count)
                    nc.gpsimd.tensor_tensor(rstd[:, :], ve[:, :], w["neghalf"][:, 0:TC],
                                            ALU.pow).then_inc(rstd_ready[name], 1)

                def body(k, parts, par):
                    for n in range(STEPS):
                        if n == LN1 and "norm" in parts:
                            inverse_deviation("ln1", k + 3)
                        if n < RS and "wkv" in parts:
                            pool.wait_ge(scanned, step(k, n))
                            nc.gpsimd.tensor_tensor(S[:, n % 2, :, :], S[:, n % 2, :, :], rT[:, par, :, :],
                                                    ALU.mult).then_inc(z_ready, 1)
                        if "front" in parts:
                            for i, name in enumerate(MIX):
                                if STEP_OF["m" + name] == n:
                                    pool.wait_ge(emptied["dve"], units.emptied(k + 2, "m" + name))
                                    xj = xmix[:, (i + 1) % 2, :, :]
                                    nc.gpsimd.tensor_tensor(xj, xj, xaT[:, :, 1:T + 1], ALU.add).then_inc(xj_ready, 1)
                        if n == STEP_OF["o"] and "back" in parts:
                            inverse_deviation("ln2", k)

                iterations(pool, body)

            @block.scalar
            def _(act):
                act.wait_ge(zeros_ready, 1)
                act.sem_inc(emptied["act"], units.per["act"])
                act.wait_ge(spread_loaded, 32)
                nc.scalar.copy(spread[:, :, :].rearrange("p j m -> p (j m)"),
                               S[:, :, :, :].rearrange("p a c n -> p (a c n)")).then_inc(spread_ready, 1)
                nc.scalar.copy(gather[:, :], xcT[:, 0, 0:P + RS - 1]).then_inc(spread_ready, 1)

                def shifted(name, dst, state, scale, bias):
                    nc.scalar.copy(dst[:, :, 0], state[:, :])
                    for c in range(KC):
                        op = nc.scalar.activation(dst[:, c, 1:T + 1], channels(name)[:, c, :], ACT.Identity,
                                                  bias=col(w["cols"], bias, c), scale=col(w["cols"], scale, c))
                    return op

                def move(k, name, par):
                    other = 1 - par
                    if name == "g":
                        act.wait_ge(filled, units.filled(k + 2, name))
                        if not first(k):
                            act.wait_ge(g_used, k)
                        nc.scalar.activation(g2T[:, par, :, :], channels(name), ACT.Tanh, scale=0.5).then_inc(th_ready, 1)
                    elif name == "xaT":
                        act.wait_ge(x_loaded, 32 * k + 96)
                        if not (isinstance(k, int) and k < -1):
                            act.wait_ge(xj_ready, NMIX * k + 2 * NMIX)
                        act.wait_ge(filled, units.filled(k + 2, name))
                        shifted(name, xaT, state1, "rln1_w", "rln1_b").then_inc(emptied["act"], 1)
                    elif name == "t":
                        act.wait_ge(filled, units.filled(k + 2, name))
                        for j, mix in enumerate(("w", "k", "v", "r", "g")):
                            rows = slice(DM * j % P, DM * j % P + DM)
                            op = nc.scalar.activation(tT[rows, j, :], channels(name)[rows, DM * j // P, :], ACT.Tanh)
                        op.then_inc(emptied["act"], 1)
                    elif name == "dec1":
                        act.wait_ge(filled, units.filled(k + 2, name))
                        nc.scalar.activation(decT[:, :], channels(name)[0:DD, 0, :], ACT.Tanh).then_inc(emptied["act"], 1)
                    elif name == "dec2":
                        if not (isinstance(k, int) and k < 1):
                            act.wait_ge(scanned, k * RS)
                        act.wait_ge(filled, units.filled(k + 2, name))
                        for c in range(KC):
                            nc.scalar.activation(wT[:, other, c, 1:T], channels(name)[:, c, 0:T - 1], ACT.Exp,
                                                 bias=col(w["cols"], "time_decay", c))
                        nc.scalar.drain()
                        nc.scalar.activation(wT[:, other, :, 1:T], wT[:, other, :, 1:T], ACT.Exp,
                                             scale=-1.0).then_inc(emptied["act"], 1)
                    elif name == "k":
                        act.wait_ge(filled, units.filled(k + 2, name))
                        nc.scalar.copy(kT[:, other, :, :], channels(name)).then_inc(emptied["act"], 1)
                    elif name == "r":
                        if not (isinstance(k, int) and k < 1):
                            act.wait_ge(z_ready, k * RS)
                        act.wait_ge(filled, units.filled(k + 2, name))
                        nc.scalar.copy(rT[:, other, :, :], channels(name)).then_inc(emptied["act"], 1)
                    elif name == "bonus":
                        act.wait_ge(filled, units.filled(k + 2, name))
                        nc.scalar.copy(bonusT[:, other, :, :], channels(name)).then_inc(emptied["act"], 1)
                    elif name == "v":
                        act.wait_ge(filled, units.filled(k + 2, name))
                        nc.scalar.copy(vh[:, other, :, :], channels(name)).then_inc(vh_ready, 1)
                    elif name == "zT":
                        act.wait_ge(filled, units.filled(k + 2, name))
                        for c in range(KC):
                            op = nc.scalar.activation(zT[:, c, :], channels(name)[:, c, :], ACT.Identity,
                                                      bias=col(w["cols"], "gn_b", c), scale=col(w["cols"], "gn_w", c))
                        op.then_inc(emptied["act"], 1)
                    elif name == "xcT":
                        act.wait_ge(x5_loaded, 32 * k)
                        act.wait_ge(filled, units.filled(k + 2, name))
                        shifted(name, xcT, state0, "rln2_w", "rln2_b").then_inc(emptied["act"], 1)
                    elif name == "kk":
                        act.wait_ge(filled, units.filled(k + 2, name))
                        nc.scalar.activation(kkT[:, :, :], channels(name), ACT.Relu).then_inc(emptied["act"], 1)
                        nc.scalar.drain()
                        nc.scalar.activation(kkT[:, :, :], kkT[:, :, :], ACT.Square).then_inc(kk_ready, 1)
                    elif name == "rr":
                        act.wait_ge(filled, units.filled(k + 2, name))
                        nc.scalar.activation(by_token(rrt), tokens(name), ACT.Tanh, scale=0.5).then_inc(emptied["act"], 1)

                def body(k, parts, par):
                    for n in range(STEPS):
                        if n < RS and "wkv" in parts:
                            if n == 0:
                                act.wait_ge(s0_loaded, 16 * k + 16)
                            if not first(k) or n >= 2:
                                act.wait_ge(zl_ready, step(k, n - 2))
                            nc.scalar.copy(S[:, n % 2, :, 0], s0[:, par, :, n]).then_inc(a0_ready, 1)
                        if 1 <= n <= RS and "wkv" in parts:
                            act.wait_ge(z_ready, step(k, n - 1))
                            if not first(k) or n >= 3:
                                act.wait_ge(summed, step(k, n - 3))
                            nc.scalar.copy(zh[:, (n - 1) % 2, :, :], S[:, (n - 1) % 2, :, :]).then_inc(zh_ready, 1)
                        if n == 1 and "back" in parts:
                            act.wait_ge(yc_ready, k)
                            nc.scalar.activation(sq[:, :, :], yc[:, :, :], ACT.Square).then_inc(sq_ready, 1)
                        if n == 2 and "back" in parts:
                            act.wait_ge(gvar_ready, k)
                            nc.scalar.activation(grstd[:, :], gvar[:, :], ACT.Sqrt).then_inc(gdev_ready, 1)
                        for name, reader in FILLS.get(n, []):
                            if PART_OF.get(name, "front") in parts:
                                move(k, name, par)
                            elif reader == "act":
                                nc.scalar.drain()
                                act.sem_inc(emptied["act"], 1)

                iterations(act, body)

            @block.vector
            def _(dve):
                dve.sem_inc(emptied["dve"], units.per["dve"])
                dve.sem_inc(g_used, 1)

                def groups(x):
                    return x.rearrange("p t (h s) -> p (t h) s", s=RS)

                def over_group(x):
                    return x[:, :].unsqueeze(2).to_broadcast([P, NG, RS])

                def shift(src, dst, mixes):
                    nc.vector.tensor_tensor(dst[:, :, :], src[:, :, 0:T], src[:, :, 1:T + 1], ALU.subtract)
                    nc.vector.drain()
                    for x, mix, ready in mixes:
                        for c in range(KC):
                            op = nc.vector.scalar_tensor_tensor(x[:, c, :], dst[:, c, :], col(w["cols"], mix, c),
                                                                src[:, c, 1:T + 1], ALU.mult, ALU.add)
                        op.then_inc(ready, 1)

                def mix(k, name):
                    dve.wait_ge(filled, units.filled(k + 2, "m" + name))
                    for c in range(KC):
                        op = nc.vector.scalar_tensor_tensor(xmix[:, (MIX.index(name) + 1) % 2, c, :],
                                                            channels("m" + name)[:, c, :],
                                                            col(w["cols"], "maa_" + name, c), sx[:, c, :], ALU.add, ALU.mult)
                    op.then_inc(emptied["dve"], 1)

                def front(k, n, other):
                    if n == STEP_OF["v"]:
                        dve.wait_ge(vh_ready, k + 2)
                        dve.wait_ge(emptied["act"], units.emptied(k + 2, "bonus"))
                        nc.vector.tensor_tensor(vl[:, other, :, :], channels("v"), vh[:, other, :, :], ALU.subtract)
                        nc.vector.tensor_tensor(bonusT[:, other, :, :], channels("v"), bonusT[:, other, :, :],
                                                ALU.mult)
                        nc.vector.drain()
                        dve.sem_inc(emptied["dve"], 1)
                    for name in MIX:
                        if n == STEP_OF["m" + name]:
                            mix(k, name)
                    if n == STEP_OF["r"]:
                        dve.wait_ge(emptied["act"], units.emptied(k + 2, "r"))
                        for c in range(KC):
                            op = nc.vector.scalar_tensor_tensor(bonusT[:, other, c, :], rT[:, other, c, :],
                                                                col(w["cols"], "faaaa", c), kT[:, other, c, :],
                                                                ALU.mult, ALU.mult)
                        op.then_inc(ruk_ready, 1)

                def back(k, n, other):
                    ln2 = norm["ln2"]
                    if n == 0:
                        dve.wait_ge(filled, units.filled(k + 2, "y"))
                        nc.vector.reduce_sum(gmean[:, :], groups(tokens("y")), axis=AX)
                        nc.vector.drain()
                        nc.vector.tensor_scalar(gmean[:, :], gmean[:, :], 1.0 / RS, None, ALU.mult)
                        nc.vector.drain()
                        nc.vector.tensor_tensor(groups(by_token(yc)), groups(tokens("y")), over_group(gmean),
                                                ALU.subtract)
                        nc.vector.drain()
                        dve.sem_inc(emptied["dve"], 1)
                        dve.sem_inc(yc_ready, 1)
                    if n == 1:
                        dve.wait_ge(sq_ready, k)
                        nc.vector.reduce_sum(gvar[:, :], groups(by_token(sq)), axis=AX)
                        nc.vector.drain()
                        nc.vector.tensor_scalar(gvar[:, :], gvar[:, :], 1.0 / RS, EPS, ALU.mult,
                                                ALU.add).then_inc(gvar_ready, 1)
                    if n == 3:
                        dve.wait_ge(gdev_ready, k)
                        nc.vector.reciprocal(grstd[:, :], grstd[:, :])
                        nc.vector.drain()
                        nc.vector.tensor_tensor(gtmp[:, :], grstd[:, :], grstd[:, :], ALU.mult)
                        nc.vector.drain()
                        nc.vector.tensor_tensor(gtmp[:, :], gtmp[:, :], gvar[:, :], ALU.mult)
                        nc.vector.drain()
                        nc.vector.tensor_scalar(gtmp[:, :], gtmp[:, :], -0.5, 1.5, ALU.mult, ALU.add)
                        nc.vector.drain()
                        nc.vector.tensor_tensor(grstd[:, :], grstd[:, :], gtmp[:, :], ALU.mult)
                        nc.vector.drain()
                        nc.vector.tensor_tensor(groups(by_token(yc)), groups(by_token(yc)), over_group(grstd),
                                                ALU.mult).then_inc(zn_ready, 1)
                    if n == STEP_OF["zT"]:
                        dve.wait_ge(emptied["act"], units.emptied(k + 2, "zT"))
                        nc.vector.tensor_tensor(zT[:, :, :], zT[:, :, :], g2T[:, other, :, :], ALU.mult).then_inc(g_used, 1)
                    if n == STEP_OF["o"]:
                        dve.wait_ge(x5_loaded, 32 * k)
                        dve.wait_ge(filled, units.filled(k + 2, "o"))
                        nc.vector.scalar_tensor_tensor(x5[:, :, :], tokens("o"), 0.5, x5[:, :, :], ALU.mult,
                                                       ALU.add).then_inc(emptied["dve"], 1)
                        nc.vector.drain()
                        layernorm_stats(nc, x5, *ln2[:3]).then_inc(stats_ready["ln2"], 1)
                    if n == STEP_OF["o"] + 1:
                        dve.wait_ge(rstd_ready["ln2"], k)
                        layernorm_apply(nc, x5, ln2[1], ln2[3], by_token(xhat)).then_inc(xhat_ready["ln2"], 1)
                    if n == STEP_OF["xcT"]:
                        dve.wait_ge(emptied["act"], units.emptied(k + 2, "xcT"))
                        shift(xcT, sxc, [(xk2, "fmaa_k", shift2_ready), (xr2, "fmaa_r", shift2_ready)])
                    if n == STEP_OF["kv"]:
                        dve.wait_ge(emptied["act"], units.emptied(k + 2, "rr"))
                        dve.wait_ge(filled, units.filled(k + 2, "kv"))
                        nc.vector.scalar_tensor_tensor(by_token(gated), by_token(rrt), 1.0, tokens("kv"), ALU.add,
                                                       ALU.mult).then_inc(emptied["dve"], 1)
                        nc.vector.drain()
                        nc.vector.scalar_tensor_tensor(x5[:, :, :], by_token(gated), 0.5, x5[:, :, :], ALU.mult,
                                                       ALU.add).then_inc(out_ready, 1)

                def layernorm_begin(s):
                    nc.vector.drain()
                    dve.wait_ge(x_loaded, 32 * s + 32)
                    layernorm_stats(nc, x_in, *norm["ln1"][:3]).then_inc(stats_ready["ln1"], 1)

                def layernorm_end(s):
                    dve.wait_ge(rstd_ready["ln1"], s + 1)
                    layernorm_apply(nc, x_in, norm["ln1"][1], norm["ln1"][3], x_in).then_inc(xhat_ready["ln1"], 1)

                def body(k, parts, par):
                    other = 1 - par
                    for n in range(STEPS):
                        if n < RS and "wkv" in parts:
                            dve.wait_ge(vb_filled, step(k, n))
                            if not first(k) or n >= 2:
                                dve.wait_ge(zl_ready, step(k, n - 2))
                            nc.vector.tensor_tensor(S[:, n % 2, :, 1:T], kT[:, par, :, 0:T - 1], vb[:, :, 0:T - 1],
                                                    ALU.mult).then_inc(a_ready, 1)
                            nc.vector.drain()
                            dve.wait_ge(a0_ready, step(k, n))
                            nc.vector.tensor_tensor_scan(flat(S[:, n % 2, :, :]), flat(wT[:, par, :, :]),
                                                         flat(S[:, n % 2, :, :]), 0.0, ALU.mult,
                                                         ALU.add).then_inc(scanned, 1)
                        if 1 <= n <= RS and "wkv" in parts:
                            dve.wait_ge(zh_ready, step(k, n - 1))
                            half = (n - 1) % 2
                            nc.vector.tensor_tensor(zl[:, half, :, :], S[:, half, :, :], zh[:, half, :, :],
                                                    ALU.subtract).then_inc(zl_ready, 1)
                        if n == LN1 and "norm" in parts:
                            layernorm_begin(k + 2)
                        if n == LN1 + 1 and "norm" in parts:
                            layernorm_end(k + 2)
                        if n == STEP_OF["xaT"] and "norm" in parts:
                            dve.wait_ge(emptied["act"], units.emptied(k + 2, "xaT"))
                            dve.wait_ge(filled, units.filled(k + 2, "v"))
                            shift(xaT, sx, [(xmix[:, 0, :, :], "maa_x", shift_ready)])
                        if n == RS + 1 and "wkv" in parts:
                            nc.vector.drain()
                            dve.wait_ge(summed, k * RS + RS)
                            nc.vector.tensor_tensor(yT[:, :, :], acc[:, :, :], bonusT[:, par, :, :],
                                                    ALU.add).then_inc(acc_read, 1)
                        if n == STEP_OF["g"] and "wkv" in parts:
                            dve.wait_ge(th_ready, k + 1)
                            nc.vector.scalar_tensor_tensor(g2T[:, par, :, :], g2T[:, par, :, :], 1.0, channels("g"),
                                                           ALU.add, ALU.mult).then_inc(emptied["dve"], 1)
                        if "front" in parts:
                            front(k, n, other)
                        if "back" in parts:
                            back(k, n, other)
                        for name, reader in FILLS.get(n, []):
                            if reader == "dve" and PART_OF.get(name, "front") not in parts:
                                nc.vector.drain()
                                dve.sem_inc(emptied["dve"], 1)

                iterations(dve, body)

            @block.tensor
            def _(pe):
                pe.wait_ge(dsem["c"], 16 * len(WEIGHTS_C))
                pe.wait_ge(zeros_ready, 1)

                def to_channel_layout(name, src):
                    for c in range(KC):
                        for tc in range(TC):
                            op = nc.tensor.transpose(channels(name)[:, c, tc * P:(tc + 1) * P],
                                                     src[:, tc, c * P:(c + 1) * P], w["ident"][:, :])
                    return op

                def part_of(count, half):
                    return range(half * (count // 2), (half + 1) * (count // 2))

                def project(name, weights, src, half):
                    for m in part_of(KC, half):
                        for c in range(KC):
                            op = nc.tensor.matmul(channels(name)[:, m, :], weights[:, c, m * P:(m + 1) * P],
                                                  src[:, c, :], start=(c == 0), stop=(c == KC - 1))
                    return op

                def project_to_tokens(name, src, weights, half):
                    for tc in part_of(TC, half):
                        for c in range(KC):
                            op = nc.tensor.matmul(tokens(name)[:, tc, :], src[:, c, tc * P:(tc + 1) * P],
                                                  weights[:, c, :], start=(c == 0), stop=(c == KC - 1))
                    return op

                def mixed(k, i, name, half):
                    pe.wait_ge(xj_ready, NMIX * k + (NMIX + i + 1))
                    return project(name, w["W" + name], xmix[:, (i + 1) % 2, :, :], half)

                def fill(k, name, other, half):
                    u = channels(name)
                    if name == "g":
                        pe.wait_ge(xj_ready, NMIX * k + NMIX)
                        op = project(name, w["Wg"], xmix[:, 1, :, :], half)
                    elif name == "xaT":
                        pe.wait_ge(xhat_ready["ln1"], k + 3)
                        op = to_channel_layout(name, x_in)
                    elif name == "t":
                        pe.wait_ge(shift_ready, k + 3)
                        for n0, n in ((0, P), (P, DM)):
                            for c in range(KC):
                                op = nc.tensor.matmul(u[0:n, n0 // P, :], w["maa_w1"][:, c, n0:n0 + n],
                                                      xmix[:, 0, c, :], start=(c == 0), stop=(c == KC - 1))
                    elif name in ("mw", "mk", "mr", "mv", "mg"):
                        if name == "mw":
                            pe.wait_ge(emptied["act"], units.emptied(k + 1, "t"))
                        j = "wkvrg".index(name[1])
                        for c in range(KC):
                            op = nc.tensor.matmul(u[:, c, :], w["maa_w2"][:, DM * j // P, c * P:(c + 1) * P],
                                                  tT[:, j, :], start=True, stop=True)
                    elif name == "dec1":
                        pe.wait_ge(xj_ready, NMIX * k + (NMIX + 1))
                        for c in range(KC):
                            op = nc.tensor.matmul(u[0:DD, 0, :], w["decay_w1"][:, c, :], xmix[:, 1, c, :],
                                                  start=(c == 0), stop=(c == KC - 1))
                    elif name == "dec2":
                        pe.wait_ge(emptied["act"], units.emptied(k + 2, "dec1"))
                        for c in range(KC):
                            op = nc.tensor.matmul(u[:, c, :], w["decay_w2"][0:DD, c * P:(c + 1) * P], decT[:, :],
                                                  start=True, stop=True)
                    elif name == "k":
                        op = mixed(k, 1, name, half)
                    elif name == "r":
                        op = mixed(k, 2, name, half)
                    elif name == "v":
                        op = mixed(k, 3, name, half)
                    elif name == "bonus":
                        pe.wait_ge(ruk_ready, k + 2)
                        for to, src in zip(halves(u), halves(bonusT[:, other, :, :])):
                            op = nc.tensor.matmul(to, w["same_head"][:, :], src, start=True, stop=True)
                    elif name == "y":
                        pe.wait_ge(acc_read, k)
                        for tc in range(TC):
                            for c in range(KC):
                                op = nc.tensor.transpose(tokens(name)[:, tc, c * P:(c + 1) * P],
                                                         yT[:, c, tc * P:(tc + 1) * P], w["ident"][:, :])
                    elif name == "zT":
                        pe.wait_ge(zn_ready, k)
                        op = to_channel_layout(name, by_token(yc))
                    elif name == "o":
                        pe.wait_ge(late_loaded, 16 * len(LATE_C))
                        pe.wait_ge(g_used, k + 1)
                        op = project_to_tokens(name, zT, w["Wo"], half)
                    elif name == "xcT":
                        pe.wait_ge(xhat_ready["ln2"], k)
                        op = to_channel_layout(name, by_token(xhat))
                    elif name == "kk":
                        pe.wait_ge(shift2_ready, 2 * k - 1)
                        op = project(name, w["fWk"], xk2, half)
                    elif name == "rr":
                        pe.wait_ge(shift2_ready, 2 * k)
                        op = project_to_tokens(name, xr2, w["fWr"], half)
                    else:
                        pe.wait_ge(kk_ready, k)
                        op = project_to_tokens(name, kkT, w["fWv"], half)
                    if half:
                        op.then_inc(filled, 1)

                def body(k, parts, par):
                    for n in range(STEPS):
                        if n < RS and "wkv" in parts:
                            if n == 0:
                                pe.wait_ge(spread_ready, 2)
                                pe.wait_ge(emptied["dve"], units.emptied_last(k + 2, "v"))
                            if not first(k) or n >= 1:
                                pe.wait_ge(a_ready, step(k, n - 1))
                            for to, high, low in zip(halves(vb), halves(vh[:, par, :, :]), halves(vl[:, par, :, :])):
                                nc.tensor.matmul(to, spread[:, n, :], high, start=True, stop=False)
                                op = nc.tensor.matmul(to, spread[:, n, :], low, start=False, stop=True)
                            op.then_inc(vb_filled, 1)
                        j = n - 2
                        if j >= 0 and "wkv" in parts:
                            pe.wait_ge(zl_ready, step(k, j))
                            if j == 0 and not first(k):
                                pe.wait_ge(acc_read, k)
                            pick = gather[:, RS - 1 - j:RS - 1 - j + P]
                            for to, high, low in zip(halves(acc), halves(zh[:, j % 2, :, :]), halves(zl[:, j % 2, :, :])):
                                nc.tensor.matmul(to, pick, high, start=(j == 0), stop=False)
                                op = nc.tensor.matmul(to, pick, low, start=False, stop=(j == RS - 1))
                            op.then_inc(summed, 1)
                        for name, _ in FILLS.get(n, []):
                            if name not in BEGUN.values():
                                reader, value = units.before(k + 2, name)
                                pe.wait_ge(emptied[reader], value)
                            if PART_OF.get(name, "front") in parts:
                                fill(k, name, 1 - par, 1)
                            else:
                                nc.tensor.drain()
                                pe.sem_inc(filled, 1)
                        if n in BEGUN:
                            name = BEGUN[n]
                            reader, value = units.before(k + 2, name)
                            pe.wait_ge(emptied[reader], value)
                            if PART_OF.get(name, "front") in parts:
                                fill(k, name, 1 - par, 0)

                iterations(pe, body)


WEIGHTS_C = {"Wk": (KC, C), "Wv": (KC, C), "Wr": (KC, C), "Wg": (KC, C), "maa_w1": (KC, NMIX * DM),
             "maa_w2": (2, C), "decay_w1": (KC, DD), "decay_w2": (C,), "same_head": (P,),
             "Wo": (KC, C), "fWk": (KC, C)}
LATE_C = ("fWr", "fWv")


def build_program(nc, d, out):
    with ExitStack() as ctx:
        def sb(name, *shape):
            return ctx.enter_context(nc.sbuf_tensor("w_" + name, list(shape), F32))

        w = {"ident": sb("ident", P, P), "cols": sb("cols", P, NCOL), "neghalf": sb("neghalf", P, TC)}
        dsem = {n: ctx.enter_context(nc.semaphore("loaded_" + n))
                for n in ("ident", "cols", "w1", "w2", "c")}
        d["x2"] = nc.dram_tensor("x2", (B, T, C), F32, kind="Internal").ap()
        d["x3"] = nc.dram_tensor("x3", (B, T, C), F32, kind="Internal").ap()
        d["x4"] = nc.dram_tensor("x4", (B, T, C), F32, kind="Internal").ap()
        attention_phase(nc, d, w, dsem, cross=False)
        attention_phase(nc, d, w, dsem, cross=True)
        weights_c = {n: sb(n, P, *shape) for n, shape in WEIGHTS_C.items()}
        with nc.sbuf_tensor("w_w1", [P, KC, FF], F32) as w1, nc.sbuf_tensor("w_w2", [P, FC, C], F32) as w2:
            phase_b(nc, d, {**w, **weights_c, "w1": w1, "w2": w2}, dsem)
        phase_c(nc, d, out, {**w, **weights_c}, dsem)


def kernel(**inputs):
    import concourse.bacc as bacc
    from concourse.bass_utils import run_bass_kernel_spmd

    g = {k: np.asarray(v) for k, v in inputs.items()}
    L0 = {k[9:]: v for k, v in g.items() if k.startswith("L0_xattn_")}
    L1 = {k[9:]: v for k, v in g.items() if k.startswith("L1_xattn_")}
    vectors = {
        "ln1_s": L0["ln1_s"], "ln1_b": L0["ln1_b"], "b_q": L0["b_qkv"][:C], "b_k": L0["b_qkv"][C:2 * C], "b_v": L0["b_qkv"][2 * C:],
        "ln2_s": L0["ln2_s"], "ln2_b": L0["ln2_b"], "b_qx": L0["b_q"], "b_kx": L0["b_kv"][:C], "b_vx": L0["b_kv"][C:],
        "ln3_s": L0["ln3_s"], "ln3_b": L0["ln3_b"], "b1": L0["b1"], "rln1_w": L1["ln1_w"], "rln1_b": L1["ln1_b"],
        "rln2_w": L1["ln2_w"], "rln2_b": L1["ln2_b"], "maa_x": L1["maa_x"], "maa_w": L1["maa_w"],
        "maa_k": L1["maa_k"], "maa_v": L1["maa_v"], "maa_r": L1["maa_r"], "maa_g": L1["maa_g"],
        "time_decay": L1["time_decay"], "faaaa": L1["faaaa"].reshape(C), "gn_w": L1["gn_w"], "gn_b": L1["gn_b"], "fmaa_k": L1["fmaa_k"],
        "fmaa_r": L1["fmaa_r"]}
    spread = {"b_ao": L0["b_ao"], "b_co": L0["b_co"], "b2": L0["b2"]}
    state = g["ctx_2048"]

    def chunked(m):
        return m.reshape(KC, P, -1).transpose(1, 0, 2)

    mix2 = [L1["maa_w2"][:4].reshape(P, C), np.zeros((P, C), np.float32)]
    mix2[1][:DM] = L1["maa_w2"][4]
    mix2 = np.stack(mix2, axis=1)
    head, chan, j = np.arange(P) // RS, np.arange(P) % RS, np.arange(RS)
    same = (head[:, None] == head[None, :]).astype(np.float32)
    arrays = {
        "x": g["x"], "ctx_2048": state, "mask_self": g["mask_1x1xSxS2_fc1"], "mask_cross": g["mask_Bx1xSxS2_ff1"],
        "cols": np.concatenate([vectors[n].reshape(k, P).T for n, k in COLUMNS], axis=1),
        "rows": np.stack([spread[n] for n in ROWS]).reshape(len(ROWS), 1, C)[:, 0],
        "ident": np.eye(P, dtype=np.float32),
        "w_qkv": L0["w_qkv"], "w_ao": L0["w_ao"], "w_q": L0["w_q"], "w_kv": L0["w_kv"], "w_co": L0["w_co"],
        "w1": L0["w1"], "w2": L0["w2"],
        "state_cols": state[:, :2].reshape(B, 2, KC, P).transpose(0, 3, 1, 2),
        "s0": state[:, 2:2 + RS].reshape(B, KC, P, RS).transpose(0, 2, 1, 3),
        "fWr": L1["fWr"].T, "fWv": L1["fWv"].T,
        "maa_w1": chunked(L1["maa_w1"]), "maa_w2": mix2,
        "decay_w1": chunked(L1["decay_w1"]), "decay_w2": L1["decay_w2"],
        "same_head": same,
        "spread": same[:, None, :] * (chan[:, None, None] == j[None, :, None]),
        "gather": (np.arange(P + RS - 1)[None, :] == (RS * head + RS - 1)[:, None]).astype(np.float32),
    }
    for n in ("Wk", "Wv", "Wr", "Wg", "Wo", "fWk"):
        arrays[n] = chunked(L1[n].T)
    nc = bacc.Bacc("TRN2", target_bir_lowering=False, num_devices=1)
    feed, d = {}, {}
    for name, a in arrays.items():
        a = np.ascontiguousarray(a)
        feed["in_" + name] = a
        d[name] = nc.dram_tensor("in_" + name, a.shape, mybir.dt.from_np(a.dtype), kind="ExternalInput").ap()
    out = nc.dram_tensor("out_0", (B, T, C), F32, kind="ExternalOutput").ap()
    build_program(nc, d, out)
    r = run_bass_kernel_spmd(nc, [feed], core_ids=[0])
    return r.results[0]["out_0"]
```
